# Optimizing a Trainium2 kernel written in Bass

```python
import numpy as np
import jax
import jax.numpy as jnp

def _softmax(x, axis=-1):
    return jax.nn.softmax(x, axis=axis)

def _gelu(x):
    return jax.nn.gelu(x, approximate=True)

def _silu(x):
    return jax.nn.silu(x)

def _sigmoid(x):
    return jax.nn.sigmoid(x)

def _layernorm(x, axis=-1, eps=1e-05):
    m = jnp.mean(x, axis=axis, keepdims=True)
    v = jnp.var(x, axis=axis, keepdims=True)
    return (x - m) / jnp.sqrt(v + eps)

def _scatter_add(tgt, idx, src, axis=0):
    return tgt.at[idx].add(src)

def _segment_sum(src, seg, n):
    return jax.ops.segment_sum(src, seg, n)
kernel_name = 'mk_gps_d1_gnn_r8_c60918'

def setup_inputs(seed: int=0):
    np.random.seed(seed)
    _w = jnp.asarray

    def _rec_inputs():
        import jax
        import jax.numpy as jnp
        _gk = jax.random.key(seed)
        x = -0.0003713 + 1 * jax.random.normal(jax.random.fold_in(_gk, 1), (6250, 256), jnp.float32)
        _s = jax.random.randint(jax.random.fold_in(_gk, 2), (50000,), 0, 6250, jnp.int32)
        _d = jax.random.randint(jax.random.fold_in(_gk, 3), (50000,), 0, 6250, jnp.int32)
        _loop = jnp.arange(6250, dtype=jnp.int32)
        src = jnp.concatenate([_s, _d, _loop])
        dst = jnp.concatenate([_d, _s, _loop])
        _o = jnp.argsort(dst, stable=True)
        src = src[_o]
        dst = dst[_o]
        edge_attr_256 = -6.47781e-05 + 0.999943 * jax.random.normal(jax.random.fold_in(_gk, 11), (106250, 256), jnp.float32)
        return (x, src, dst, edge_attr_256)
    x, src, dst, edge_attr_256 = _rec_inputs()

    def _L0_gnn_setup():
        import jax, jax.numpy as jnp
        import numpy as np
        N_NODES = 6250
        N_EDGES = 100000
        DIM = 256
        LEAKY_SLOPE = 0.015

        def leaky_relu(x):
            return jnp.where(x > 0, x, LEAKY_SLOPE * x)
        key = jax.random.key(seed)
        k_v, k_e, k_idx, k_w1, k_w2 = jax.random.split(key, 5)
        v = jax.random.normal(k_v, (N_NODES, DIM), dtype=jnp.float32)
        e = jax.random.normal(k_e, (N_EDGES, DIM), dtype=jnp.float32)
        edge_index = jax.random.randint(k_idx, (2, N_EDGES), 0, N_NODES, dtype=jnp.int64)
        limit = float(np.sqrt(6.0 / (DIM + DIM)))
        W1 = jax.random.uniform(k_w1, (DIM, DIM), minval=-limit, maxval=limit, dtype=jnp.float32)
        b1 = jnp.zeros((DIM,), dtype=jnp.float32)
        W2 = jax.random.uniform(k_w2, (DIM, DIM), minval=-limit, maxval=limit, dtype=jnp.float32)
        b2 = jnp.zeros((DIM,), dtype=jnp.float32)
        return {'v': v, 'e': e, 'edge_index': edge_index, 'W1': W1, 'b1': b1, 'W2': W2, 'b2': b2}
    _L0_gnn_all = _L0_gnn_setup()
    _L0_gnn_in = {k: v for k, v in _L0_gnn_all.items() if k in ('W1', 'b1', 'W2', 'b2')}
    del _L0_gnn_all

    def _L0_mix_setup():
        import jax, jax.numpy as jnp
        import numpy as np
        D_MODEL = 256
        NUM_HEADS = 8
        DEPTH = D_MODEL // NUM_HEADS
        B, L = (32, 512)

        def _feature_map(x):
            return jax.nn.elu(x) + 1.0
        key = jax.random.key(seed)
        ks = jax.random.split(key, 9)
        sc = 1.0 / np.sqrt(D_MODEL)
        return {'x': jax.random.normal(ks[0], (B, L, D_MODEL), dtype=jnp.float32), 'wq': jax.random.normal(ks[1], (D_MODEL, D_MODEL), dtype=jnp.float32) * sc, 'bq': jnp.zeros((D_MODEL,), dtype=jnp.float32), 'wk': jax.random.normal(ks[2], (D_MODEL, D_MODEL), dtype=jnp.float32) * sc, 'bk': jnp.zeros((D_MODEL,), dtype=jnp.float32), 'wv': jax.random.normal(ks[3], (D_MODEL, D_MODEL), dtype=jnp.float32) * sc, 'bv': jnp.zeros((D_MODEL,), dtype=jnp.float32), 'wo': jax.random.normal(ks[4], (D_MODEL, D_MODEL), dtype=jnp.float32) * sc, 'bo': jnp.zeros((D_MODEL,), dtype=jnp.float32)}
    _L0_mix_all = _L0_mix_setup()
    _L0_mix_in = {k: v for k, v in _L0_mix_all.items() if k in ('wq', 'bq', 'wk', 'bk', 'wv', 'bv', 'wo', 'bo')}
    del _L0_mix_all

    def _L0_ffn_setup():
        import math
        import jax, jax.numpy as jnp
        import numpy as np
        CAPACITY_FACTOR = 1.25
        TOP_K = 2
        LN_EPS = 1e-05

        def _layer_norm(x, gamma, beta):
            mu = jnp.mean(x, axis=-1, keepdims=True)
            var = jnp.var(x, axis=-1, keepdims=True)
            return (x - mu) * jax.lax.rsqrt(var + LN_EPS) * gamma + beta
        key = jax.random.key(seed)
        ks = jax.random.split(key, 4)
        B, S, D, F, E = (8, 512, 256, 512, 8)
        x = jax.random.normal(ks[0], (B, S, D), dtype=jnp.float32)
        Wr = jax.random.normal(ks[1], (D, E), dtype=jnp.float32) / np.sqrt(D)
        br = jnp.zeros((E,), jnp.float32)
        W1 = jax.random.normal(ks[2], (E, D, F), dtype=jnp.float32) / np.sqrt(D)
        b1 = jnp.zeros((E, F), jnp.float32)
        W2 = jax.random.normal(ks[3], (E, F, D), dtype=jnp.float32) / np.sqrt(F)
        b2 = jnp.zeros((E, D), jnp.float32)
        gamma = jnp.ones((D,), jnp.float32)
        beta = jnp.zeros((D,), jnp.float32)
        return {'x': x, 'Wr': Wr, 'br': br, 'W1': W1, 'b1': b1, 'W2': W2, 'b2': b2, 'gamma': gamma, 'beta': beta}
    _L0_ffn_all = _L0_ffn_setup()
    _L0_ffn_in = {k: v for k, v in _L0_ffn_all.items() if k in ('Wr', 'br', 'W1', 'b1', 'W2', 'b2', 'gamma', 'beta')}
    del _L0_ffn_all
    return {'x': x, 'src': src, 'dst': dst, 'edge_attr_256': edge_attr_256, 'L0_gnn_W1': _L0_gnn_in['W1'], 'L0_gnn_b1': _L0_gnn_in['b1'], 'L0_gnn_W2': _L0_gnn_in['W2'], 'L0_gnn_b2': _L0_gnn_in['b2'], 'L0_mix_wq': _L0_mix_in['wq'], 'L0_mix_bq': _L0_mix_in['bq'], 'L0_mix_wk': _L0_mix_in['wk'], 'L0_mix_bk': _L0_mix_in['bk'], 'L0_mix_wv': _L0_mix_in['wv'], 'L0_mix_bv': _L0_mix_in['bv'], 'L0_mix_wo': _L0_mix_in['wo'], 'L0_mix_bo': _L0_mix_in['bo'], 'L0_ffn_Wr': _L0_ffn_in['Wr'], 'L0_ffn_br': _L0_ffn_in['br'], 'L0_ffn_W1': _L0_ffn_in['W1'], 'L0_ffn_b1': _L0_ffn_in['b1'], 'L0_ffn_W2': _L0_ffn_in['W2'], 'L0_ffn_b2': _L0_ffn_in['b2'], 'L0_ffn_gamma': _L0_ffn_in['gamma'], 'L0_ffn_beta': _L0_ffn_in['beta']}

def reference(x, src, dst, edge_attr_256, L0_gnn_W1, L0_gnn_b1, L0_gnn_W2, L0_gnn_b2, L0_mix_wq, L0_mix_bq, L0_mix_wk, L0_mix_bk, L0_mix_wv, L0_mix_bv, L0_mix_wo, L0_mix_bo, L0_ffn_Wr, L0_ffn_br, L0_ffn_W1, L0_ffn_b1, L0_ffn_W2, L0_ffn_b2, L0_ffn_gamma, L0_ffn_beta):
    import jax
    import jax.numpy as jnp

    def _L0_gnn_ref(v, e, edge_index, W1, b1, W2, b2):
        import jax, jax.numpy as jnp
        import numpy as np
        N_NODES = 6250
        N_EDGES = 100000
        DIM = 256
        LEAKY_SLOPE = 0.015

        def leaky_relu(x):
            return jnp.where(x > 0, x, LEAKY_SLOPE * x)
        dst = edge_index[1]
        agg = jax.ops.segment_sum(e, dst, num_segments=v.shape[0])
        h = leaky_relu(agg @ W1.T + b1)
        h = h @ W2.T + b2
        return v + h

    def _L0_mix_ref(x, wq, bq, wk, bk, wv, bv, wo, bo):
        import jax, jax.numpy as jnp
        import numpy as np
        D_MODEL = 256
        NUM_HEADS = 8
        DEPTH = D_MODEL // NUM_HEADS
        B, L = (32, 512)

        def _feature_map(x):
            return jax.nn.elu(x) + 1.0
        b, l, _ = x.shape
        q = (x @ wq + bq).reshape(b, l, NUM_HEADS, DEPTH)
        k = (x @ wk + bk).reshape(b, l, NUM_HEADS, DEPTH)
        v = (x @ wv + bv).reshape(b, l, NUM_HEADS, DEPTH)
        q = _feature_map(q)
        k = _feature_map(k)
        kv = jnp.einsum('blhd,blhe->bhde', k, v)
        k_sum = jnp.sum(k, axis=1)
        qkv = jnp.einsum('blhd,bhde->blhe', q, kv)
        normalizer = jnp.einsum('blhd,bhd->blh', q, k_sum) + 1e-06
        out = qkv / normalizer[..., None]
        out = out.reshape(b, l, D_MODEL)
        return out @ wo + bo

    def _L0_ffn_ref(x, Wr, br, W1, b1, W2, b2, gamma, beta):
        import math
        import jax, jax.numpy as jnp
        import numpy as np
        CAPACITY_FACTOR = 1.25
        TOP_K = 2
        LN_EPS = 1e-05

        def _layer_norm(x, gamma, beta):
            mu = jnp.mean(x, axis=-1, keepdims=True)
            var = jnp.var(x, axis=-1, keepdims=True)
            return (x - mu) * jax.lax.rsqrt(var + LN_EPS) * gamma + beta
        B, S, D = x.shape
        E = Wr.shape[1]
        N = B * S
        K = TOP_K
        logits = jnp.mean(x, axis=1) @ Wr + br
        routing_weights = jax.nn.softmax(logits, axis=-1)
        capacity = float(math.ceil(N * CAPACITY_FACTOR / E))
        expected_loads = routing_weights.sum(axis=0) * (N / B)
        scale = jnp.where(expected_loads > capacity, capacity / expected_loads, 1.0)
        routing_weights = jax.nn.softmax(routing_weights * scale, axis=-1)
        rw_tok = jnp.broadcast_to(routing_weights[:, None, :], (B, S, E)).reshape(N, E)
        top_w, top_i = jax.lax.top_k(rw_tok, K)
        top_w = jax.nn.softmax(top_w, axis=-1)
        xf = x.reshape(N, D)
        h = jax.nn.gelu(jnp.einsum('nd,edf->enf', xf, W1) + b1[:, None, :], approximate=False)
        y = jnp.einsum('enf,efd->end', h, W2) + b2[:, None, :]
        w_dense = jnp.zeros((N, E), x.dtype).at[jnp.arange(N)[:, None], top_i].add(top_w)
        out = jnp.einsum('ne,end->nd', w_dense, y).reshape(B, S, D)
        out = _layer_norm(out + x, gamma, beta)
        return out
    edge_index = jnp.stack([src, dst])
    xn = _layernorm(x, axis=-1)
    x = x + _L0_gnn_ref(xn, edge_attr_256, edge_index, L0_gnn_W1, L0_gnn_b1, L0_gnn_W2, L0_gnn_b2) + _L0_mix_ref(xn[None], L0_mix_wq, L0_mix_bq, L0_mix_wk, L0_mix_bk, L0_mix_wv, L0_mix_bv, L0_mix_wo, L0_mix_bo)[0]
    x = x + _L0_ffn_ref(_layernorm(x, axis=-1)[None], L0_ffn_Wr, L0_ffn_br, L0_ffn_W1, L0_ffn_b1, L0_ffn_W2, L0_ffn_b2, L0_ffn_gamma, L0_ffn_beta)[0]
    return x

_drawn_inputs = setup_inputs


def setup_inputs(seed=0):
    import zlib

    import numpy as np

    out = dict(_drawn_inputs(seed))
    spreads = {'L0_gnn_b1': (0.0, 0.383),
     'L0_gnn_b2': (0.0, 0.267),
     'L0_mix_bq': (0.0, 0.8),
     'L0_mix_bk': (0.0, 0.8),
     'L0_mix_bv': (0.0, 0.277),
     'L0_mix_bo': (0.0, 0.298),
     'L0_ffn_br': (0.0, 0.1),
     'L0_ffn_b1': (0.0, 0.8),
     'L0_ffn_b2': (0.0, 0.534),
     'L0_ffn_gamma': (1.0, 0.2),
     'L0_ffn_beta': (0.0, 0.363)}
    factors = {'L0_mix_wq': 8.0, 'L0_mix_wk': 8.0, 'L0_mix_wv': 8.0}
    for name, (base, spread) in spreads.items():
        noise = np.random.default_rng([zlib.crc32(name.encode()), seed]).standard_normal(out[name].shape)
        drawn = base * np.exp(spread * noise) if base else spread * noise
        out[name] = jnp.asarray(drawn.astype(out[name].dtype))
    for name, factor in factors.items():
        out[name] = (out[name] * factor).astype(out[name].dtype)
    return out
```

```python
import numpy as np
import concourse.bass as bass
from concourse import mybir
from contextlib import ExitStack

F32 = mybir.dt.float32
F32R = mybir.dt.float32r
I32 = mybir.dt.int32
U32 = mybir.dt.uint32
ALU = mybir.AluOpType
ACT = mybir.ActivationFunctionType
AX = mybir.AxisListType

N = 6250
D = 256
KC = D // 128
NE = 106250
TOK = 125
NT = N // TOK
BLK = 2 * TOK
NB = N // BLK
HD = 32
EXP, FF, TOPK = 8, 512, 2
FC = FF // 128
CAP = float(-(-N * 5 // (4 * EXP)))
EPS = 1e-5
SLOPE = 0.015

GRP, NG = 256, 4
SUP = GRP * NG
NSUP = -(-NE // SUP)
NPAIR = NSUP // 2
LAST = NE - SUP
OVER = (NSUP - 1) * SUP - LAST
GWIN = 32
SHIFT = 60
WIN = 160
PAD = 38
AGW = SHIFT * (NSUP - 1) + WIN
PW = SHIFT + WIN
assert NSUP % 2 == 0 and AGW >= PAD + N and N % BLK == 0

MAGIC = 1597463007.0
ROOT_STEPS = 3
ROOT_OPS = 4 * ROOT_STEPS


def due(n):
    return not isinstance(n, int) or n > 0


def live(b, n=NB):
    return not isinstance(b, int) or 0 <= b < n


def run_steps(eng, step, first, low, doubles, end):
    for k in range(first, low):
        step(k, k % 2)
    with eng.Fori(0, doubles) as i:
        for p in range(2):
            step(2 * i + (low + p), (low + p) % 2)
    for k in range(low + 2 * doubles, end):
        step(k, k % 2)


def three_products(pe, out, a, b, first, last):
    (ah, al), (bh, bl) = a, b
    pe.matmul(out, ah, bh, start=first, stop=False)
    pe.matmul(out, ah, bl, start=False, stop=False)
    return pe.matmul(out, al, bh, start=False, stop=last)


def build(nc, a, out):
    with ExitStack() as ctx:
        _build(nc, a, out, ctx)


def _build(nc, a, out, ctx):
    def sb(name, shape, dt=F32, stack=None):
        return (stack or ctx).enter_context(nc.sbuf_tensor(name, shape, dt))

    def sem(name, stack=None):
        return ctx.enter_context(nc.semaphore(name))

    ps = ctx.enter_context(nc.psum_tensor("ps", [128, 8, 512], F32))

    def bank(i, n=1):
        return ps[:, i:i + n, :].rearrange("p b n -> p (b n)")

    x = sb("x", [TOK, NT, D])
    mv = sb("mv", [TOK, NT, 2])
    rstd = sb("rstd", [TOK, NT, 1])
    half3 = sb("half3", [TOK, 1])
    nv, nh, ny, nw = (sb(n, [TOK, 2, 2, 1]) for n in ("nv", "nh", "ny", "nw"))
    ni = sb("ni", [TOK, 2, 2, 1], I32)
    mvs = sb("mvs", [TOK, 2, 2, 2])
    ident = sb("ident", [128, 128])
    ones = sb("ones", [128, 128])
    flag = sb("flag", [1, 1], I32)
    mean_t = sb("mean_t", [128, KC])

    agg_stack = ctx.enter_context(ExitStack())
    aggT = sb("aggT", [128, KC, AGW], F32, agg_stack)
    dstf = sb("dstf", [128, NSUP, 8], F32, agg_stack)
    edge_stack = ExitStack()
    ring = sb("ring", [128, 4, NG, 2 * D], F32, edge_stack)
    rel = sb("rel", [128, NSUP, 8], F32, edge_stack)
    rowrel = sb("rowrel", [128, NSUP], F32, edge_stack)
    iota = sb("iota", [128, WIN], F32, edge_stack)
    oh1 = sb("oh1", [128, 2, 16, GWIN], F32, edge_stack)
    oh2 = sb("oh2", [128, 2, 2, WIN], F32, edge_stack)
    rows = sb("rows", [128, 2, 2, D], F32, edge_stack)

    x_in = [sem(f"x_in{c}") for c in range(5)]
    edges_in = [sem(f"edges_in{c}") for c in range(4)]
    edges_used = sem("edges_used")
    oh1_ready, oh2_ready = sem("oh1_ready"), sem("oh2_ready")
    rows_ps, rows_ready = sem("rows_ps"), sem("rows_ready")
    win_ps, agg_added = sem("win_ps"), sem("agg_added")
    consts = sem("consts")
    dst_in = sem("dst_in")
    dst_ready = sem("dst_ready")

    psR = bank(0).rearrange("p (h n) -> p h n", h=2)
    psW = bank(1).rearrange("p (h n) -> p h n", h=2)
    e_sup = a["edge"][0:(NSUP - 1) * SUP, :].rearrange("(s g p j) d -> s p g (j d)", g=NG, p=128, j=2)
    e_last = a["edge"][LAST:NE, :].rearrange("(g p j) d -> p g (j d)", g=NG, p=128, j=2)

    def load_pair(sp, u, par):
        for h in range(2):
            if due(2 * u + h - 3):
                sp.wait_ge(edges_used, 2 * u + h - 3)
            dst = ring[:, 2 * par + h]
            if isinstance(u, int) and 2 * u + h == NSUP - 1:
                src = e_last
            elif isinstance(u, int):
                src = e_sup[2 * u + h]
            else:
                src = e_sup[bass.ds(2 * u + h, 1)].rearrange("o p g n -> (o p) g n")
            sp.dma_start(dst, src).then_inc(edges_in[2 * par + h], 16)

    def onehots(dve, u, par):
        if due(2 * u - 2):
            dve.wait_ge(edges_used, 2 * u - 2)
        dve.tensor_tensor(
            oh1[:, par],
            rel[:, bass.ds(2 * u, 2), :].rearrange("p s c -> p (s c)").unsqueeze(2).to_broadcast([128, 16, GWIN]),
            iota[:, 0:GWIN].unsqueeze(1).to_broadcast([128, 16, GWIN]), ALU.is_equal).then_inc(oh1_ready, 1)
        if due(u - 1):
            dve.wait_ge(win_ps, u - 1)
        dve.tensor_tensor(
            oh2[:, par],
            rowrel[:, bass.ds(2 * u, 2)].unsqueeze(2).to_broadcast([128, 2, WIN]),
            iota[:, 0:WIN].unsqueeze(1).to_broadcast([128, 2, WIN]), ALU.is_equal).then_inc(oh2_ready, 1)

    def sum_groups(pe, u, par):
        pe.wait_ge(oh1_ready, u + 1)
        if due(u):
            pe.wait_ge(rows_ready, u)
        for h in range(2):
            pe.wait_ge(edges_in[2 * par + h], 8 * u + (16 - 8 * par))
            for j in range(2):
                for g in range(NG):
                    last = pe.matmul(psR[32 * g:32 * g + 32, h, :], oh1[:, par, 8 * h + 2 * g + j, :],
                                     ring[:, 2 * par + h, g, j * D:(j + 1) * D],
                                     start=(j == 0), stop=(j == 1), skip_group_check=True)
            last.then_inc(edges_used, 1)

    def rows_out(act, u, par):
        act.wait_ge(edges_used, 2 * u + 2)
        if due(u - 1):
            act.wait_ge(win_ps, u - 1)
        act.activation(rows[:, par], psR[:, :, :], ACT.Copy).then_inc(rows_ready, 1)

    def sum_windows(pe, u, par):
        pe.wait_ge(rows_ready, u + 1)
        pe.wait_ge(oh2_ready, u + 1)
        if due(u):
            pe.wait_ge(agg_added, u)
        for h in range(2):
            for f in range(KC):
                last = pe.matmul(psW[:, f, SHIFT * h:SHIFT * h + WIN], rows[:, par, h, 128 * f:128 * f + 128],
                                 oh2[:, par, h, :], start=(h == 0 and f == 0), stop=(h == 1 and f == 1),
                                 skip_group_check=True)
        last.then_inc(win_ps, 1)

    def add_window(dve, u, par):
        dve.wait_ge(win_ps, u + 1)
        dve.wait_ge(agg_added, u) if due(u) else dve.wait_ge(consts, 5)
        w = aggT[:, :, bass.ds(2 * SHIFT * u, PW)]
        dve.tensor_tensor(w, w, psW[:, :, 0:PW], ALU.add).then_inc(agg_added, 1)

    root_seed, root_step = sem("root_seed"), sem("root_step")

    def root_of(par):
        return nv[:, par], nh[:, par], ni[:, par], ny[:, par], nw[:, par]

    def seed_root(dve, var, tiles_of, done):
        v, h, i, y, _ = tiles_of
        dve.tensor_scalar(v, var, EPS, None, ALU.add).then_inc(root_seed, 1)
        dve.tensor_scalar(h, var, EPS, -0.5, ALU.add, ALU.mult).then_inc(root_seed, 1)
        dve.wait_ge(root_seed, 4 * done + 1)
        dve.tensor_scalar(i, v.bitcast(I32), 1, None, ALU.logical_shift_right).then_inc(root_seed, 1)
        dve.wait_ge(root_seed, 4 * done + 3)
        dve.tensor_scalar(y.bitcast(I32), i, -1.0, MAGIC, ALU.mult, ALU.add).then_inc(root_seed, 1)

    def newton_root(pool, tiles_of, done):
        _, h, _, y, w = tiles_of
        pool.wait_ge(root_seed, 4 * done + 4)
        c = ROOT_OPS * done
        for it in range(ROOT_STEPS):
            if it:
                pool.wait_ge(root_step, c)
            pool.tensor_tensor(w, y, y, ALU.mult).then_inc(root_step, 1)
            pool.wait_ge(root_step, c + 1)
            pool.tensor_tensor(w, w, h, ALU.mult).then_inc(root_step, 1)
            pool.wait_ge(root_step, c + 2)
            pool.tensor_tensor(w, w, half3[:].unsqueeze(1).to_broadcast(w.shape), ALU.add).then_inc(root_step, 1)
            pool.wait_ge(root_step, c + 3)
            pool.tensor_tensor(y, y, w, ALU.mult).then_inc(root_step, 1)
            c = c + 4

    def bcast(row, n=TOK):
        return row.partition_broadcast(n)

    attn_stack = ExitStack()
    wq = [sb(f"wq{i}", [128, KC, D], F32R, attn_stack) for i in range(2)]
    wo = [sb(f"wo{i}", [128, KC, D], F32R, attn_stack) for i in range(2)]
    kvm = [sb(f"kvm{i}", [128, KC, 128], F32R, attn_stack) for i in range(2)]
    ksm = [sb(f"ksm{i}", [128, KC, 128], F32R, attn_stack) for i in range(2)]
    xn = sb("xn", [TOK, 2, 2, D], F32, attn_stack)
    xt = [sb(f"xt{i}", [128, 2, KC, BLK], F32R, attn_stack) for i in range(2)]
    bq = sb("bq", [128, KC], F32, attn_stack)

    s1 = ExitStack()
    wkv = [sb(f"wkv{i}", [128, KC, 2 * D], F32R, s1) for i in range(2)]
    wraw = sb("wraw", [128, KC, 2, D], F32, s1)
    bkv = sb("bkv", [TOK, 4, 128], F32, s1)
    bn6 = sb("bn6", [TOK, 10, 6], F32, s1)
    kvt = sb("kvt", [TOK, 2, 2, 4, 130], F32, s1)
    kf_ = sb("kf", [128, 2, 2, D], F32, s1)
    ek_ = sb("ek", [128, 2, D], F32, s1)
    rk_ = sb("rk", [128, 2, D], F32, s1)
    kf, ek, rk = kf_[0:TOK], ek_[0:TOK], rk_[0:TOK]
    rowi = sb("rowi", [128, NSUP], I32, s1)

    def scratch(t, dims, shape, dt):
        flat = t[:].rearrange(dims).bitcast(dt)[:, 0:NSUP * shape]
        return flat.rearrange("p (s g) -> p s g", g=shape)

    dsti = scratch(kf_, "p a b n -> p (a b n)", 8, I32)
    basei = scratch(ek_, "p a n -> p (a n)", NG, I32)
    basef = scratch(rk_, "p a n -> p (a n)", NG, F32)
    spare = [(kf_[0:TOK].rearrange("p a b n -> p (a b n)"), NSUP * 8 + NT * i) for i in range(3)]
    spare.append((ek_[0:TOK].rearrange("p a n -> p (a n)"), NSUP * NG))
    rv, rh, ri, rw = (t[:, o:o + NT].unsqueeze(2) for t, o in spare)
    root_all = (rv, rh, ri.bitcast(I32), rstd[:], rw)
    wrel = scratch(rows, "p a b n -> p (a b n)", 8, F32)
    woff = sb("woff", [128, NSUP], F32, s1)
    rowoff = sb("rowoff", [128, NSUP], F32, s1)
    mm4 = sb("mm4", [128, 4], F32, s1)
    bad = sb("bad", [128, 4], F32, s1)
    badsum = sb("badsum", [128, 1], F32, s1)
    mask = rk_[:, 0, 0:128]
    kvf = ek_[:].rearrange("p a (c n) -> p a c n", c=KC)

    w_in = [sem("w_in_kv"), sem("w_in_qo"), sem("b_in")]
    w_split, w_rest = sem("w_split"), sem("w_rest")
    stats, dchk = sem("stats"), sem("dchk")
    mask_ready = sem("mask_ready")
    flag_ps, flag_set = sem("flag_ps"), sem("flag_set")
    xn_ready, xt_ps, xh_ready, xl_ready = sem("xn_ready"), sem("xt_ps"), sem("xh_ready"), sem("xl_ready")
    kv_ps, kvt_ready, ek_ready, kf_ready = (sem(n) for n in ("kv_ps", "kvt_ready", "ek_ready", "kf_ready"))
    kv_summed, kvm_f, kvm_h, kvm_l = sem("kv_summed"), sem("kvm_f"), sem("kvm_h"), sem("kvm_l")

    psT = bank(2)[:, 0:2 * BLK].rearrange("p (c n) -> p c n", c=KC)
    psKV = [bank(3), bank(4)]
    psA = bank(5)[:, 0:2 * 130].rearrange("p (c n) -> p c n", c=KC)
    xv = a["x"].rearrange("(t p) d -> p t d", p=TOK)
    FIRST_PAIRS = 28

    with nc.Block() as block:
        @block.sync
        def _(sp):
            sp.dma_start(dsti[:], a["dst_t"]).then_inc(dst_in, 16)
            sp.dma_start(basei[:].rearrange("p s g -> p (s g)"), bcast(a["dst_base"], 128)).then_inc(dst_in, 16)
            for g in range(NG):
                sp.dma_start(rowi[32 * g:32 * g + 32, :], bcast(a["dst_row"][g], 32)).then_inc(dst_in, 16)

            def step(k, kp):
                load_pair(sp, k + 2, kp)
                for c in range(3 * k + 6, min(3 * k + 9, 5)) if isinstance(k, int) else ():
                    sp.dma_start(x[:, 10 * c:10 * c + 10, :], xv[:, 10 * c:10 * c + 10, :]).then_inc(x_in[c], 16)
            run_steps(sp, step, -2, 3, 11, 26)

        @block.scalar
        def _(act):
            act.dma_start(wraw[:, :, 0, :], a["wk"].rearrange("(c p) n -> p c n", p=128)).then_inc(w_in[0], 16)
            act.dma_start(wraw[:, :, 1, :], a["wv"].rearrange("(c p) n -> p c n", p=128)).then_inc(w_in[0], 16)
            act.dma_start(bkv[:, 0:2, :].rearrange("p a n -> p (a n)"), bcast(a["bk"])).then_inc(w_in[2], 16)
            act.dma_start(bkv[:, 2:4, :].rearrange("p a n -> p (a n)"), bcast(a["bv"])).then_inc(w_in[2], 16)
            act.dma_start(bq[:], a["bq"]).then_inc(w_in[2], 16)
            act.wait_ge(w_in[0], 32)
            act.activation(wkv[0][:], wraw[:].rearrange("p c a n -> p c (a n)"), ACT.Copy).then_inc(w_split, 1)

            def step(k, kp):
                if live(k + 1):
                    act.wait_ge(xt_ps, k + 2)
                    if due(2 * k - 2 + 2):
                        act.wait_ge(kv_ps, 2 * k)
                    act.activation(xt[0][:, 1 - kp], psT[:, :, :], ACT.Copy).then_inc(xh_ready, 1)
                if live(k):
                    for t in range(2):
                        act.wait_ge(kvt_ready, 2 * k + t + 1)
                        if due(2 * k + t - 1):
                            act.wait_ge(kf_ready, 2 * k + t - 1)
                        act.activation(ek[:, t, :].rearrange("p (a n) -> p a n", a=2),
                                       kvt[:, kp, t, 0:2, 0:128], ACT.Exp)
                        act.activation(rk[:, t, :].rearrange("p (a n) -> p a n", a=2),
                                       kvt[:, kp, t, 0:2, 0:128], ACT.Relu).then_inc(ek_ready, 1)
                if isinstance(k, int) and k == 0:
                    act.wait_ge(w_rest, 1)
                    act.dma_start(wraw[:, :, 0, :], a["wq"].rearrange("(c p) n -> p c n", p=128)).then_inc(w_in[1], 16)
                    act.dma_start(wraw[:, :, 1, :], a["wo"].rearrange("(c p) n -> p c n", p=128)).then_inc(w_in[1], 16)
                if isinstance(k, int) and k == 23:
                    act.wait_ge(w_in[1], 32)
                    act.activation(wq[0][:], wraw[:, :, 0, :], ACT.Copy).then_inc(w_split, 1)
                    act.activation(wo[0][:], wraw[:, :, 1, :], ACT.Copy).then_inc(w_split, 1)
                rows_out(act, k + 2, kp)
            run_steps(act, step, -2, 1, 11, 26)
            act.wait_ge(kvm_f, 2)
            for i, w in enumerate((kvm, ksm)):
                act.activation(w[0][:], kvf[:, i], ACT.Copy).then_inc(kvm_h, 1)

        @block.gpsimd
        def _(pool):
            pool.memset(ones[:], 1.0).then_inc(consts, 1)
            pool.memset(ident[:], 0.0).then_inc(consts, 1)
            pool.iota(iota[:], pattern=[[1, WIN]], base=0, channel_multiplier=0,
                      allow_small_or_imprecise_dtypes=True).then_inc(consts, 1)
            pool.wait_ge(consts, 3)
            pool.affine_select(out=ident[:], in_=ident[:], compare_op=ALU.not_equal, fill=1.0, base=0,
                               pattern=[[-1, 128]], channel_multiplier=1).then_inc(consts, 1)
            pool.iota(woff[:], pattern=[[-SHIFT, NSUP]], base=PAD, channel_multiplier=0,
                      allow_small_or_imprecise_dtypes=True).then_inc(dst_ready, 1)
            for g in range(NG):
                pool.wait_ge(dst_ready, g + 1)
                pool.iota(rowoff[32 * g:32 * g + 32, :], pattern=[[-SHIFT, NSUP]], base=PAD, channel_multiplier=1,
                          allow_small_or_imprecise_dtypes=True).then_inc(dst_ready, 1)
            pool.wait_ge(dst_ready, 5)
            pool.memset(aggT[:], 0.0).then_inc(consts, 1)
            pool.memset(kvt[:, :, :, :, 128:130], 1.0).then_inc(consts, 1)
            pool.memset(half3[:], 1.5).then_inc(consts, 1)
            pool.wait_ge(consts, 7)
            newton_root(pool, root_all, 0)
            pool.wait_ge(dchk, 7)
            pool.affine_select(out=dstf[:, NSUP - 1, 0:2], in_=dstf[:, NSUP - 1, 0:2], compare_op=ALU.is_ge,
                               fill=-1.0, base=-OVER, pattern=[[1, 2]], channel_multiplier=2).then_inc(dst_ready, 1)
            pool.affine_select(out=rel[:, NSUP - 1, 0:2], in_=rel[:, NSUP - 1, 0:2], compare_op=ALU.is_ge,
                               fill=-1.0, base=-OVER, pattern=[[1, 2]], channel_multiplier=2).then_inc(dst_ready, 1)

            pool.wait_ge(kf_ready, NT)
            pool.memset(mask, 0.0).then_inc(mask_ready, 1)
            for h in range(4):
                pool.wait_ge(mask_ready, h + 1)
                pool.memset(mask[32 * h:32 * h + 32, 32 * h:32 * h + 32], 1.0).then_inc(mask_ready, 1)

        @block.vector
        def _(dve):
            dve.wait_ge(dst_in, 96)
            dve.tensor_copy(dstf[:], dsti[:]).then_inc(dchk, 1)
            dve.tensor_copy(basef[:], basei[:]).then_inc(dchk, 1)
            dve.tensor_copy(rowrel[:], rowi[:]).then_inc(dchk, 1)
            dve.wait_ge(dchk, 3)
            dve.wait_ge(dst_ready, 5)
            d4 = dstf[:].rearrange("p s (g j) -> p (s g) j", j=2)
            dve.tensor_tensor(rel[:].rearrange("p s (g j) -> p (s g) j", j=2), d4,
                              basef[:].rearrange("p s g -> p (s g)").unsqueeze(2).to_broadcast([128, NSUP * NG, 2]),
                              ALU.subtract).then_inc(dchk, 1)
            dve.tensor_tensor(rowrel[:], rowrel[:], rowoff[:], ALU.add).then_inc(dchk, 1)
            dve.tensor_tensor(wrel[:], dstf[:], woff[:].unsqueeze(2).to_broadcast([128, NSUP, 8]), ALU.add)\
               .then_inc(dchk, 1)
            dve.wait_ge(dchk, 6)
            dve.tensor_reduce(mm4[:, 0:1], rel[:].rearrange("p s c -> p (s c)"), AX.X, ALU.min)
            dve.tensor_reduce(mm4[:, 1:2], rel[:].rearrange("p s c -> p (s c)"), AX.X, ALU.max)
            dve.tensor_reduce(mm4[:, 2:3], wrel[:].rearrange("p s c -> p (s c)"), AX.X, ALU.min)
            dve.tensor_reduce(mm4[:, 3:4], wrel[:].rearrange("p s c -> p (s c)"), AX.X, ALU.max).then_inc(dchk, 1)
            dve.wait_ge(dchk, 7)
            for c in range(4):
                limit, op = ((0.0, ALU.is_lt), (GWIN - 1.0, ALU.is_gt), (0.0, ALU.is_lt), (WIN - 1.0, ALU.is_gt))[c]
                last = dve.tensor_scalar(bad[:, c:c + 1], mm4[:, c:c + 1], limit, None, op)
            last.then_inc(dchk, 1)
            dve.wait_ge(dchk, 8)
            dve.tensor_reduce(badsum[:], bad[:], AX.X, ALU.add).then_inc(dchk, 1)

            for c in range(5):
                dve.wait_ge(x_in[c], 16)
                if c:
                    dve.wait_ge(stats, 2 * c)
                for t in range(10):
                    last = dve.bn_stats(bn6[:, t, :], x[:, 10 * c + t, :])
                last.then_inc(stats, 1)
                dve.wait_ge(stats, 2 * c + 1)
                for t in range(10):
                    last = dve.bn_aggr(mv[:, 10 * c + t, :], bn6[:, t, :])
                last.then_inc(stats, 1)
            dve.wait_ge(stats, 10)
            seed_root(dve, mv[:, :, 1:2], root_all, 0)
            dve.wait_ge(w_split, 1)
            dve.tensor_tensor(wkv[1][:], wraw[:].rearrange("p c a n -> p c (a n)"), wkv[0][:].bitcast(F32),
                              ALU.subtract).then_inc(w_rest, 1)
            dve.wait_ge(flag_ps, 1)
            dve.tensor_copy(flag[:], bank(7)[0:1, 0:1]).then_inc(flag_set, 1)
            dve.wait_ge(dst_ready, 7)
            dve.wait_ge(w_in[2], 48)
            dve.wait_ge(consts, 6)

            def normalize(b, par):
                if due(b - 1):
                    dve.wait_ge(xt_ps, b - 1)
                for t in range(2):
                    last = dve.tensor_scalar(xn[:, par, t, :], x[:, bass.ds(2 * b + t, 1), :].rearrange("p o d -> p (o d)"),
                                             mv[:, bass.ds(2 * b + t, 1), 0:1].rearrange("p o d -> p (o d)"),
                                             rstd[:, bass.ds(2 * b + t, 1), :].rearrange("p o d -> p (o d)"),
                                             ALU.subtract, ALU.mult)
                last.then_inc(xn_ready, 1)

            def step(k, kp):
                onehots(dve, k + 2, kp)
                if live(k + 2):
                    if isinstance(k, int) and k == -2:
                        dve.wait_ge(root_step, ROOT_OPS)
                    normalize(k + 2, kp)
                if live(k + 1):
                    dve.wait_ge(xh_ready, k + 2)
                    dve.tensor_tensor(xt[1][:, 1 - kp], psT[:, :, :], xt[0][:, 1 - kp].bitcast(F32),
                                      ALU.subtract).then_inc(xl_ready, 1)
                if live(k - 1):
                    for t in range(2):
                        n = 2 * (k - 1) + t + 1
                        dve.wait_ge(ek_ready, n)
                        if due(k - 2):
                            dve.wait_ge(kv_summed, k - 2)
                        dve.scalar_tensor_tensor(kf[:, 1 - kp, t, :], ek[:, t, :], 1.0, rk[:, t, :],
                                                 ALU.min, ALU.add).then_inc(kf_ready, 1)
                if live(k):
                    for t in range(2):
                        dve.wait_ge(kv_ps, 2 * k + t + 1)
                        if due(k - 1):
                            dve.wait_ge(kv_summed, k - 1)
                        dve.tensor_tensor(kvt[:, kp, t, :, 0:128], psKV[t][0:TOK, :].rearrange("p (a n) -> p a n", a=4),
                                          bkv[:], ALU.add).then_inc(kvt_ready, 1)
                if isinstance(k, int) and k == 24:
                    dve.wait_ge(w_split, 3)
                    dve.tensor_tensor(wq[1][:], wraw[:, :, 0, :], wq[0][:].bitcast(F32), ALU.subtract).then_inc(w_rest, 1)
                    dve.tensor_tensor(wo[1][:], wraw[:, :, 1, :], wo[0][:].bitcast(F32), ALU.subtract).then_inc(w_rest, 1)
                if live(k + 1, FIRST_PAIRS - 1):
                    add_window(dve, k + 1, 1 - kp)
            run_steps(dve, step, -2, 2, 10, 26)
            dve.wait_ge(kv_summed, NB)
            dve.wait_ge(mask_ready, 5)
            dve.tensor_tensor(kvf[:, 0], psA[:, :, 0:128], mask.unsqueeze(1).to_broadcast([128, KC, 128]),
                              ALU.mult).then_inc(kvm_f, 1)
            for c in range(KC):
                last = dve.tensor_scalar(kvf[:, 1, c, :], mask, psA[:, c, 128:129], None, ALU.mult)
            last.then_inc(kvm_f, 1)
            dve.wait_ge(kvm_f, 2)
            for i, w in enumerate((kvm, ksm)):
                dve.wait_ge(kvm_h, i + 1)
                dve.tensor_tensor(w[1][:], kvf[:, i], w[0][:].bitcast(F32), ALU.subtract).then_inc(kvm_l, 1)

        @block.tensor
        def _(pe):
            pe.wait_ge(consts, 4)
            pe.wait_ge(dchk, 9)
            pe.matmul(bank(7)[0:1, 0:1], badsum[:], ones[:, 0:1], start=True, stop=True).then_inc(flag_ps, 1)
            pe.wait_ge(dst_ready, 7)

            def step(k, kp):
                if live(k + 1):
                    pe.wait_ge(xn_ready, k + 2)
                    if due(k + 1):
                        pe.wait_ge(xl_ready, k + 1)
                    for t in range(2):
                        for c in range(KC):
                            last = pe.transpose(psT[:, c, TOK * t:TOK * t + TOK], xn[:, 1 - kp, t, 128 * c:128 * c + 128],
                                                ident[0:TOK, 0:TOK])
                    last.then_inc(xt_ps, 1)
                sum_groups(pe, k + 2, kp)
                if live(k):
                    pe.wait_ge(xl_ready, k + 1)
                    if isinstance(k, int) and k == 0:
                        pe.wait_ge(w_rest, 1)
                    for t in range(2):
                        if due(2 * k + t - 1):
                            pe.wait_ge(kvt_ready, 2 * k + t - 1)
                        for c in range(KC):
                            last = three_products(pe, psKV[t][0:TOK, :],
                                                  [w[:, kp, c, TOK * t:TOK * t + TOK] for w in xt],
                                                  [w[:, c, :] for w in wkv], c == 0, c == KC - 1)
                        last.then_inc(kv_ps, 1)
                if live(k + 1, FIRST_PAIRS - 1):
                    sum_windows(pe, k + 1, 1 - kp)
                if live(k - 1):
                    pe.wait_ge(kf_ready, 2 * k)
                    for t in range(2):
                        for c in range(KC):
                            first = isinstance(k, int) and k == 1 and t == 0 and c == 0
                            end = isinstance(k, int) and k == NB and t == 1
                            last = pe.matmul(psA[:, c, :], kf[:, 1 - kp, t, 128 * c:128 * c + 128],
                                             kvt[:, 1 - kp, t, 2 + c, :], start=first, stop=end, skip_group_check=True)
                    last.then_inc(kv_summed, 1)
            run_steps(pe, step, -2, 2, 10, 26)


    s1.close()
    s2 = ExitStack()
    eq = sb("eq", [128, KC, BLK], F32, s2)
    rq = sb("rq", [128, KC, BLK], F32, s2)
    qf = sb("qf", [128, KC, BLK], F32, s2)
    qs = [sb(f"qs{i}", [128, 2, KC, BLK], F32R, s2) for i in range(2)]
    den = sb("den", [128, KC, BLK], F32, s2)
    rden = sb("rden", [128, KC, BLK], F32, s2)
    at = sb("at", [128, KC, BLK], F32, s2)
    ats = [sb(f"ats{i}", [128, 2, KC, BLK], F32R, s2) for i in range(2)]
    b_out = sb("b_out", [TOK, D], F32, s2)
    b_out2 = sb("b_out2", [TOK, D], F32, s2)
    xnb = sb("xnb", [TOK, 2, D], F32, s2)
    tiny = sb("tiny", [128, 1], F32, s2)

    b2_in, b2_sum = sem("b2_in"), sem("b2_sum")
    xn2_ready, xt2_ps, xh2_ready, xl2_ready = (sem(n) for n in ("xn2_ready", "xt2_ps", "xh2_ready", "xl2_ready"))
    q_ps, eq_ready, rq_ready, q_ready, qh_ready, ql_ready = (
        sem(n) for n in ("q_ps", "eq_ready", "rq_ready", "q_ready", "qh_ready", "ql_ready"))
    att_ps, den_ready, rden_ready, at_ready, ah_ready, al_ready = (
        sem(n) for n in ("att_ps", "den_ready", "rden_ready", "at_ready", "ah_ready", "al_ready"))
    mix_ps, xnb_ready, x_xn, x_mixed = sem("mix_ps"), sem("xnb_ready"), sem("x_xn"), sem("x_mixed")

    def halves(i):
        return bank(i)[:, 0:KC * BLK].rearrange("p (c n) -> p c n", c=KC)

    def tiles(i):
        return bank(i)[0:TOK, :].rearrange("p (t n) -> p t n", t=2)

    psT, psQ, psN, psD, psM = halves(2), halves(3), halves(4), halves(5), tiles(6)
    U0 = FIRST_PAIRS

    with nc.Block() as block:
        @block.sync
        def _(sp):
            def step(k, kp):
                if live(k + 2, NPAIR - U0):
                    load_pair(sp, k + (2 + U0), kp)
            run_steps(sp, step, -2, 2, 9, 22)

        @block.scalar
        def _(act):
            act.dma_start(b_out[:], bcast(a["bo"])).then_inc(b2_in, 16)
            act.dma_start(b_out2[:], bcast(a["gnn_b2"])).then_inc(b2_in, 16)

            def step(k, kp):
                if live(k + 1):
                    act.wait_ge(xt2_ps, k + 2)
                    if due(k):
                        act.wait_ge(q_ps, k)
                    act.activation(xt[0][:, 1 - kp], psT, ACT.Copy).then_inc(xh2_ready, 1)
                if live(k):
                    act.wait_ge(q_ps, k + 1)
                    if due(k):
                        act.wait_ge(q_ready, k)
                    for c in range(KC):
                        last = act.activation(eq[:, c, :], psQ[:, c, :], ACT.Exp, bias=bq[:, c:c + 1])
                    last.then_inc(eq_ready, 1)
                if live(k - 1):
                    act.wait_ge(att_ps, k)
                    if due(k - 1):
                        act.wait_ge(rden_ready, k - 1)
                    act.activation(den[:], psD, ACT.Identity, bias=tiny[:]).then_inc(den_ready, 1)
                if live(k):
                    act.wait_ge(q_ready, k + 1)
                    if due(k - 1):
                        act.wait_ge(att_ps, k - 1)
                    act.activation(qs[0][:, kp], qf[:], ACT.Copy).then_inc(qh_ready, 1)
                if live(k + 2, NPAIR - U0):
                    rows_out(act, k + (2 + U0), kp)
                if live(k - 1):
                    act.wait_ge(at_ready, k)
                    if due(k - 2):
                        act.wait_ge(mix_ps, k - 2)
                    act.activation(ats[0][:, 1 - kp], at[:], ACT.Copy).then_inc(ah_ready, 1)
            run_steps(act, step, -2, 2, 9, 27)

        @block.gpsimd
        def _(pool):
            pool.memset(tiny[:], 1e-6).then_inc(b2_sum, 1)
            pool.wait_ge(b2_in, 32)
            pool.tensor_tensor(b_out[:], b_out[:], b_out2[:], ALU.add).then_inc(b2_sum, 1)
            pool.wait_ge(b2_sum, 2)

            def step(k, kp):
                if live(k):
                    pool.wait_ge(xn2_ready, k + 1)
                    if due(k):
                        pool.wait_ge(x_xn, k)
                    pool.tensor_tensor(xnb[:], xn[:, kp], b_out[:].unsqueeze(1).to_broadcast([TOK, 2, D]), ALU.add)\
                        .then_inc(xnb_ready, 1)
                    pool.wait_ge(xnb_ready, k + 1)
                    xb = x[:, bass.ds(2 * k, 2), :]
                    pool.tensor_tensor(xb, xb, xnb[:], ALU.add).then_inc(x_xn, 1)
                    pool.wait_ge(qh_ready, k + 1)
                    pool.tensor_tensor(qs[1][:, kp], qf[:], qs[0][:, kp].bitcast(F32), ALU.subtract)\
                        .then_inc(ql_ready, 1)
                if live(k - 1):
                    pool.wait_ge(ah_ready, k)
                    pool.tensor_tensor(ats[1][:, 1 - kp], at[:], ats[0][:, 1 - kp].bitcast(F32), ALU.subtract)\
                        .then_inc(al_ready, 1)
            run_steps(pool, step, -2, 2, 9, 27)

        @block.vector
        def _(dve):
            def normalize(b, par):
                if due(b - 1):
                    dve.wait_ge(xt2_ps, b - 1)
                    dve.wait_ge(x_xn, b - 1)
                for t in range(2):
                    last = dve.tensor_scalar(xn[:, par, t, :], x[:, bass.ds(2 * b + t, 1), :].rearrange("p o d -> p (o d)"),
                                             mv[:, bass.ds(2 * b + t, 1), 0:1].rearrange("p o d -> p (o d)"),
                                             rstd[:, bass.ds(2 * b + t, 1), :].rearrange("p o d -> p (o d)"),
                                             ALU.subtract, ALU.mult)
                last.then_inc(xn2_ready, 1)

            def step(k, kp):
                if live(k + 2, NPAIR - U0):
                    onehots(dve, k + (2 + U0), kp)
                if live(k + 2):
                    normalize(k + 2, kp)
                if live(k + 1):
                    dve.wait_ge(xh2_ready, k + 2)
                    dve.tensor_tensor(xt[1][:, 1 - kp], psT, xt[0][:, 1 - kp].bitcast(F32),
                                      ALU.subtract).then_inc(xl2_ready, 1)
                if live(k - 1):
                    dve.wait_ge(den_ready, k)
                    dve.reciprocal(rden[:], den[:]).then_inc(rden_ready, 1)
                    dve.wait_ge(rden_ready, k)
                    if due(k - 1):
                        dve.wait_ge(al_ready, k - 1)
                    dve.tensor_tensor(at[:], psN, rden[:], ALU.mult).then_inc(at_ready, 1)
                if live(k):
                    dve.wait_ge(eq_ready, k + 1)
                    for c in range(KC):
                        last = dve.tensor_scalar(rq[:, c, :], psQ[:, c, :], bq[:, c:c + 1], 0.0, ALU.add, ALU.max)
                    last.then_inc(rq_ready, 1)
                    dve.wait_ge(rq_ready, k + 1)
                    if due(k):
                        dve.wait_ge(ql_ready, k)
                    dve.scalar_tensor_tensor(qf[:], eq[:], 1.0, rq[:], ALU.min, ALU.add).then_inc(q_ready, 1)
                if live(k - 2):
                    dve.wait_ge(mix_ps, k - 1)
                    dve.wait_ge(x_xn, k - 1)
                    xb = x[:, bass.ds(2 * (k - 2), 2), :]
                    dve.tensor_tensor(xb, xb, psM, ALU.add).then_inc(x_mixed, 1)
                if live(k + 2, NPAIR - U0 + 1):
                    add_window(dve, k + (1 + U0), 1 - kp)
            run_steps(dve, step, -2, 2, 9, 27)

        @block.tensor
        def _(pe):
            def step(k, kp):
                if live(k + 1):
                    pe.wait_ge(xn2_ready, k + 2)
                    if due(k + 1):
                        pe.wait_ge(xl2_ready, k + 1)
                    for t in range(2):
                        for c in range(KC):
                            last = pe.transpose(psT[:, c, TOK * t:TOK * t + TOK], xn[:, 1 - kp, t, 128 * c:128 * c + 128],
                                                ident[0:TOK, 0:TOK])
                    last.then_inc(xt2_ps, 1)
                if live(k):
                    pe.wait_ge(xl2_ready, k + 1)
                    if due(k):
                        pe.wait_ge(rq_ready, k)
                        pe.wait_ge(eq_ready, k)
                    for o in range(KC):
                        for c in range(KC):
                            last = three_products(pe, psQ[:, o, :], [w[:, c, 128 * o:128 * o + 128] for w in wq],
                                                  [w[:, kp, c, :] for w in xt], c == 0, c == KC - 1)
                    last.then_inc(q_ps, 1)
                if live(k + 2, NPAIR - U0 + 1):
                    sum_windows(pe, k + (1 + U0), 1 - kp)
                if live(k - 1):
                    pe.wait_ge(ql_ready, k)
                    if due(k - 1):
                        pe.wait_ge(den_ready, k - 1)
                        pe.wait_ge(at_ready, k - 1)
                    for m, o_ps in ((ksm, psD), (kvm, psN)):
                        for c in range(KC):
                            last = three_products(pe, o_ps[:, c, :], [w[:, c, :] for w in m],
                                                  [w[:, 1 - kp, c, :] for w in qs], True, True)
                    last.then_inc(att_ps, 1)
                if live(k + 2, NPAIR - U0):
                    sum_groups(pe, k + (2 + U0), kp)
                if live(k - 2):
                    pe.wait_ge(al_ready, k - 1)
                    if due(k - 2):
                        pe.wait_ge(x_mixed, k - 2)
                    for t in range(2):
                        for c in range(KC):
                            last = three_products(pe, psM[:, t, :], [w[:, kp, c, TOK * t:TOK * t + TOK] for w in ats],
                                                  [w[:, c, :] for w in wo], c == 0, c == KC - 1)
                    last.then_inc(mix_ps, 1)
            run_steps(pe, step, -2, 2, 9, 27)

    s2.close()
    attn_stack.close()
    edge_stack.close()
    sg = ExitStack()
    g_edges = sb("g_edges", [128, NG, 2 * D], F32, sg)
    g_oh = sb("g_oh", [128, 8, BLK], F32, sg)
    g_node = sb("g_node", [128, BLK], F32, sg)
    g_in, g_ready, g_ps, g_added, g_nodes, g_zero = (
        sem(n) for n in ("g_in", "g_ready", "g_ps", "g_added", "g_nodes", "g_zero"))
    psG = halves(0)

    with nc.Block() as block:
        @block.sync
        def _(sp):
            def load(n, src):
                sp.wait_ge(g_added, n)
                sp.dma_start(g_edges[:], src).then_inc(g_in, 16)

            general = sp.value_load(flag[0:1, 0:1], min_val=0, max_val=512)
            with sp.If(general != 0):
                with sp.Fori(0, NB) as nb:
                    with sp.Fori(0, NSUP - 1) as s:
                        load(nb * NSUP + s, e_sup[bass.ds(s, 1)].rearrange("o p g n -> (o p) g n"))
                    load(nb * NSUP + (NSUP - 1), e_last)
            sp.end_ifs()

        @block.gpsimd
        def _(pool):
            pool.iota(g_node[:], pattern=[[1, BLK]], base=-BLK, channel_multiplier=0,
                      allow_small_or_imprecise_dtypes=True).then_inc(g_zero, 1)

        @block.vector
        def _(dve):
            def take(n, s, nb):
                dve.wait_ge(g_nodes, nb + 1)
                dve.tensor_tensor(g_oh[:], dstf[:, bass.ds(s, 1), :].rearrange("p s c -> p (s c)").unsqueeze(2).to_broadcast([128, 8, BLK]),
                                  g_node[:].unsqueeze(1).to_broadcast([128, 8, BLK]), ALU.is_equal).then_inc(g_ready, 1)
                dve.wait_ge(g_ps, n + 1)
                w = aggT[:, :, bass.ds(BLK * nb + PAD, BLK)]
                dve.tensor_tensor(w, w, psG, ALU.add).then_inc(g_added, 1)
                dve.wait_ge(g_added, n + 1)

            dve.wait_ge(g_zero, 1)
            general = dve.value_load(flag[0:1, 0:1], min_val=0, max_val=512)
            with dve.If(general != 0):
                dve.memset(aggT[:], 0.0).then_inc(g_zero, 1)
                dve.wait_ge(g_zero, 2)
                with dve.Fori(0, NB) as nb:
                    dve.tensor_scalar(g_node[:], g_node[:], float(BLK), None, ALU.add).then_inc(g_nodes, 1)
                    with dve.Fori(0, NSUP - 1) as s:
                        take(nb * NSUP + s, s, nb)
                    take(nb * NSUP + (NSUP - 1), NSUP - 1, nb)
            dve.end_ifs()

        @block.tensor
        def _(pe):
            def sums(n):
                pe.wait_ge(g_in, 16 * n + 16)
                pe.wait_ge(g_ready, n + 1)
                for f in range(KC):
                    for c in range(8):
                        o = (c % 2) * D + 128 * f
                        last = pe.matmul(psG[:, f, :], g_edges[:, c // 2, o:o + 128], g_oh[:, c, :],
                                         start=(c == 0), stop=(c == 7))
                last.then_inc(g_ps, 1)

            general = pe.value_load(flag[0:1, 0:1], min_val=0, max_val=512)
            with pe.If(general != 0):
                with pe.Fori(0, NB * NSUP) as n:
                    sums(n)
            pe.end_ifs()
    sg.close()

    s3 = ExitStack()
    raw3 = sb("raw3", [128, 2, KC, D], F32, s3)
    w1 = [sb(f"w1{i}", [128, KC, D], F32R, s3) for i in range(2)]
    w2 = [sb(f"w2{i}", [128, KC, D], F32R, s3) for i in range(2)]
    b1 = sb("b1", [128, KC], F32, s3)
    ag = [sb(f"ag{i}", [128, 2, KC, BLK], F32R, s3) for i in range(2)]
    z = sb("z", [128, KC, BLK], F32, s3)
    hf = sb("hf", [128, KC, BLK], F32, s3)
    hs = [sb(f"hs{i}", [128, 2, KC, BLK], F32R, s3) for i in range(2)]
    xn3 = sb("xn3", [TOK, 2, 2, D], F32, s3)
    bn3 = sb("bn3", [TOK, 2, 6], F32, s3)
    x1 = sb("x1", [TOK, 2, 2, D], F32, s3)

    w3_in, w3_h, w3_l = sem("w3_in"), sem("w3_h"), sem("w3_l")
    gh_ready, gl_ready, h_ps, z_ready, hf_ready, hh_ready, hl_ready, y_ps = (
        sem(n) for n in ("gh_ready", "gl_ready", "h_ps", "z_ready", "hf_ready", "hh_ready", "hl_ready", "y_ps"))
    x1_ready, bn3_ready, mv3_ready, xn3_ready, mean_ps, mean_out = (
        sem(n) for n in ("x1_ready", "bn3_ready", "mv3_ready", "xn3_ready", "mean_ps", "mean_out"))
    x1_kept = sem("x1_kept")
    psH, psY, psMean = halves(0), tiles(1), bank(2)[:, 0:KC]

    with nc.Block() as block:
        @block.sync
        def _(sp):
            sp.dma_start(raw3[:, 0], a["gnn_w1t"].rearrange("(c p) n -> p c n", p=128)).then_inc(w3_in, 16)
            sp.dma_start(raw3[:, 1], a["gnn_w2t"].rearrange("(c p) n -> p c n", p=128)).then_inc(w3_in, 16)
            sp.dma_start(b1[:], a["gnn_b1"]).then_inc(w3_in, 16)

        @block.scalar
        def _(act):
            act.wait_ge(w3_in, 48)
            act.activation(w1[0][:], raw3[:, 0], ACT.Copy).then_inc(w3_h, 1)
            act.activation(w2[0][:], raw3[:, 1], ACT.Copy).then_inc(w3_h, 1)

            def step(k, kp):
                if live(k):
                    if due(k - 1):
                        act.wait_ge(h_ps, k - 1)
                    act.activation(ag[0][:, kp], aggT[:, :, bass.ds(BLK * k + PAD, BLK)], ACT.Copy).then_inc(gh_ready, 1)
                if live(k - 1):
                    act.wait_ge(h_ps, k)
                    if due(k - 1):
                        act.wait_ge(hf_ready, k - 1)
                    for c in range(KC):
                        last = act.activation(z[:, c, :], psH[:, c, :], ACT.Identity, bias=b1[:, c:c + 1])
                    last.then_inc(z_ready, 1)
                    act.wait_ge(hf_ready, k)
                    if due(k - 2):
                        act.wait_ge(y_ps, k - 2)
                    act.activation(hs[0][:, 1 - kp], hf[:], ACT.Copy).then_inc(hh_ready, 1)
                if live(k - 2):
                    act.wait_ge(x1_ready, k - 1)
                    act.activation(x[:, bass.ds(2 * (k - 2), 2), :], x1[:, kp], ACT.Copy).then_inc(x1_kept, 1)
            run_steps(act, step, 0, 3, 11, 29)

        @block.gpsimd
        def _(pool):
            def step(k, kp):
                if live(k):
                    pool.wait_ge(gh_ready, k + 1)
                    pool.tensor_tensor(ag[1][:, kp], aggT[:, :, bass.ds(BLK * k + PAD, BLK)],
                                       ag[0][:, kp].bitcast(F32), ALU.subtract).then_inc(gl_ready, 1)
                if live(k - 3):
                    newton_root(pool, root_of(1 - kp), k - 2)
            run_steps(pool, step, 0, 3, 11, 29)

        @block.vector
        def _(dve):
            for i, w in enumerate((w1, w2)):
                dve.wait_ge(w3_h, i + 1)
                dve.tensor_tensor(w[1][:], raw3[:, i], w[0][:].bitcast(F32), ALU.subtract).then_inc(w3_l, 1)

            def step(k, kp):
                if live(k - 4):
                    dve.wait_ge(root_step, ROOT_OPS * (k - 2))
                    dve.tensor_scalar(rstd[:, bass.ds(2 * (k - 4), 2), :], ny[:, kp], 1.0, None, ALU.mult)
                    dve.tensor_scalar(mv[:, bass.ds(2 * (k - 4), 2), 0:1], mvs[:, kp, :, 0:1], 1.0, None, ALU.mult)
                    dve.wait_ge(x1_kept, k - 3)
                    if due(k - 5):
                        dve.wait_ge(mean_ps, k - 5)
                    for t in range(2):
                        n = 2 * (k - 4) + t
                        last = dve.tensor_scalar(xn3[:, kp, t, :], x[:, bass.ds(n, 1), :].rearrange("p o d -> p (o d)"),
                                                 mvs[:, kp, t, 0:1], ny[:, kp, t, :], ALU.subtract, ALU.mult)
                    last.then_inc(xn3_ready, 1)
                if live(k - 1):
                    dve.wait_ge(z_ready, k)
                    if due(k - 1):
                        dve.wait_ge(hl_ready, k - 1)
                    dve.scalar_tensor_tensor(hf[:], z[:], SLOPE, z[:], ALU.mult, ALU.max).then_inc(hf_ready, 1)
                if live(k - 2):
                    dve.wait_ge(y_ps, k - 1)
                    if due(k - 3):
                        dve.wait_ge(x1_kept, k - 3)
                    dve.tensor_tensor(x1[:, kp], x[:, bass.ds(2 * (k - 2), 2), :], psY, ALU.add).then_inc(x1_ready, 1)
                    dve.wait_ge(x1_ready, k - 1)
                    for t in range(2):
                        last = dve.bn_stats(bn3[:, t, :], x1[:, kp, t, :])
                    last.then_inc(bn3_ready, 1)
                if live(k - 2):
                    dve.wait_ge(bn3_ready, k - 1)
                if live(k - 1):
                    dve.wait_ge(hh_ready, k)
                    dve.tensor_tensor(hs[1][:, 1 - kp], hf[:], hs[0][:, 1 - kp].bitcast(F32),
                                      ALU.subtract).then_inc(hl_ready, 1)
                if live(k - 2):
                    for t in range(2):
                        last = dve.bn_aggr(mvs[:, kp, t, :], bn3[:, t, :])
                    last.then_inc(mv3_ready, 1)
                    dve.wait_ge(mv3_ready, k - 1)
                    seed_root(dve, mvs[:, kp, :, 1:2], root_of(kp), k - 1)
            run_steps(dve, step, 0, 5, 10, 29)
            dve.wait_ge(mean_ps, NB)
            dve.tensor_scalar(mean_t[:], psMean, 1.0 / N, None, ALU.mult).then_inc(mean_out, 1)

        @block.tensor
        def _(pe):
            pe.wait_ge(w3_l, 2)

            def step(k, kp):
                if live(k):
                    pe.wait_ge(gl_ready, k + 1)
                    if due(k):
                        pe.wait_ge(z_ready, k)
                    for o in range(KC):
                        for c in range(KC):
                            last = three_products(pe, psH[:, o, :], [w[:, c, 128 * o:128 * o + 128] for w in w1],
                                                  [w[:, kp, c, :] for w in ag], c == 0, c == KC - 1)
                    last.then_inc(h_ps, 1)
                if live(k - 4):
                    pe.wait_ge(xn3_ready, k - 3)
                    for t in range(2):
                        for c in range(KC):
                            first = isinstance(k, int) and k == 4 and t == 0 and c == 0
                            end = isinstance(k, int) and k == NB + 3 and t == 1
                            last = pe.matmul(psMean[:, c:c + 1], xn3[:, kp, t, 128 * c:128 * c + 128], ones[0:TOK, 0:1],
                                             start=first, stop=end, skip_group_check=True)
                    last.then_inc(mean_ps, 1)
                if live(k - 1):
                    pe.wait_ge(hl_ready, k)
                    if due(k - 1):
                        pe.wait_ge(x1_ready, k - 1)
                    for t in range(2):
                        for c in range(KC):
                            last = three_products(pe, psY[:, t, :], [w[:, 1 - kp, c, TOK * t:TOK * t + TOK] for w in hs],
                                                  [w[:, c, :] for w in w2], c == 0, c == KC - 1)
                    last.then_inc(y_ps, 1)
            run_steps(pe, step, 0, 5, 10, 29)
    s3.close()
    agg_stack.close()

    raw1 = sb("raw1", [128, TOPK, KC, FF])
    raw2 = sb("raw2", [128, TOPK, FC, D])
    ws2 = sb("ws2", [128, TOPK, FC, D])
    e1 = [sb(f"e1{i}", [128, TOPK, KC, FF], F32R) for i in range(2)]
    e2 = [sb(f"e2{i}", [128, TOPK, FC, D], F32R) for i in range(2)]
    eb1 = sb("eb1", [128, TOPK, FC])
    eb2 = sb("eb2", [TOK, TOPK, D])
    b2w = sb("b2w", [TOK, D])
    gamma, beta = sb("gamma", [TOK, D]), sb("beta", [TOK, D])
    wr = sb("wr", [128, KC, EXP])
    br = sb("br", [1, EXP])
    r = sb("r", [1, 12, EXP])
    idx = sb("idx", [1, EXP], U32)
    wb = sb("wb", [128, TOPK])
    r_in, r_dve, r_act, r_ps = sem("r_in"), sem("r_dve"), sem("r_act"), sem("r_ps")
    idx_ready = sem("idx_ready")
    e1_in, e2_in, eb_in, e_h, e_l = sem("e1_in"), sem("e2_in"), sem("eb_in"), sem("e_h"), sem("e_l")

    with nc.Block() as block:
        @block.sync
        def _(sp):
            sp.dma_start(wr[:], a["wr"].rearrange("(c p) n -> p c n", p=128)).then_inc(r_in, 16)
            sp.dma_start(br[:], a["br"]).then_inc(r_in, 16)
            sp.dma_start(gamma[:], bcast(a["gamma"])).then_inc(r_in, 16)
            sp.dma_start(beta[:], bcast(a["beta"])).then_inc(r_in, 16)
            sp.wait_ge(idx_ready, 1)
            for i in range(TOPK):
                e = sp.value_load(idx[0:1, i:i + 1], min_val=0, max_val=EXP - 1)
                sp.dma_start(raw1[:, i], a["w1"].rearrange("e (c p) n -> e p c n", p=128)[bass.ds(e, 1)]
                             .rearrange("o p c n -> (o p) c n")).then_inc(e1_in, 16)
                sp.dma_start(raw2[:, i], a["w2"].rearrange("e (c p) n -> e p c n", p=128)[bass.ds(e, 1)]
                             .rearrange("o p c n -> (o p) c n")).then_inc(e2_in, 16)
                sp.dma_start(eb1[:, i], a["b1"][bass.ds(e, 1)].rearrange("o p c -> (o p) c")).then_inc(eb_in, 16)
                sp.dma_start(eb2[:, i], bcast(a["b2"][bass.ds(e, 1)].rearrange("o n -> (o n)"))).then_inc(eb_in, 16)

        @block.scalar
        def _(act):
            act.wait_ge(r_dve, 3)
            act.activation(r[:, 1, :], r[:, 0, :], ACT.Exp, bias=r[:, 8, 0:1]).then_inc(r_act, 1)
            act.wait_ge(r_dve, 11)
            act.activation(r[:, 4, :], r[:, 3, :], ACT.Exp, bias=r[:, 8, 3:4]).then_inc(r_act, 1)
            act.wait_ge(r_dve, 17)
            act.activation(r[:, 7, 0:TOPK], r[:, 6, 0:TOPK], ACT.Exp, bias=r[:, 8, 6:7]).then_inc(r_act, 1)
            act.wait_ge(e1_in, 16 * TOPK)
            act.activation(e1[0][:], raw1[:], ACT.Copy).then_inc(e_h, 1)
            act.wait_ge(e_l, 1)
            act.activation(e2[0][:], ws2[:], ACT.Copy).then_inc(e_h, 1)

        @block.vector
        def _(dve):
            n = [0]

            def link(ins):
                n[0] += 1
                ins.then_inc(r_dve, 1)
                dve.wait_ge(r_dve, n[0])

            def softmax(src, dst, col, act_done, width):
                link(dve.tensor_reduce(r[:, 8, col + 1:col + 2], r[:, src, 0:width], AX.X, ALU.max))
                link(dve.tensor_scalar(r[:, 8, col:col + 1], r[:, 8, col + 1:col + 2], -1.0, None, ALU.mult))
                dve.wait_ge(r_act, act_done)
                link(dve.tensor_reduce(r[:, 8, col + 2:col + 3], r[:, src + 1, 0:width], AX.X, ALU.add))
                link(dve.reciprocal(r[:, 9, col:col + 1], r[:, 8, col + 2:col + 3]))
                link(dve.tensor_scalar(r[:, dst, 0:width], r[:, src + 1, 0:width], r[:, 9, col:col + 1], None, ALU.mult))

            dve.wait_ge(r_in, 64)
            dve.wait_ge(r_ps, 1)
            link(dve.tensor_tensor(r[:, 0, :], bank(3)[0:1, 0:EXP], br[:], ALU.add))
            softmax(0, 2, 0, 1, EXP)
            link(dve.tensor_scalar(r[:, 10, :], r[:, 2, :], float(N), None, ALU.mult))
            link(dve.reciprocal(r[:, 11, :], r[:, 10, :]))
            link(dve.tensor_scalar(r[:, 10, :], r[:, 11, :], CAP, 1.0, ALU.mult, ALU.min))
            dve.tensor_tensor(r[:, 3, :], r[:, 2, :], r[:, 10, :], ALU.mult).then_inc(r_ps, 1)
            dve.wait_ge(r_ps, 2)
            softmax(3, 5, 3, 2, EXP)
            link(dve.max(r[:, 6, :], r[:, 5, :]))
            dve.max_index(idx[:], r[:, 6, :], r[:, 5, :]).then_inc(idx_ready, 1)
            softmax(6, 1, 5, 3, TOPK)
            dve.wait_ge(r_ps, 3)
            link(dve.tensor_copy(wb[:], bank(3)[:, 8:8 + TOPK]))
            dve.wait_ge(e2_in, 16 * TOPK)
            dve.wait_ge(eb_in, 32 * TOPK)
            for i in range(TOPK):
                last = dve.tensor_scalar(ws2[:, i], raw2[:, i], wb[:, i:i + 1], None, ALU.mult)
            last.then_inc(e_l, 1)
            dve.wait_ge(e_h, 1)
            dve.tensor_tensor(e1[1][:], raw1[:], e1[0][:].bitcast(F32), ALU.subtract).then_inc(e_l, 1)
            link(dve.tensor_scalar(b2w[:], eb2[:, 0], wb[0:TOK, 0:1], None, ALU.mult))
            link(dve.scalar_tensor_tensor(b2w[:], eb2[:, 1], wb[0:TOK, 1:2], b2w[:], ALU.mult, ALU.add))
            dve.wait_ge(e_h, 2)
            dve.tensor_tensor(e2[1][:], ws2[:], e2[0][:].bitcast(F32), ALU.subtract).then_inc(e_l, 1)

        @block.tensor
        def _(pe):
            pe.wait_ge(r_in, 64)
            for c in range(KC):
                last = pe.matmul(bank(3)[0:1, 0:EXP], mean_t[:, c:c + 1], wr[:, c, :], start=(c == 0), stop=(c == KC - 1))
            last.then_inc(r_ps, 1)
            pe.wait_ge(r_dve, 20)
            pe.matmul(bank(3)[:, 8:8 + TOPK], ones[0:1, :], r[0:1, 1, 0:TOPK], start=True, stop=True).then_inc(r_ps, 1)

    xn5 = sb("xn5", [TOK, 2, 2, D])
    u5 = sb("u5", [TOK, 2, 2, D])
    xs = [sb(f"xs{i}", [128, 2, KC, BLK], F32R) for i in range(2)]
    g = sb("g", [128, 4, 2, BLK])
    gs = [sb(f"gs{i}", [128, 8, BLK], F32R) for i in range(2)]
    z5 = sb("z5", [TOK, 2, 2, D])
    bn5 = sb("bn5", [TOK, 2, 6])
    zn = sb("zn", [TOK, 2, D])
    zg = sb("zg", [TOK, 2, D])
    o5 = sb("o5", [TOK, 2, 2, D])
    names = ("xn5_ready", "u5_ready", "xt5_ps", "xh5_ready", "xl5_ready", "f_ps", "g_act", "gh_done", "gl_done",
             "e_ps", "z5_ready", "bn5_ready", "mv5_ready", "zn_ready", "zg_ready", "x1b_ready", "o5_ready")
    (xn5_ready, u5_ready, xt5_ps, xh5_ready, xl5_ready, f_ps, g_act, gh_done, gl_done,
     e_ps, z5_ready, bn5_ready, mv5_ready, zn_ready, zg_ready, x1b_ready, o5_ready) = (sem(n) for n in names)
    out_done = [sem(f"out_done{i}") for i in range(2)]
    psF = [halves(j) for j in range(4)]
    psT, psE = halves(4), tiles(5)
    ROOTS3 = NB + 1
    ov = out.rearrange("(t p) d -> p t d", p=TOK)

    def rows2(t, b, n=2):
        return t[:, bass.ds(2 * b, n), :]

    with nc.Block() as block:
        @block.sync
        def _(sp):
            def step(k, kp):
                sp.wait_ge(o5_ready, k + 1)
                sp.dma_start(ov[:, bass.ds(2 * k, 2), :], o5[:, kp]).then_inc(out_done[kp], 16)
            run_steps(sp, step, 0, 1, 12, 25)
            sp.wait_ge(out_done[0], 16 * 13)
            sp.wait_ge(out_done[1], 16 * 12)

        @block.scalar
        def _(act):
            def step(k, kp):
                if live(k):
                    for j in range(4):
                        act.wait_ge(f_ps, 4 * k + j + 1)
                        if due(4 * k + j - 3):
                            act.wait_ge(gl_done, 4 * k + j - 3)
                        for i in range(2):
                            c = 2 * j + i
                            last = act.activation(g[:, j, i, :], psF[j][:, i, :], ACT.Gelu,
                                                  bias=eb1[:, c // FC, c % FC:c % FC + 1])
                        last.then_inc(g_act, 1)
                        act.wait_ge(g_act, 4 * k + j + 1)
                        if j == 0 and due(k):
                            act.wait_ge(e_ps, k)
                        act.activation(gs[0][:, 2 * j:2 * j + 2, :], g[:, j], ACT.Copy).then_inc(gh_done, 1)
                        if j == 1 and live(k + 1):
                            act.wait_ge(xt5_ps, k + 2)
                            act.activation(xs[0][:, 1 - kp], psT, ACT.Copy).then_inc(xh5_ready, 1)
                elif k == -1:
                    act.wait_ge(xt5_ps, 1)
                    act.activation(xs[0][:, 0], psT, ACT.Copy).then_inc(xh5_ready, 1)
            run_steps(act, step, -1, 1, 11, 25)

        @block.gpsimd
        def _(pool):
            gb = gamma[:].unsqueeze(1).to_broadcast([TOK, 2, D])
            bb = beta[:].unsqueeze(1).to_broadcast([TOK, 2, D])
            b2 = b2w[:].unsqueeze(1).to_broadcast([TOK, 2, D])

            def step(k, kp):
                if live(k - 2):
                    pool.wait_ge(zn_ready, k - 1)
                    if due(k - 2):
                        pool.wait_ge(o5_ready, k - 2)
                    pool.tensor_tensor(zg[:], zn[:], gb, ALU.mult).then_inc(zg_ready, 1)
                if live(k + 1):
                    pool.wait_ge(xn5_ready, k + 2)
                    if due(k):
                        pool.wait_ge(z5_ready, k)
                    pool.tensor_tensor(u5[:, 1 - kp], xn5[:, 1 - kp], b2, ALU.add).then_inc(u5_ready, 1)
                if live(k - 1):
                    newton_root(pool, root_of(1 - kp), ROOTS3 + k - 1)
                    xb = rows2(x, k - 1)
                    pool.tensor_tensor(xb, xb, bb, ALU.add).then_inc(x1b_ready, 1)
            run_steps(pool, step, -1, 2, 10, 27)

        @block.vector
        def _(dve):
            def step(k, kp):
                if live(k + 2):
                    b = k + 2
                    if due(b - 1):
                        dve.wait_ge(xt5_ps, b - 1)
                        dve.wait_ge(u5_ready, b - 1)
                    for t in range(2):
                        n = 2 * b + t
                        last = dve.tensor_scalar(xn5[:, kp, t, :], x[:, bass.ds(n, 1), :].rearrange("p o d -> p (o d)"),
                                                 mv[:, bass.ds(n, 1), 0:1].rearrange("p o d -> p (o d)"),
                                                 rstd[:, bass.ds(n, 1), :].rearrange("p o d -> p (o d)"),
                                                 ALU.subtract, ALU.mult)
                    last.then_inc(xn5_ready, 1)
                if live(k - 1):
                    dve.wait_ge(e_ps, k)
                    dve.wait_ge(u5_ready, k)
                    if due(k - 2):
                        dve.wait_ge(zn_ready, k - 2)
                    dve.tensor_tensor(z5[:, 1 - kp], psE, u5[:, 1 - kp], ALU.add).then_inc(z5_ready, 1)
                    dve.wait_ge(z5_ready, k)
                    if due(k - 1):
                        dve.wait_ge(mv5_ready, k - 1)
                    for t in range(2):
                        last = dve.bn_stats(bn5[:, t, :], z5[:, 1 - kp, t, :])
                    last.then_inc(bn5_ready, 1)
                    dve.wait_ge(bn5_ready, k)
                if live(k):
                    lower_part(k, 0)
                if live(k - 1):
                    for t in range(2):
                        last = dve.bn_aggr(mvs[:, 1 - kp, t, :], bn5[:, t, :])
                    last.then_inc(mv5_ready, 1)
                    dve.wait_ge(mv5_ready, k)
                    seed_root(dve, mvs[:, 1 - kp, :, 1:2], root_of(1 - kp), ROOTS3 + k - 1)
                if live(k):
                    for j in range(1, 4):
                        lower_part(k, j)
                        if j == 1 and live(k + 1):
                            dve.wait_ge(xh5_ready, k + 2)
                            dve.tensor_tensor(xs[1][:, 1 - kp], psT, xs[0][:, 1 - kp].bitcast(F32),
                                              ALU.subtract).then_inc(xl5_ready, 1)
                        if j == 2 and live(k - 1):
                            last_norm(k - 1, 1 - kp)
                        if j == 3 and live(k - 2):
                            last_sum(k - 2, kp)
                elif isinstance(k, int) and k == -1:
                    dve.wait_ge(xh5_ready, 1)
                    dve.tensor_tensor(xs[1][:, 0], psT, xs[0][:, 0].bitcast(F32), ALU.subtract).then_inc(xl5_ready, 1)
                else:
                    if live(k - 1):
                        last_norm(k - 1, 1 - kp)
                    if live(k - 2):
                        last_sum(k - 2, kp)

            def lower_part(k, j):
                dve.wait_ge(gh_done, 4 * k + j + 1)
                dve.tensor_tensor(gs[1][:, 2 * j:2 * j + 2, :], g[:, j], gs[0][:, 2 * j:2 * j + 2, :].bitcast(F32),
                                  ALU.subtract).then_inc(gl_done, 1)

            def last_norm(b, par):
                dve.wait_ge(root_step, ROOT_OPS * (ROOTS3 + b + 1))
                if due(b):
                    dve.wait_ge(zg_ready, b)
                for t in range(2):
                    last = dve.tensor_scalar(zn[:, t, :], z5[:, par, t, :], mvs[:, par, t, 0:1], ny[:, par, t, :],
                                             ALU.subtract, ALU.mult)
                last.then_inc(zn_ready, 1)

            def last_sum(b, par):
                dve.wait_ge(zg_ready, b + 1)
                dve.wait_ge(x1b_ready, b + 1)
                if due(b - 1):
                    dve.wait_ge(out_done[par], 8 * (b - par))
                dve.tensor_tensor(o5[:, par], zg[:], rows2(x, b), ALU.add).then_inc(o5_ready, 1)
            run_steps(dve, step, -2, 2, 10, 27)

        @block.tensor
        def _(pe):
            def transposes(b, par):
                pe.wait_ge(xn5_ready, b + 1)
                if due(b):
                    pe.wait_ge(xl5_ready, b)
                for t in range(2):
                    for c in range(KC):
                        last = pe.transpose(psT[:, c, TOK * t:TOK * t + TOK], xn5[:, par, t, 128 * c:128 * c + 128],
                                            ident[0:TOK, 0:TOK])
                last.then_inc(xt5_ps, 1)

            def step(k, kp):
                if live(k):
                    pe.wait_ge(xl5_ready, k + 1)
                    for j in range(4):
                        if due(k):
                            pe.wait_ge(g_act, 4 * (k - 1) + j + 1)
                        for i in range(2):
                            c = 2 * j + i
                            e, f = c // FC, c % FC
                            for kc in range(KC):
                                last = three_products(pe, psF[j][:, i, :], [w[:, e, kc, 128 * f:128 * f + 128] for w in e1],
                                                      [w[:, kp, kc, :] for w in xs], kc == 0, kc == KC - 1)
                        last.then_inc(f_ps, 1)
                        if j == 0 and live(k + 1):
                            transposes(k + 1, 1 - kp)
                elif k == -1:
                    transposes(0, 0)
                if live(k):
                    if due(k):
                        pe.wait_ge(z5_ready, k)
                    for t in range(2):
                        for c in range(8):
                            if t == 0 and c % 2 == 0:
                                pe.wait_ge(gl_done, 4 * k + c // 2 + 1)
                            last = three_products(pe, psE[:, t, :], [w[:, c, TOK * t:TOK * t + TOK] for w in gs],
                                                  [w[:, c // FC, c % FC, :] for w in e2], c == 0, c == 7)
                    last.then_inc(e_ps, 1)
            run_steps(pe, step, -1, 1, 11, 25)


_NAMES = {
    "edge": "edge_attr_256", "x": "x", "wk": "L0_mix_wk", "wv": "L0_mix_wv", "wq": "L0_mix_wq", "wo": "L0_mix_wo",
    "bk": "L0_mix_bk", "bv": "L0_mix_bv", "bo": "L0_mix_bo", "gnn_b2": "L0_gnn_b2", "wr": "L0_ffn_Wr",
    "gamma": "L0_ffn_gamma", "beta": "L0_ffn_beta", "w1": "L0_ffn_W1", "w2": "L0_ffn_W2", "b2": "L0_ffn_b2",
}


def kernel(**inputs):
    import concourse.bacc as bacc
    from concourse.bass_utils import run_bass_kernel_spmd

    host = {k: np.ascontiguousarray(inputs[v]) for k, v in _NAMES.items()}
    host["bq"] = np.ascontiguousarray(np.asarray(inputs["L0_mix_bq"]).reshape(KC, 128).T)
    host["gnn_b1"] = np.ascontiguousarray(np.asarray(inputs["L0_gnn_b1"]).reshape(KC, 128).T)
    host["gnn_w1t"] = np.ascontiguousarray(np.asarray(inputs["L0_gnn_W1"]).T)
    host["gnn_w2t"] = np.ascontiguousarray(np.asarray(inputs["L0_gnn_W2"]).T)
    host["b1"] = np.ascontiguousarray(np.asarray(inputs["L0_ffn_b1"]).reshape(EXP, FC, 128).transpose(0, 2, 1))
    host["br"] = np.asarray(inputs["L0_ffn_br"]).reshape(1, EXP)
    dst = np.asarray(inputs["dst"])
    sups = np.concatenate([dst[:(NSUP - 1) * SUP], dst[LAST:]]).reshape(NSUP, NG, 128, 2)
    host["dst_t"] = np.ascontiguousarray(sups.transpose(2, 0, 1, 3)).reshape(128, NSUP, NG * 2)
    host["dst_base"] = np.ascontiguousarray(sups[:, :, 0, 0]).reshape(-1)
    host["dst_row"] = np.ascontiguousarray(sups[:, :, 0, 0].T)

    nc = bacc.Bacc("TRN2", target_bir_lowering=False, num_devices=1)
    args = {k: nc.dram_tensor(f"in_{k}", list(v.shape), mybir.dt.from_np(v.dtype), kind="ExternalInput").ap()
            for k, v in host.items()}
    out = nc.dram_tensor("out_x", [N, D], F32, kind="ExternalOutput").ap()
    build(nc, args, out)
    result = run_bass_kernel_spmd(nc, [{f"in_{k}": v for k, v in host.items()}], core_ids=[0])
    return result.results[0]["out_x"]
```

```python
import numpy as np
import concourse.bass as bass
from concourse import mybir
from contextlib import ExitStack

F32 = mybir.dt.float32
F32R = mybir.dt.float32r
I32 = mybir.dt.int32
U32 = mybir.dt.uint32
ALU = mybir.AluOpType
ACT = mybir.ActivationFunctionType
AX = mybir.AxisListType

N = 6250
D = 256
KC = D // 128
NE = 106250
TOK = 125
NT = N // TOK
BLK = 2 * TOK
NB = N // BLK
HD = 32
EXP, FF, TOPK = 8, 512, 2
FC = FF // 128
CAP = float(-(-N * 5 // (4 * EXP)))
EPS = 1e-5
SLOPE = 0.015

GRP, NG = 256, 4
SUP = GRP * NG
NSUP = -(-NE // SUP)
NPAIR = NSUP // 2
LAST = NE - SUP
OVER = (NSUP - 1) * SUP - LAST
GWIN = 32
SHIFT = 60
WIN = 160
PAD = 38
AGW = SHIFT * (NSUP - 1) + WIN
PW = SHIFT + WIN
assert NSUP % 2 == 0 and AGW >= PAD + N and N % BLK == 0

MAGIC = 1597463007.0
ROOT_STEPS = 3
ROOT_OPS = 4 * ROOT_STEPS


def due(n):
    return not isinstance(n, int) or n > 0


def live(b, n=NB):
    return not isinstance(b, int) or 0 <= b < n


def run_steps(eng, step, first, low, doubles, end):
    for k in range(first, low):
        step(k, k % 2)
    with eng.Fori(0, doubles) as i:
        for p in range(2):
            step(2 * i + (low + p), (low + p) % 2)
    for k in range(low + 2 * doubles, end):
        step(k, k % 2)


def three_products(pe, out, a, b, first, last):
    (ah, al), (bh, bl) = a, b
    pe.matmul(out, ah, bh, start=first, stop=False)
    pe.matmul(out, ah, bl, start=False, stop=False)
    return pe.matmul(out, al, bh, start=False, stop=last)


def build(nc, a, out):
    with ExitStack() as ctx:
        _build(nc, a, out, ctx)


def _build(nc, a, out, ctx):
    def sb(name, shape, dt=F32, stack=None):
        return (stack or ctx).enter_context(nc.sbuf_tensor(name, shape, dt))

    def sem(name, stack=None):
        return ctx.enter_context(nc.semaphore(name))

    ps = ctx.enter_context(nc.psum_tensor("ps", [128, 8, 512], F32))

    def bank(i, n=1):
        return ps[:, i:i + n, :].rearrange("p b n -> p (b n)")

    x = sb("x", [TOK, NT, D])
    mv = sb("mv", [TOK, NT, 2])
    rstd = sb("rstd", [TOK, NT, 1])
    half3 = sb("half3", [TOK, 1])
    nv, nh, ny, nw = (sb(n, [TOK, 2, 2, 1]) for n in ("nv", "nh", "ny", "nw"))
    ni = sb("ni", [TOK, 2, 2, 1], I32)
    mvs = sb("mvs", [TOK, 2, 2, 2])
    ident = sb("ident", [128, 128])
    ones = sb("ones", [128, 128])
    flag = sb("flag", [1, 1], I32)
    mean_t = sb("mean_t", [128, KC])

    agg_stack = ctx.enter_context(ExitStack())
    aggT = sb("aggT", [128, KC, AGW], F32, agg_stack)
    dstf = sb("dstf", [128, NSUP, 8], F32, agg_stack)
    edge_stack = ExitStack()
    ring = sb("ring", [128, 4, NG, 2 * D], F32, edge_stack)
    rel = sb("rel", [128, NSUP, 8], F32, edge_stack)
    rowrel = sb("rowrel", [128, NSUP], F32, edge_stack)
    iota = sb("iota", [128, WIN], F32, edge_stack)
    oh1 = sb("oh1", [128, 2, 16, GWIN], F32, edge_stack)
    oh2 = sb("oh2", [128, 2, 2, WIN], F32, edge_stack)
    rows = sb("rows", [128, 2, 2, D], F32, edge_stack)

    x_in = [sem(f"x_in{c}") for c in range(2)]
    edges_in = [sem(f"edges_in{c}") for c in range(4)]
    edges_used = sem("edges_used")
    oh1_ready, oh2_ready = sem("oh1_ready"), sem("oh2_ready")
    rows_ps, rows_ready = sem("rows_ps"), sem("rows_ready")
    win_ps, agg_added = sem("win_ps"), sem("agg_added")
    consts = sem("consts")
    zeroed = sem("zeroed")
    EARLY = 5
    dst_in = sem("dst_in")
    dst_ready = sem("dst_ready")

    psR = bank(0).rearrange("p (h n) -> p h n", h=2)
    psW = bank(1).rearrange("p (h n) -> p h n", h=2)
    e_sup = a["edge"][0:(NSUP - 1) * SUP, :].rearrange("(s g p j) d -> s p g (j d)", g=NG, p=128, j=2)
    e_last = a["edge"][LAST:NE, :].rearrange("(g p j) d -> p g (j d)", g=NG, p=128, j=2)

    def load_pair(sp, u, par):
        for h in range(2):
            if due(2 * u + h - 3):
                sp.wait_ge(edges_used, 2 * u + h - 3)
            dst = ring[:, 2 * par + h]
            if isinstance(u, int) and 2 * u + h == NSUP - 1:
                src = e_last
            elif isinstance(u, int):
                src = e_sup[2 * u + h]
            else:
                src = e_sup[bass.ds(2 * u + h, 1)].rearrange("o p g n -> (o p) g n")
            sp.dma_start(dst, src).then_inc(edges_in[2 * par + h], 16)

    def onehot1(dve, u, par):
        if due(2 * u - 2):
            dve.wait_ge(edges_used, 2 * u - 2)
        dve.tensor_tensor(
            oh1[:, par],
            rel[:, bass.ds(2 * u, 2), :].rearrange("p s c -> p (s c)").unsqueeze(2).to_broadcast([128, 16, GWIN]),
            iota[:, 0:GWIN].unsqueeze(1).to_broadcast([128, 16, GWIN]), ALU.is_equal).then_inc(oh1_ready, 1)

    def onehot2(dve, u, par):
        if due(u - 1):
            dve.wait_ge(win_ps, u - 1)
        dve.tensor_tensor(
            oh2[:, par],
            rowrel[:, bass.ds(2 * u, 2)].unsqueeze(2).to_broadcast([128, 2, WIN]),
            iota[:, 0:WIN].unsqueeze(1).to_broadcast([128, 2, WIN]), ALU.is_equal).then_inc(oh2_ready, 1)

    def sum_groups(pe, u, par, h):
        if h == 0:
            pe.wait_ge(oh1_ready, u + 1)
            if due(u):
                pe.wait_ge(rows_ready, u)
        pe.wait_ge(edges_in[2 * par + h], 8 * u + (16 - 8 * par))
        for j in range(2):
            for g in range(NG):
                last = pe.matmul(psR[32 * g:32 * g + 32, h, :], oh1[:, par, 8 * h + 2 * g + j, :],
                                 ring[:, 2 * par + h, g, j * D:(j + 1) * D],
                                 start=(j == 0), stop=(j == 1), skip_group_check=True)
        last.then_inc(edges_used, 1)

    def rows_out(act, u, par):
        act.wait_ge(edges_used, 2 * u + 2)
        if due(u - 1):
            act.wait_ge(win_ps, u - 1)
        act.activation(rows[:, par], psR[:, :, :], ACT.Copy).then_inc(rows_ready, 1)

    def sum_windows(pe, u, par):
        pe.wait_ge(rows_ready, u + 1)
        pe.wait_ge(oh2_ready, u + 1)
        if due(u):
            pe.wait_ge(agg_added, u)
        for h in range(2):
            for f in range(KC):
                last = pe.matmul(psW[:, f, SHIFT * h:SHIFT * h + WIN], rows[:, par, h, 128 * f:128 * f + 128],
                                 oh2[:, par, h, :], start=(h == 0 and f == 0), stop=(h == 1 and f == 1),
                                 skip_group_check=True)
        last.then_inc(win_ps, 1)

    def add_window(dve, u, par):
        dve.wait_ge(win_ps, u + 1)
        if due(u):
            dve.wait_ge(agg_added, u)
        if isinstance(u, int) and u in (0, EARLY):
            dve.wait_ge(zeroed, 1 if u == 0 else 2)
        w = aggT[:, :, bass.ds(2 * SHIFT * u, PW)]
        dve.tensor_tensor(w, w, psW[:, :, 0:PW], ALU.add).then_inc(agg_added, 1)

    root_seed, root_step = sem("root_seed"), sem("root_step")

    def root_of(par):
        return nv[:, par], nh[:, par], ni[:, par], ny[:, par], nw[:, par]

    def seed_root(dve, var, tiles_of, done):
        v, h, i, y, _ = tiles_of
        dve.tensor_scalar(v, var, EPS, None, ALU.add).then_inc(root_seed, 1)
        dve.tensor_scalar(h, var, EPS, -0.5, ALU.add, ALU.mult).then_inc(root_seed, 1)
        dve.wait_ge(root_seed, 4 * done + 1)
        dve.tensor_scalar(i, v.bitcast(I32), 1, None, ALU.logical_shift_right).then_inc(root_seed, 1)
        dve.wait_ge(root_seed, 4 * done + 3)
        dve.tensor_scalar(y.bitcast(I32), i, -1.0, MAGIC, ALU.mult, ALU.add).then_inc(root_seed, 1)

    def newton_root(pool, tiles_of, done):
        _, h, _, y, w = tiles_of
        pool.wait_ge(root_seed, 4 * done + 4)
        c = ROOT_OPS * done
        for it in range(ROOT_STEPS):
            if it:
                pool.wait_ge(root_step, c)
            pool.tensor_tensor(w, y, y, ALU.mult).then_inc(root_step, 1)
            pool.wait_ge(root_step, c + 1)
            pool.tensor_tensor(w, w, h, ALU.mult).then_inc(root_step, 1)
            pool.wait_ge(root_step, c + 2)
            pool.tensor_tensor(w, w, half3[:].unsqueeze(1).to_broadcast(w.shape), ALU.add).then_inc(root_step, 1)
            pool.wait_ge(root_step, c + 3)
            pool.tensor_tensor(y, y, w, ALU.mult).then_inc(root_step, 1)
            c = c + 4

    def bcast(row, n=TOK):
        return row.partition_broadcast(n)

    attn_stack = ExitStack()
    wq = [sb(f"wq{i}", [128, KC, D], F32R, attn_stack) for i in range(2)]
    wo = [sb(f"wo{i}", [128, KC, D], F32R, attn_stack) for i in range(2)]
    kvm = [sb(f"kvm{i}", [128, KC, 132], F32R, attn_stack) for i in range(2)]
    xn = sb("xn", [TOK, 2, 2, D], F32, attn_stack)
    xt = [sb(f"xt{i}", [128, 2, KC, BLK], F32R, attn_stack) for i in range(2)]
    bq = sb("bq", [128, KC], F32, attn_stack)

    s1 = ExitStack()
    wkv = [sb(f"wkv{i}", [128, KC, 2 * D], F32R, s1) for i in range(2)]
    wraw = sb("wraw", [128, KC, 2, D], F32, s1)
    bkv = sb("bkv", [TOK, 4, 128], F32, s1)
    bn1 = sb("bn1", [TOK, 2, 6], F32, s1)
    kvt = sb("kvt", [TOK, 2, 2, 4, 130], F32, s1)
    kf_ = sb("kf", [128, 2, 2, D], F32, s1)
    ek_ = sb("ek", [128, 2, D], F32, s1)
    rk_ = sb("rk", [128, 2, D], F32, s1)
    kf, ek, rk = kf_[0:TOK], ek_[0:TOK], rk_[0:TOK]
    rowi = sb("rowi", [128, NSUP], I32, s1)

    def scratch(t, dims, shape, dt):
        flat = t[:].rearrange(dims).bitcast(dt)[:, 0:NSUP * shape]
        return flat.rearrange("p (s g) -> p s g", g=shape)

    dsti = scratch(kf_, "p a b n -> p (a b n)", 8, I32)
    basei = scratch(ek_, "p a n -> p (a n)", NG, I32)
    basef = scratch(rk_, "p a n -> p (a n)", NG, F32)
    wrel = scratch(kf_, "p a b n -> p (a b n)", 8, F32)
    woff = sb("woff", [128, NSUP], F32, s1)
    rowoff = sb("rowoff", [128, NSUP], F32, s1)
    mm4 = sb("mm4", [128, 4], F32, s1)
    bad = sb("bad", [128, 4], F32, s1)
    badsum = sb("badsum", [128, 1], F32, s1)
    mask = rk_[:, 0, 0:128]
    kvf = kf_[:].rearrange("p a b n -> p (a b n)")[:, 0:KC * 132].rearrange("p (c n) -> p c n", c=KC)

    w_in = [sem("w_in_kv"), sem("w_in_qo"), sem("b_in")]
    w_split, w_rest = sem("w_split"), sem("w_rest")
    stats, dchk = sem("stats"), sem("dchk")
    mask_ready = sem("mask_ready")
    bn1_ready, mv1_ready = sem("bn1_ready"), sem("mv1_ready")
    flag_ps, flag_set = sem("flag_ps"), sem("flag_set")
    xn_ready, xt_ps, xh_ready, xl_ready = sem("xn_ready"), sem("xt_ps"), sem("xh_ready"), sem("xl_ready")
    kv_ps, kvt_ready, ek_ready, kf_ready = (sem(n) for n in ("kv_ps", "kvt_ready", "ek_ready", "kf_ready"))
    kv_summed, kvm_f, kvm_h, kvm_l = sem("kv_summed"), sem("kvm_f"), sem("kvm_h"), sem("kvm_l")

    psT = bank(2)[:, 0:2 * BLK].rearrange("p (c n) -> p c n", c=KC)
    psKV = [bank(3), bank(4)]
    psA = bank(5)[:, 0:2 * 130].rearrange("p (c n) -> p c n", c=KC)
    xv = a["x"].rearrange("(t p) d -> p t d", p=TOK)
    FIRST_PAIRS = 30

    with nc.Block() as block:
        @block.sync
        def _(sp):
            sp.dma_start(dsti[:], a["dst_t"]).then_inc(dst_in, 16)
            sp.dma_start(basei[:].rearrange("p s g -> p (s g)"), bcast(a["dst_base"], 128)).then_inc(dst_in, 16)
            for g in range(NG):
                sp.dma_start(rowi[32 * g:32 * g + 32, :], bcast(a["dst_row"][g], 32)).then_inc(dst_in, 16)

            def load_x(b, par):
                if due(b - 1):
                    sp.wait_ge(bn1_ready, b - 1)
                sp.dma_start(x[:, bass.ds(2 * b, 2), :], xv[:, bass.ds(2 * b, 2), :]).then_inc(x_in[par], 16)

            load_x(0, 0)
            load_x(1, 1)

            def step(k, kp):
                load_pair(sp, k + 4, kp)
                if live(k + 6):
                    load_x(k + 6, kp)
            run_steps(sp, step, -4, 1, 9, 26)

        @block.scalar
        def _(act):
            act.dma_start(wraw[:, :, 0, :], a["wk"].rearrange("(c p) n -> p c n", p=128)).then_inc(w_in[0], 16)
            act.dma_start(wraw[:, :, 1, :], a["wv"].rearrange("(c p) n -> p c n", p=128)).then_inc(w_in[0], 16)
            act.dma_start(bkv[:, 0:2, :].rearrange("p a n -> p (a n)"), bcast(a["bk"])).then_inc(w_in[2], 16)
            act.dma_start(bkv[:, 2:4, :].rearrange("p a n -> p (a n)"), bcast(a["bv"])).then_inc(w_in[2], 16)
            act.dma_start(bq[:], a["bq"]).then_inc(w_in[2], 16)
            act.wait_ge(w_in[0], 32)
            act.activation(wkv[0][:], wraw[:].rearrange("p c a n -> p c (a n)"), ACT.Copy).then_inc(w_split, 1)

            def step(k, kp):
                if live(k + 1):
                    act.wait_ge(xt_ps, k + 2)
                    if due(2 * k - 2 + 2):
                        act.wait_ge(kv_ps, 2 * k)
                    act.activation(xt[0][:, 1 - kp], psT[:, :, :], ACT.Copy).then_inc(xh_ready, 1)
                if live(k):
                    for t in range(2):
                        act.wait_ge(kvt_ready, 2 * k + t + 1)
                        if due(2 * k + t - 1):
                            act.wait_ge(kf_ready, 2 * k + t - 1)
                        act.activation(ek[:, t, :].rearrange("p (a n) -> p a n", a=2),
                                       kvt[:, kp, t, 0:2, 0:128], ACT.Exp)
                        act.activation(rk[:, t, :].rearrange("p (a n) -> p a n", a=2),
                                       kvt[:, kp, t, 0:2, 0:128], ACT.Relu).then_inc(ek_ready, 1)
                if isinstance(k, int) and k == 0:
                    act.wait_ge(w_rest, 1)
                    act.dma_start(wraw[:, :, 0, :], a["wq"].rearrange("(c p) n -> p c n", p=128)).then_inc(w_in[1], 16)
                    act.dma_start(wraw[:, :, 1, :], a["wo"].rearrange("(c p) n -> p c n", p=128)).then_inc(w_in[1], 16)
                if isinstance(k, int) and k == 23:
                    act.wait_ge(w_in[1], 32)
                    act.activation(wq[0][:], wraw[:, :, 0, :], ACT.Copy).then_inc(w_split, 1)
                    act.activation(wo[0][:], wraw[:, :, 1, :], ACT.Copy).then_inc(w_split, 1)
                rows_out(act, k + 4, kp)
            run_steps(act, step, -4, 3, 9, 26)
            act.wait_ge(kvm_f, 2)
            act.activation(kvm[0][:], kvf, ACT.Copy).then_inc(kvm_h, 1)

        @block.gpsimd
        def _(pool):
            pool.memset(ones[:], 1.0).then_inc(consts, 1)
            pool.memset(ident[:], 0.0).then_inc(consts, 1)
            pool.iota(iota[:], pattern=[[1, WIN]], base=0, channel_multiplier=0,
                      allow_small_or_imprecise_dtypes=True).then_inc(consts, 1)
            pool.wait_ge(consts, 3)
            pool.affine_select(out=ident[:], in_=ident[:], compare_op=ALU.not_equal, fill=1.0, base=0,
                               pattern=[[-1, 128]], channel_multiplier=1).then_inc(consts, 1)
            pool.iota(woff[:], pattern=[[-SHIFT, NSUP]], base=PAD, channel_multiplier=0,
                      allow_small_or_imprecise_dtypes=True).then_inc(dst_ready, 1)
            for g in range(NG):
                pool.wait_ge(dst_ready, g + 1)
                pool.iota(rowoff[32 * g:32 * g + 32, :], pattern=[[-SHIFT, NSUP]], base=PAD, channel_multiplier=1,
                          allow_small_or_imprecise_dtypes=True).then_inc(dst_ready, 1)
            pool.wait_ge(dst_ready, 5)
            early = 2 * SHIFT * (EARLY - 1) + PW
            pool.memset(aggT[:, :, 0:early], 0.0).then_inc(zeroed, 1)
            pool.memset(kvt[:, :, :, :, 128:130], 1.0).then_inc(consts, 1)
            pool.memset(half3[:], 1.5).then_inc(consts, 1)
            pool.memset(aggT[:, :, early:], 0.0).then_inc(zeroed, 1)
            pool.wait_ge(consts, 6)

            def step(k, kp):
                newton_root(pool, root_of(kp), k + 4)
                if isinstance(k, int) and k == -2:
                    pool.wait_ge(dchk, 7)
                    pool.affine_select(out=dstf[:, NSUP - 1, 0:2], in_=dstf[:, NSUP - 1, 0:2], compare_op=ALU.is_ge,
                                       fill=-1.0, base=-OVER, pattern=[[1, 2]], channel_multiplier=2).then_inc(dst_ready, 1)
                    pool.affine_select(out=rel[:, NSUP - 1, 0:2], in_=rel[:, NSUP - 1, 0:2], compare_op=ALU.is_ge,
                                       fill=-1.0, base=-OVER, pattern=[[1, 2]], channel_multiplier=2).then_inc(dst_ready, 1)
            run_steps(pool, step, -4, -1, 11, 21)
            pool.wait_ge(kf_ready, NT)
            pool.memset(mask, 0.0).then_inc(mask_ready, 1)
            for h in range(4):
                pool.wait_ge(mask_ready, h + 1)
                pool.memset(mask[32 * h:32 * h + 32, 32 * h:32 * h + 32], 1.0).then_inc(mask_ready, 1)

        @block.vector
        def _(dve):
            dve.wait_ge(dst_in, 96)
            dve.tensor_copy(dstf[:], dsti[:]).then_inc(dchk, 1)
            dve.tensor_copy(basef[:], basei[:]).then_inc(dchk, 1)
            dve.tensor_copy(rowrel[:], rowi[:]).then_inc(dchk, 1)
            dve.wait_ge(dchk, 3)
            dve.wait_ge(dst_ready, 5)
            d4 = dstf[:].rearrange("p s (g j) -> p (s g) j", j=2)
            dve.tensor_tensor(rel[:].rearrange("p s (g j) -> p (s g) j", j=2), d4,
                              basef[:].rearrange("p s g -> p (s g)").unsqueeze(2).to_broadcast([128, NSUP * NG, 2]),
                              ALU.subtract).then_inc(dchk, 1)
            dve.tensor_tensor(rowrel[:], rowrel[:], rowoff[:], ALU.add).then_inc(dchk, 1)
            dve.tensor_tensor(wrel[:], dstf[:], woff[:].unsqueeze(2).to_broadcast([128, NSUP, 8]), ALU.add)\
               .then_inc(dchk, 1)
            def normalize(b, par):
                dve.wait_ge(root_step, ROOT_OPS * (b + 1))
                dve.tensor_scalar(rstd[:, bass.ds(2 * b, 2), :], ny[:, par], 1.0, None, ALU.mult)
                dve.tensor_scalar(mv[:, bass.ds(2 * b, 2), 0:1], mvs[:, par, :, 0:1], 1.0, None, ALU.mult)
                if due(b - 1):
                    dve.wait_ge(xt_ps, b - 1)
                for t in range(2):
                    last = dve.tensor_scalar(xn[:, par, t, :], x[:, bass.ds(2 * b + t, 1), :].rearrange("p o d -> p (o d)"),
                                             mvs[:, par, t, 0:1], ny[:, par, t, :], ALU.subtract, ALU.mult)
                last.then_inc(xn_ready, 1)

            def step(k, kp):
                if live(k + 4):
                    dve.wait_ge(x_in[kp], 8 * (k + 4) + (16 - 8 * kp))
                onehot2(dve, k + 4, kp)
                if live(k + 4):
                    for t in range(2):
                        last = dve.bn_stats(bn1[:, t, :], x[:, bass.ds(2 * (k + 4) + t, 1), :].rearrange("p o d -> p (o d)"))
                    last.then_inc(bn1_ready, 1)
                if live(k + 2):
                    normalize(k + 2, kp)
                    if live(k + 4):
                        dve.wait_ge(xn_ready, k + 3)
                if live(k + 4):
                    dve.wait_ge(bn1_ready, k + 5)
                if live(k + 1):
                    dve.wait_ge(xh_ready, k + 2)
                    dve.tensor_tensor(xt[1][:, 1 - kp], psT[:, :, :], xt[0][:, 1 - kp].bitcast(F32),
                                      ALU.subtract).then_inc(xl_ready, 1)
                if live(k + 4):
                    for t in range(2):
                        last = dve.bn_aggr(mvs[:, kp, t, :], bn1[:, t, :])
                    last.then_inc(mv1_ready, 1)
                    dve.wait_ge(mv1_ready, k + 5)
                    seed_root(dve, mvs[:, kp, :, 1:2], root_of(kp), k + 4)
                if isinstance(k, int) and k == -3:
                    dve.wait_ge(dchk, 6)
                    dve.tensor_reduce(mm4[:, 0:1], rel[:].rearrange("p s c -> p (s c)"), AX.X, ALU.min)
                    dve.tensor_reduce(mm4[:, 1:2], rel[:].rearrange("p s c -> p (s c)"), AX.X, ALU.max)
                    dve.tensor_reduce(mm4[:, 2:3], wrel[:].rearrange("p s c -> p (s c)"), AX.X, ALU.min)
                    dve.tensor_reduce(mm4[:, 3:4], wrel[:].rearrange("p s c -> p (s c)"), AX.X, ALU.max).then_inc(dchk, 1)
                    dve.wait_ge(dchk, 7)
                    for c in range(4):
                        limit, op = ((0.0, ALU.is_lt), (GWIN - 1.0, ALU.is_gt), (0.0, ALU.is_lt), (WIN - 1.0, ALU.is_gt))[c]
                        last = dve.tensor_scalar(bad[:, c:c + 1], mm4[:, c:c + 1], limit, None, op)
                    last.then_inc(dchk, 1)
                    dve.wait_ge(dchk, 8)
                    dve.tensor_reduce(badsum[:], bad[:], AX.X, ALU.add).then_inc(dchk, 1)
                    dve.wait_ge(w_split, 1)
                    dve.tensor_tensor(wkv[1][:], wraw[:].rearrange("p c a n -> p c (a n)"), wkv[0][:].bitcast(F32),
                                      ALU.subtract).then_inc(w_rest, 1)
                    dve.wait_ge(w_in[2], 48)
                    dve.wait_ge(consts, 5)
                if live(k - 1):
                    for t in range(2):
                        n = 2 * (k - 1) + t + 1
                        dve.wait_ge(ek_ready, n)
                        if due(k - 2):
                            dve.wait_ge(kv_summed, k - 2)
                        dve.scalar_tensor_tensor(kf[:, 1 - kp, t, :], ek[:, t, :], 1.0, rk[:, t, :],
                                                 ALU.min, ALU.add).then_inc(kf_ready, 1)
                if live(k):
                    for t in range(2):
                        dve.wait_ge(kv_ps, 2 * k + t + 1)
                        if due(k - 1):
                            dve.wait_ge(kv_summed, k - 1)
                        dve.tensor_tensor(kvt[:, kp, t, :, 0:128], psKV[t][0:TOK, :].rearrange("p (a n) -> p a n", a=4),
                                          bkv[:], ALU.add).then_inc(kvt_ready, 1)
                if isinstance(k, int) and k == 1:
                    dve.wait_ge(flag_ps, 1)
                    dve.tensor_copy(flag[:], bank(7)[0:1, 0:1]).then_inc(flag_set, 1)
                    dve.wait_ge(dst_ready, 7)
                if isinstance(k, int) and k == 24:
                    dve.wait_ge(w_split, 3)
                    dve.tensor_tensor(wq[1][:], wraw[:, :, 0, :], wq[0][:].bitcast(F32), ALU.subtract).then_inc(w_rest, 1)
                    dve.tensor_tensor(wo[1][:], wraw[:, :, 1, :], wo[0][:].bitcast(F32), ALU.subtract).then_inc(w_rest, 1)
                onehot1(dve, k + 5, 1 - kp)
                if live(k + 3, FIRST_PAIRS - 1):
                    add_window(dve, k + 3, 1 - kp)
            dve.wait_ge(dchk, 5)
            onehot1(dve, 0, 0)
            run_steps(dve, step, -4, 3, 9, 26)
            dve.wait_ge(kv_summed, NB)
            dve.wait_ge(mask_ready, 5)
            dve.tensor_tensor(kvf[:, :, 0:128], psA[:, :, 0:128], mask.unsqueeze(1).to_broadcast([128, KC, 128]),
                              ALU.mult)
            for c in range(KC):
                heads = mask.rearrange("p (h n) -> p h n", n=HD)[:, :, 0]
                last = dve.tensor_scalar(kvf[:, c, 128:132], heads, psA[:, c, 128:129], None, ALU.mult)
            last.then_inc(kvm_f, 2)
            dve.wait_ge(kvm_h, 1)
            dve.tensor_tensor(kvm[1][:], kvf, kvm[0][:].bitcast(F32), ALU.subtract).then_inc(kvm_l, 1)

        @block.tensor
        def _(pe):
            pe.wait_ge(consts, 4)

            def step(k, kp):
                if live(k + 1):
                    pe.wait_ge(xn_ready, k + 2)
                    if due(k + 1):
                        pe.wait_ge(xl_ready, k + 1)
                    for t in range(2):
                        for c in range(KC):
                            last = pe.transpose(psT[:, c, TOK * t:TOK * t + TOK], xn[:, 1 - kp, t, 128 * c:128 * c + 128],
                                                ident[0:TOK, 0:TOK])
                    last.then_inc(xt_ps, 1)
                if isinstance(k, int) and k == 0:
                    pe.wait_ge(dchk, 9)
                    pe.matmul(bank(7)[0:1, 0:1], badsum[:], ones[:, 0:1], start=True, stop=True).then_inc(flag_ps, 1)
                sum_groups(pe, k + 4, kp, 0)
                if not live(k):
                    sum_groups(pe, k + 4, kp, 1)
                if live(k):
                    pe.wait_ge(xl_ready, k + 1)
                    if isinstance(k, int) and k == 0:
                        pe.wait_ge(w_rest, 1)
                    for t in range(2):
                        if t == 1:
                            sum_groups(pe, k + 4, kp, 1)
                        if due(2 * k + t - 1):
                            pe.wait_ge(kvt_ready, 2 * k + t - 1)
                        for c in range(KC):
                            last = three_products(pe, psKV[t][0:TOK, :],
                                                  [w[:, kp, c, TOK * t:TOK * t + TOK] for w in xt],
                                                  [w[:, c, :] for w in wkv], c == 0, c == KC - 1)
                        last.then_inc(kv_ps, 1)
                if live(k + 3, FIRST_PAIRS - 1):
                    sum_windows(pe, k + 3, 1 - kp)
                if live(k - 1):
                    pe.wait_ge(kf_ready, 2 * k)
                    for t in range(2):
                        for c in range(KC):
                            first = isinstance(k, int) and k == 1 and t == 0 and c == 0
                            end = isinstance(k, int) and k == NB and t == 1
                            last = pe.matmul(psA[:, c, :], kf[:, 1 - kp, t, 128 * c:128 * c + 128],
                                             kvt[:, 1 - kp, t, 2 + c, :], start=first, stop=end, skip_group_check=True)
                    last.then_inc(kv_summed, 1)
            run_steps(pe, step, -4, 3, 9, 26)


    s1.close()
    s2 = ExitStack()
    eq = sb("eq", [128, KC, BLK], F32, s2)
    rq = sb("rq", [128, KC, BLK], F32, s2)
    qf = sb("qf", [128, KC, BLK], F32, s2)
    qs = [sb(f"qs{i}", [128, 2, KC, BLK], F32R, s2) for i in range(2)]
    den = sb("den", [TOK, 2, KC, 4], F32, s2)
    rden = sb("rden", [TOK, 2, KC, 4], F32, s2)
    at = sb("at", [TOK, 2, 2, D], F32, s2)
    ats = [sb(f"ats{i}", [128, 2, KC, BLK], F32R, s2) for i in range(2)]
    b_out = sb("b_out", [TOK, D], F32, s2)
    b_out2 = sb("b_out2", [TOK, D], F32, s2)
    xnb = sb("xnb", [TOK, 2, D], F32, s2)

    b2_in, b2_sum = sem("b2_in"), sem("b2_sum")
    xn2_ready, xt2_ps, xh2_ready, xl2_ready = (sem(n) for n in ("xn2_ready", "xt2_ps", "xh2_ready", "xl2_ready"))
    q_ps, eq_ready, rq_ready, q_ready, qh_ready, ql_ready = (
        sem(n) for n in ("q_ps", "eq_ready", "rq_ready", "q_ready", "qh_ready", "ql_ready"))
    att_ps, den_ready, rden_ready, at_ready, at_t, ah_ready, al_ready = (
        sem(n) for n in ("att_ps", "den_ready", "rden_ready", "at_ready", "at_t", "ah_ready", "al_ready"))
    mix_ps, xnb_ready, x_xn, x_mixed = sem("mix_ps"), sem("xnb_ready"), sem("x_xn"), sem("x_mixed")

    def halves(i):
        return bank(i)[:, 0:KC * BLK].rearrange("p (c n) -> p c n", c=KC)

    def tiles(i):
        return bank(i)[0:TOK, :].rearrange("p (t n) -> p t n", t=2)

    psT, psQ, psO, psM = halves(2), halves(3), halves(6), tiles(7)
    psN = ps[0:TOK, 4:6, 0:KC * 132].rearrange("p t (c n) -> p t c n", c=KC)
    U0 = FIRST_PAIRS
    flat = ring[:].rearrange("p s g n -> p s (g n)")
    raw3 = flat[:, 0, 0:2 * KC * D].rearrange("p (w c n) -> p w c n", w=2, c=KC)
    w1 = wq
    w2 = [t[:].rearrange("p b c n -> p (b c n)")[:, 0:KC * D].rearrange("p (c n) -> p c n", c=KC) for t in xt]
    w3_in, w3_h, w3_l = sem("w3_in"), sem("w3_h"), sem("w3_l")

    with nc.Block() as block:
        @block.sync
        def _(sp):
            def step(k, kp):
                if live(k + 2, NPAIR - U0):
                    load_pair(sp, k + (2 + U0), kp)
            run_steps(sp, step, -2, 2, 8, 20)

        @block.scalar
        def _(act):
            act.dma_start(b_out[:], bcast(a["bo"])).then_inc(b2_in, 16)
            act.dma_start(b_out2[:], bcast(a["gnn_b2"])).then_inc(b2_in, 16)

            def step(k, kp):
                if live(k + 1):
                    act.wait_ge(xt2_ps, k + 2)
                    if due(k):
                        act.wait_ge(q_ps, k)
                    act.activation(xt[0][:, 1 - kp], psT, ACT.Copy).then_inc(xh2_ready, 1)
                if live(k):
                    act.wait_ge(q_ps, k + 1)
                    if due(k):
                        act.wait_ge(q_ready, k)
                    for c in range(KC):
                        act.activation(eq[:, c, :], psQ[:, c, :], ACT.Exp, bias=bq[:, c:c + 1])
                        last = act.activation(rq[:, c, :], psQ[:, c, :], ACT.Relu, bias=bq[:, c:c + 1])
                    last.then_inc(eq_ready, 1)
                if live(k - 2):
                    act.wait_ge(at_t, k - 1)
                    if due(k - 3):
                        act.wait_ge(mix_ps, k - 3)
                    act.activation(ats[0][:, kp], psO, ACT.Copy).then_inc(ah_ready, 1)
                if live(k):
                    act.wait_ge(q_ready, k + 1)
                    if due(k - 1):
                        act.wait_ge(att_ps, k - 1)
                    act.activation(qs[0][:, kp], qf[:], ACT.Copy).then_inc(qh_ready, 1)
                if live(k + 2, NPAIR - U0):
                    rows_out(act, k + (2 + U0), kp)
                if isinstance(k, int) and k == 20:
                    act.wait_ge(edges_used, 2 * NPAIR - 2)
                    act.dma_start(raw3[:, 0], a["gnn_w1t"].rearrange("(c p) n -> p c n", p=128)).then_inc(w3_in, 16)
                    act.dma_start(raw3[:, 1], a["gnn_w2t"].rearrange("(c p) n -> p c n", p=128)).then_inc(w3_in, 16)
                if isinstance(k, int) and k == 24:
                    act.wait_ge(w3_in, 32)
                    act.wait_ge(q_ps, NB)
                    act.activation(w1[0][:], raw3[:, 0], ACT.Copy).then_inc(w3_h, 1)
                    act.activation(w2[0], raw3[:, 1], ACT.Copy).then_inc(w3_h, 1)
            run_steps(act, step, -2, 4, 7, 28)

        @block.gpsimd
        def _(pool):
            pool.wait_ge(b2_in, 32)
            pool.tensor_tensor(b_out[:], b_out[:], b_out2[:], ALU.add).then_inc(b2_sum, 1)
            pool.wait_ge(b2_sum, 1)

            def step(k, kp):
                if live(k):
                    pool.wait_ge(xn2_ready, k + 1)
                    if due(k):
                        pool.wait_ge(x_xn, k)
                    pool.tensor_tensor(xnb[:], xn[:, kp], b_out[:].unsqueeze(1).to_broadcast([TOK, 2, D]), ALU.add)\
                        .then_inc(xnb_ready, 1)
                    pool.wait_ge(xnb_ready, k + 1)
                    xb = x[:, bass.ds(2 * k, 2), :]
                    pool.tensor_tensor(xb, xb, xnb[:], ALU.add).then_inc(x_xn, 1)
                    pool.wait_ge(qh_ready, k + 1)
                    pool.tensor_tensor(qs[1][:, kp], qf[:], qs[0][:, kp].bitcast(F32), ALU.subtract)\
                        .then_inc(ql_ready, 1)
            run_steps(pool, step, -2, 4, 7, 28)

        @block.vector
        def _(dve):
            def normalize(b, par):
                if due(b - 1):
                    dve.wait_ge(xt2_ps, b - 1)
                    dve.wait_ge(x_xn, b - 1)
                for t in range(2):
                    last = dve.tensor_scalar(xn[:, par, t, :], x[:, bass.ds(2 * b + t, 1), :].rearrange("p o d -> p (o d)"),
                                             mv[:, bass.ds(2 * b + t, 1), 0:1].rearrange("p o d -> p (o d)"),
                                             rstd[:, bass.ds(2 * b + t, 1), :].rearrange("p o d -> p (o d)"),
                                             ALU.subtract, ALU.mult)
                last.then_inc(xn2_ready, 1)

            def step(k, kp):
                if live(k + 2, NPAIR - U0):
                    onehot2(dve, k + (2 + U0), kp)
                if live(k + 2):
                    normalize(k + 2, kp)
                if live(k + 1):
                    dve.wait_ge(xh2_ready, k + 2)
                    dve.tensor_tensor(xt[1][:, 1 - kp], psT, xt[0][:, 1 - kp].bitcast(F32),
                                      ALU.subtract).then_inc(xl2_ready, 1)
                if live(k - 1):
                    dve.wait_ge(att_ps, k)
                    dve.tensor_scalar(den[:], psN[:, :, :, 128:132], 1e-6, None, ALU.add).then_inc(den_ready, 1)
                    dve.wait_ge(den_ready, k)
                    dve.reciprocal(rden[:], den[:]).then_inc(rden_ready, 1)
                    dve.wait_ge(rden_ready, k)
                    if due(k - 2):
                        dve.wait_ge(at_t, k - 2)
                    for t in range(2):
                        last = dve.tensor_tensor(
                            at[:, 1 - kp, t, :].rearrange("p (c h n) -> p c h n", c=KC, h=4),
                            psN[:, t, :, 0:128].rearrange("p c (h n) -> p c h n", h=4),
                            rden[:, t].unsqueeze(3).to_broadcast([TOK, KC, 4, HD]), ALU.mult)
                    last.then_inc(at_ready, 1)
                if live(k):
                    dve.wait_ge(eq_ready, k + 1)
                    if due(k):
                        dve.wait_ge(ql_ready, k)
                    dve.scalar_tensor_tensor(qf[:], eq[:], 1.0, rq[:], ALU.min, ALU.add).then_inc(q_ready, 1)
                if live(k - 2):
                    dve.wait_ge(ah_ready, k - 1)
                    dve.tensor_tensor(ats[1][:, kp], psO, ats[0][:, kp].bitcast(F32), ALU.subtract).then_inc(al_ready, 1)
                if live(k + 3, NPAIR - U0):
                    onehot1(dve, k + (3 + U0), 1 - kp)
                if live(k + 2, NPAIR - U0 + 1):
                    add_window(dve, k + (1 + U0), 1 - kp)
                if live(k - 3):
                    dve.wait_ge(mix_ps, k - 2)
                    dve.wait_ge(x_xn, k - 2)
                    xb = x[:, bass.ds(2 * (k - 3), 2), :]
                    dve.tensor_tensor(xb, xb, psM, ALU.add).then_inc(x_mixed, 1)
                if isinstance(k, int) and k == 25:
                    for i, w in enumerate((w1, w2)):
                        dve.wait_ge(w3_h, i + 1)
                        dve.tensor_tensor(w[1][:], raw3[:, i], w[0][:].bitcast(F32), ALU.subtract).then_inc(w3_l, 1)
            run_steps(dve, step, -2, 4, 7, 28)

        @block.tensor
        def _(pe):
            def step(k, kp):
                if live(k + 1):
                    pe.wait_ge(xn2_ready, k + 2)
                    if due(k + 1):
                        pe.wait_ge(xl2_ready, k + 1)
                    for t in range(2):
                        for c in range(KC):
                            last = pe.transpose(psT[:, c, TOK * t:TOK * t + TOK], xn[:, 1 - kp, t, 128 * c:128 * c + 128],
                                                ident[0:TOK, 0:TOK])
                    last.then_inc(xt2_ps, 1)
                if live(k):
                    pe.wait_ge(xl2_ready, k + 1)
                    if due(k):
                        pe.wait_ge(eq_ready, k)
                    for o in range(KC):
                        for c in range(KC):
                            last = three_products(pe, psQ[:, o, :], [w[:, c, 128 * o:128 * o + 128] for w in wq],
                                                  [w[:, kp, c, :] for w in xt], c == 0, c == KC - 1)
                    last.then_inc(q_ps, 1)
                if live(k + 2, NPAIR - U0):
                    sum_groups(pe, k + (2 + U0), kp, 0)
                if live(k + 2, NPAIR - U0 + 1):
                    sum_windows(pe, k + (1 + U0), 1 - kp)
                if live(k - 1):
                    pe.wait_ge(ql_ready, k)
                    if due(k - 1):
                        pe.wait_ge(at_ready, k - 1)
                    if isinstance(k, int) and k == 1:
                        pe.wait_ge(kvm_l, 1)
                    for t in range(2):
                        for c in range(KC):
                            last = three_products(pe, psN[:, t, c, :],
                                                  [w[:, 1 - kp, c, TOK * t:TOK * t + TOK] for w in qs],
                                                  [w[:, c, :] for w in kvm], True, True)
                    last.then_inc(att_ps, 1)
                if live(k - 2):
                    pe.wait_ge(at_ready, k - 1)
                    if due(k - 2):
                        pe.wait_ge(al_ready, k - 2)
                    for t in range(2):
                        for c in range(KC):
                            last = pe.transpose(psO[:, c, TOK * t:TOK * t + TOK], at[:, kp, t, 128 * c:128 * c + 128],
                                                ident[0:TOK, 0:TOK])
                    last.then_inc(at_t, 1)
                if live(k + 2, NPAIR - U0):
                    sum_groups(pe, k + (2 + U0), kp, 1)
                if live(k - 3):
                    pe.wait_ge(al_ready, k - 2)
                    if due(k - 3):
                        pe.wait_ge(x_mixed, k - 3)
                    for t in range(2):
                        for c in range(KC):
                            last = three_products(pe, psM[:, t, :], [w[:, 1 - kp, c, TOK * t:TOK * t + TOK] for w in ats],
                                                  [w[:, c, :] for w in wo], c == 0, c == KC - 1)
                    last.then_inc(mix_ps, 1)
            run_steps(pe, step, -2, 4, 7, 28)

    s2.close()
    sg = ExitStack()
    g_edges = ring[:, 0]
    g_oh = sb("g_oh", [128, 8, BLK], F32, sg)
    g_node = sb("g_node", [128, BLK], F32, sg)
    g_in, g_ready, g_ps, g_added, g_nodes, g_zero = (
        sem(n) for n in ("g_in", "g_ready", "g_ps", "g_added", "g_nodes", "g_zero"))
    psG = halves(0)

    with nc.Block() as block:
        @block.sync
        def _(sp):
            def load(n, src):
                sp.wait_ge(g_added, n + 1)
                sp.dma_start(g_edges, src).then_inc(g_in, 16)

            general = sp.value_load(flag[0:1, 0:1], min_val=0, max_val=512)
            with sp.If(general != 0):
                with sp.Fori(0, NB) as nb:
                    with sp.Fori(0, NSUP - 1) as s:
                        load(nb * NSUP + s, e_sup[bass.ds(s, 1)].rearrange("o p g n -> (o p) g n"))
                    load(nb * NSUP + (NSUP - 1), e_last)
            sp.end_ifs()

        @block.gpsimd
        def _(pool):
            pool.iota(g_node[:], pattern=[[1, BLK]], base=-BLK, channel_multiplier=0,
                      allow_small_or_imprecise_dtypes=True).then_inc(g_zero, 1)

        @block.vector
        def _(dve):
            def take(n, s, nb):
                dve.wait_ge(g_nodes, nb + 1)
                dve.tensor_tensor(g_oh[:], dstf[:, bass.ds(s, 1), :].rearrange("p s c -> p (s c)").unsqueeze(2).to_broadcast([128, 8, BLK]),
                                  g_node[:].unsqueeze(1).to_broadcast([128, 8, BLK]), ALU.is_equal).then_inc(g_ready, 1)
                dve.wait_ge(g_ps, n + 1)
                w = aggT[:, :, bass.ds(BLK * nb + PAD, BLK)]
                dve.tensor_tensor(w, w, psG, ALU.add).then_inc(g_added, 1)
                dve.wait_ge(g_added, n + 2)

            dve.wait_ge(g_zero, 1)
            general = dve.value_load(flag[0:1, 0:1], min_val=0, max_val=512)
            with dve.If(general != 0):
                dve.memset(aggT[:], 0.0).then_inc(g_added, 1)
                dve.wait_ge(g_added, 1)
                with dve.Fori(0, NB) as nb:
                    dve.tensor_scalar(g_node[:], g_node[:], float(BLK), None, ALU.add).then_inc(g_nodes, 1)
                    with dve.Fori(0, NSUP - 1) as s:
                        take(nb * NSUP + s, s, nb)
                    take(nb * NSUP + (NSUP - 1), NSUP - 1, nb)
            dve.end_ifs()

        @block.tensor
        def _(pe):
            def sums(n):
                pe.wait_ge(g_in, 16 * n + 16)
                pe.wait_ge(g_ready, n + 1)
                for f in range(KC):
                    for c in range(8):
                        o = (c % 2) * D + 128 * f
                        last = pe.matmul(psG[:, f, :], g_edges[:, c // 2, o:o + 128], g_oh[:, c, :],
                                         start=(c == 0), stop=(c == 7))
                last.then_inc(g_ps, 1)

            general = pe.value_load(flag[0:1, 0:1], min_val=0, max_val=512)
            with pe.If(general != 0):
                with pe.Fori(0, NB * NSUP) as n:
                    sums(n)
            pe.end_ifs()
    sg.close()

    s3 = ExitStack()
    b1 = sb("b1", [128, KC], F32, s3)
    ag = [sb(f"ag{i}", [128, 2, KC, BLK], F32R, s3) for i in range(2)]
    z = sb("z", [128, 2, KC, BLK], F32, s3)
    hf = sb("hf", [128, KC, BLK], F32, s3)
    hs = [sb(f"hs{i}", [128, 2, KC, BLK], F32R, s3) for i in range(2)]
    bn3 = sb("bn3", [TOK, 2, 6], F32, s3)

    b1_in, sums_in = sem("b1_in"), sem("sums_in")
    gh_ready, gl_ready, h_ps, z_ready, hf_ready, hh_ready, hl_ready, y_ps = (
        sem(n) for n in ("gh_ready", "gl_ready", "h_ps", "z_ready", "hf_ready", "hh_ready", "hl_ready", "y_ps"))
    x1_ready, bn3_ready, mv3_ready, kept3 = (sem(n) for n in ("x1_ready", "bn3_ready", "mv3_ready", "kept3"))
    psH, psY = [halves(0), halves(1)], [tiles(2), tiles(3)]

    with nc.Block() as block:
        @block.sync
        def _(sp):
            sp.dma_start(b1[:], a["gnn_b1"]).then_inc(b1_in, 16)

        @block.scalar
        def _(act):
            act.wait_ge(b1_in, 16)

            def step(k, kp):
                if live(k + 1):
                    if due(k):
                        act.wait_ge(h_ps, k)
                    act.activation(ag[0][:, 1 - kp], aggT[:, :, bass.ds(BLK * (k + 1) + PAD, BLK)], ACT.Copy)\
                       .then_inc(gh_ready, 1)
                if live(k - 1):
                    act.wait_ge(hf_ready, k)
                    if due(k - 2):
                        act.wait_ge(y_ps, k - 2)
                    act.activation(hs[0][:, 1 - kp], hf[:], ACT.Copy).then_inc(hh_ready, 1)
                if live(k):
                    act.wait_ge(h_ps, k + 1)
                    if due(k - 1):
                        act.wait_ge(hf_ready, k - 1)
                    for c in range(KC):
                        last = act.activation(z[:, kp, c, :], psH[kp][:, c, :], ACT.Identity, bias=b1[:, c:c + 1])
                    last.then_inc(z_ready, 1)
            run_steps(act, step, -1, 3, 10, 26)

        @block.gpsimd
        def _(pool):
            def step(k, kp):
                if live(k + 1):
                    pool.wait_ge(gh_ready, k + 2)
                    pool.tensor_tensor(ag[1][:, 1 - kp], aggT[:, :, bass.ds(BLK * (k + 1) + PAD, BLK)],
                                       ag[0][:, 1 - kp].bitcast(F32), ALU.subtract).then_inc(gl_ready, 1)
            run_steps(pool, step, -1, 0, 12, 24)

        @block.vector
        def _(dve):
            def step(k, kp):
                if live(k - 3):
                    dve.wait_ge(y_ps, k - 2)
                    if live(k - 4) and due(k - 3):
                        dve.wait_ge(x1_ready, k - 3)
                    xb = x[:, bass.ds(2 * (k - 3), 2), :]
                    dve.tensor_tensor(xb, xb, psY[1 - kp], ALU.add).then_inc(x1_ready, 1)
                if live(k - 5):
                    dve.wait_ge(mv3_ready, k - 4)
                    dve.tensor_scalar(mv[:, bass.ds(2 * (k - 5), 2), :], mvs[:, 1 - kp], 1.0, None, ALU.mult)\
                       .then_inc(kept3, 1)
                if live(k - 1):
                    dve.wait_ge(z_ready, k)
                    if due(k - 1):
                        dve.wait_ge(hl_ready, k - 1)
                    zb = z[:, 1 - kp]
                    dve.scalar_tensor_tensor(hf[:], zb, SLOPE, zb, ALU.mult, ALU.max).then_inc(hf_ready, 1)
                if live(k - 4):
                    if not live(k - 3):
                        dve.wait_ge(x1_ready, k - 3)
                    for t in range(2):
                        last = dve.bn_stats(bn3[:, t, :], x[:, bass.ds(2 * (k - 4) + t, 1), :].rearrange("p o d -> p (o d)"))
                    last.then_inc(bn3_ready, 1)
                    dve.wait_ge(bn3_ready, k - 3)
                if live(k - 1):
                    dve.wait_ge(hh_ready, k)
                    dve.tensor_tensor(hs[1][:, 1 - kp], hf[:], hs[0][:, 1 - kp].bitcast(F32),
                                      ALU.subtract).then_inc(hl_ready, 1)
                if live(k - 4):
                    for t in range(2):
                        last = dve.bn_aggr(mvs[:, kp, t, :], bn3[:, t, :])
                    last.then_inc(mv3_ready, 1)
            run_steps(dve, step, 1, 6, 9, 30)

        @block.tensor
        def _(pe):
            def step(k, kp):
                if live(k):
                    pe.wait_ge(gl_ready, k + 1)
                    if due(k - 1):
                        pe.wait_ge(z_ready, k - 1)
                    for o in range(KC):
                        for c in range(KC):
                            last = three_products(pe, psH[kp][:, o, :], [w[:, c, 128 * o:128 * o + 128] for w in w1],
                                                  [w[:, kp, c, :] for w in ag], c == 0, c == KC - 1)
                    last.then_inc(h_ps, 1)
                if live(k - 2):
                    pe.wait_ge(hl_ready, k - 1)
                    if due(k - 3):
                        pe.wait_ge(x1_ready, k - 3)
                    for t in range(2):
                        for c in range(KC):
                            last = three_products(pe, psY[kp][:, t, :], [w[:, kp, c, TOK * t:TOK * t + TOK] for w in hs],
                                                  [w[:, c, :] for w in w2], c == 0, c == KC - 1)
                    last.then_inc(y_ps, 1)
            run_steps(pe, step, 0, 5, 10, 27)
    s3.close()
    attn_stack.close()
    edge_stack.close()
    agg_stack.close()

    vroot, hroot, wroot, rm = (sb(n, [TOK, NT, 1]) for n in ("vroot", "hroot", "wroot", "rm"))
    iroot = sb("iroot", [TOK, NT, 1], I32)
    rm_sum = sb("rm_sum", [TOK, 2])
    xr = sb("xr", [128, D])
    gelu_one = sb("gelu_one", [1, 2])
    raw1 = sb("raw1", [128, TOPK, KC, FF])
    raw2 = sb("raw2", [128, TOPK, FC, D])
    ws2 = sb("ws2", [128, TOPK, FC, D])
    e1 = [sb(f"e1{i}", [128, TOPK, KC, FF], F32R) for i in range(2)]
    e2 = [sb(f"e2{i}", [128, TOPK, FC, D], F32R) for i in range(2)]
    eb1 = sb("eb1", [128, TOPK, FC])
    eb2 = sb("eb2", [TOK, TOPK, D])
    b2w = sb("b2w", [TOK, D])
    gamma, beta = sb("gamma", [TOK, D]), sb("beta", [TOK, D])
    wr = sb("wr", [128, KC, EXP])
    br = sb("br", [1, EXP])
    r = sb("r", [1, 12, EXP])
    idx = sb("idx", [1, EXP], U32)
    wb = sb("wb", [128, TOPK])
    r_in, r_dve, r_act, r_ps = sem("r_in"), sem("r_dve"), sem("r_act"), sem("r_ps")
    idx_ready = sem("idx_ready")
    e1_in = [sem(f"e1_in{i}") for i in range(TOPK)]
    e2_in, eb_in = sem("e2_in"), sem("eb_in")
    e1_h, e1_l, e2_w, e2_h, e2_l, b2_ready = (sem(n) for n in ("e1_h", "e1_l", "e2_w", "e2_h", "e2_l", "b2_ready"))
    chain, xr_ps, xr_ready, rm_ready, mean_ps, mean_out = (
        sem(n) for n in ("chain", "xr_ps", "xr_ready", "rm_ready", "mean_ps", "mean_out"))

    xn5 = sb("xn5", [TOK, 2, 2, D])
    u5 = sb("u5", [TOK, 2, 2, D])
    xs = [sb(f"xs{i}", [128, 2, KC, BLK], F32R) for i in range(2)]
    g = sb("g", [128, 4, 2, BLK])
    gs = [sb(f"gs{i}", [128, 2, 8, BLK], F32R) for i in range(2)]
    z5 = sb("z5", [TOK, 2, 2, D])
    bn5 = sb("bn5", [TOK, 2, 6])
    zn = sb("zn", [TOK, 2, D])
    zg = sb("zg", [TOK, 2, D])
    o5 = sb("o5", [TOK, 2, 2, D])
    names = ("xn5_ready", "u5_ready", "xt5_ps", "xh5_ready", "xl5_ready", "f_ps", "g_act", "gh_done", "gl_done",
             "e_ps", "z5_ready", "bn5_ready", "mv5_ready", "zn_ready", "zg_ready", "x1b_ready", "o5_ready")
    (xn5_ready, u5_ready, xt5_ps, xh5_ready, xl5_ready, f_ps, g_act, gh_done, gl_done,
     e_ps, z5_ready, bn5_ready, mv5_ready, zn_ready, zg_ready, x1b_ready, o5_ready) = (sem(n) for n in names)
    out_done = [sem(f"out_done{i}") for i in range(2)]
    psF = [halves(j) for j in range(4)]
    psT, psE = halves(4), tiles(5)
    psX, psMean, psRt = bank(6)[:, 0:D], bank(7)[:, 0:KC], bank(7)[:, KC:KC + 16]
    SAME = 32
    ROOTS3 = NB
    ov = out.rearrange("(t p) d -> p t d", p=TOK)

    def rows2(t, b, n=2):
        return t[:, bass.ds(2 * b, n), :]

    with nc.Block() as block:
        @block.sync
        def _(sp):
            sp.dma_start(wr[:], a["wr"].rearrange("(c p) n -> p c n", p=128)).then_inc(r_in, 16)
            sp.dma_start(br[:], a["br"]).then_inc(r_in, 16)
            sp.dma_start(gamma[:], bcast(a["gamma"])).then_inc(r_in, 16)
            sp.dma_start(beta[:], bcast(a["beta"])).then_inc(r_in, 16)
            sp.wait_ge(idx_ready, 1)
            es = [sp.value_load(idx[0:1, i:i + 1], min_val=0, max_val=EXP - 1) for i in range(TOPK)]
            for i, e in enumerate(es):
                sp.dma_start(raw1[:, i], a["w1"].rearrange("e (c p) n -> e p c n", p=128)[bass.ds(e, 1)]
                             .rearrange("o p c n -> (o p) c n")).then_inc(e1_in[i], 16)
                sp.dma_start(eb1[:, i], a["b1"][bass.ds(e, 1)].rearrange("o p c -> (o p) c")).then_inc(e1_in[i], 16)
            for i, e in enumerate(es):
                sp.dma_start(raw2[:, i], a["w2"].rearrange("e (c p) n -> e p c n", p=128)[bass.ds(e, 1)]
                             .rearrange("o p c n -> (o p) c n")).then_inc(e2_in, 16)
                sp.dma_start(eb2[:, i], bcast(a["b2"][bass.ds(e, 1)].rearrange("o n -> (o n)"))).then_inc(eb_in, 16)

            def step(k, kp):
                sp.wait_ge(o5_ready, k + 1)
                sp.dma_start(ov[:, bass.ds(2 * k, 2), :], o5[:, kp]).then_inc(out_done[kp], 16)
            run_steps(sp, step, 0, 1, 12, 25)
            sp.wait_ge(out_done[0], 16 * 13)
            sp.wait_ge(out_done[1], 16 * 12)

        @block.scalar
        def _(act):
            act.wait_ge(xr_ps, 1)
            act.activation(xr[:], psX, ACT.Copy).then_inc(xr_ready, 1)
            act.wait_ge(r_dve, 3)
            act.activation(r[:, 1, :], r[:, 0, :], ACT.Exp, bias=r[:, 8, 0:1]).then_inc(r_act, 1)
            act.wait_ge(r_dve, 11)
            act.activation(r[:, 4, :], r[:, 3, :], ACT.Exp, bias=r[:, 8, 3:4]).then_inc(r_act, 1)
            act.wait_ge(r_dve, 17)
            act.activation(r[:, 7, 0:TOPK], r[:, 6, 0:TOPK], ACT.Exp, bias=r[:, 8, 6:7]).then_inc(r_act, 1)
            act.activation(gelu_one[:, 0:1], half3[0:1, :], ACT.Gelu)

            def step(k, kp):
                if live(k):
                    for j in range(4):
                        act.wait_ge(f_ps, 4 * k + j + 1)
                        if due(4 * k + j - 3):
                            act.wait_ge(gl_done, 4 * k + j - 3)
                        for i in range(2):
                            c = 2 * j + i
                            last = act.activation(g[:, j, i, :], psF[j][:, i, :], ACT.Gelu,
                                                  bias=eb1[:, c // FC, c % FC:c % FC + 1])
                        last.then_inc(g_act, 1)
                        act.wait_ge(g_act, 4 * k + j + 1)
                        if j == 0 and due(k - 1):
                            act.wait_ge(e_ps, k - 1)
                        act.activation(gs[0][:, kp, 2 * j:2 * j + 2, :], g[:, j], ACT.Copy).then_inc(gh_done, 1)
                        if j == 2 and live(k + 1):
                            act.wait_ge(xt5_ps, k + 2)
                            act.activation(xs[0][:, 1 - kp], psT, ACT.Copy).then_inc(xh5_ready, 1)
                elif k == -1:
                    act.wait_ge(xt5_ps, 1)
                    act.activation(xs[0][:, 0], psT, ACT.Copy).then_inc(xh5_ready, 1)
            step(-1, 1)
            for i in range(TOPK):
                act.wait_ge(e1_in[i], 32)
                act.activation(e1[0][:, i], raw1[:, i], ACT.Copy).then_inc(e1_h, 1)
            step(0, 0)
            act.wait_ge(e2_w, 1)
            act.activation(e2[0][:], ws2[:], ACT.Copy).then_inc(e2_h, 1)
            run_steps(act, step, 1, 2, 11, 25)

        @block.gpsimd
        def _(pool):
            gb = gamma[:].unsqueeze(1).to_broadcast([TOK, 2, D])
            bb = beta[:].unsqueeze(1).to_broadcast([TOK, 2, D])
            b2 = b2w[:].unsqueeze(1).to_broadcast([TOK, 2, D])
            pool.wait_ge(b2_ready, 2)

            def step(k, kp):
                if live(k - 3):
                    pool.wait_ge(zn_ready, k - 2)
                    if due(k - 3):
                        pool.wait_ge(o5_ready, k - 3)
                    pool.tensor_tensor(zg[:], zn[:], gb, ALU.mult).then_inc(zg_ready, 1)
                if live(k - 2):
                    newton_root(pool, root_of(kp), ROOTS3 + k - 2)
                    xb = rows2(x, k - 2)
                    pool.tensor_tensor(xb, xb, bb, ALU.add).then_inc(x1b_ready, 1)
                if live(k):
                    pool.wait_ge(xn5_ready, k + 1)
                    if due(k - 1):
                        pool.wait_ge(z5_ready, k - 1)
                    pool.tensor_tensor(u5[:, kp], xn5[:, kp], b2, ALU.add).then_inc(u5_ready, 1)
            run_steps(pool, step, 0, 5, 9, 28)

        @block.vector
        def _(dve):
            c = [0]

            def chained(ins):
                c[0] += 1
                ins.then_inc(chain, 1)
                dve.wait_ge(chain, c[0])

            chained(dve.tensor_scalar(vroot[:], mv[:, :, 1:2], EPS, None, ALU.add))
            chained(dve.tensor_scalar(iroot[:], vroot[:].bitcast(I32), 1, None, ALU.logical_shift_right))
            chained(dve.tensor_scalar(rstd[:].bitcast(I32), iroot[:], -1.0, MAGIC, ALU.mult, ALU.add))
            chained(dve.tensor_scalar(hroot[:], vroot[:], -0.5, None, ALU.mult))
            for _ in range(ROOT_STEPS):
                chained(dve.tensor_tensor(wroot[:], rstd[:], rstd[:], ALU.mult))
                chained(dve.tensor_tensor(wroot[:], wroot[:], hroot[:], ALU.mult))
                chained(dve.scalar_tensor_tensor(rstd[:], wroot[:], 1.5, rstd[:], ALU.add, ALU.mult))
            chained(dve.tensor_tensor(rm[:], rstd[:], mv[:, :, 0:1], ALU.mult))
            chained(dve.tensor_reduce(rm_sum[:, 0:1], rm[:].rearrange("p t o -> p (t o)"), AX.X, ALU.add))
            dve.tensor_scalar(rm_sum[:, 1:2], rm_sum[:, 0:1], -float(SAME), None, ALU.mult).then_inc(rm_ready, 1)
            dve.wait_ge(mean_ps, 1)
            dve.tensor_scalar(mean_t[:], psMean, 1.0 / (SAME * N), None, ALU.mult).then_inc(mean_out, 1)

            n = [0]

            def link(ins):
                n[0] += 1
                ins.then_inc(r_dve, 1)
                dve.wait_ge(r_dve, n[0])

            def softmax(src, dst, col, act_done, width):
                link(dve.tensor_reduce(r[:, 8, col + 1:col + 2], r[:, src, 0:width], AX.X, ALU.max))
                link(dve.tensor_scalar(r[:, 8, col:col + 1], r[:, 8, col + 1:col + 2], -1.0, None, ALU.mult))
                dve.wait_ge(r_act, act_done)
                link(dve.tensor_reduce(r[:, 8, col + 2:col + 3], r[:, src + 1, 0:width], AX.X, ALU.add))
                link(dve.reciprocal(r[:, 9, col:col + 1], r[:, 8, col + 2:col + 3]))
                link(dve.tensor_scalar(r[:, dst, 0:width], r[:, src + 1, 0:width], r[:, 9, col:col + 1], None, ALU.mult))

            dve.wait_ge(r_in, 64)
            dve.wait_ge(r_ps, 1)
            link(dve.tensor_tensor(r[:, 0, :], psRt[0:1, 0:EXP], br[:], ALU.add))
            softmax(0, 2, 0, 1, EXP)
            link(dve.tensor_scalar(r[:, 10, :], r[:, 2, :], float(N), None, ALU.mult))
            link(dve.reciprocal(r[:, 11, :], r[:, 10, :]))
            link(dve.tensor_scalar(r[:, 10, :], r[:, 11, :], CAP, 1.0, ALU.mult, ALU.min))
            dve.tensor_tensor(r[:, 3, :], r[:, 2, :], r[:, 10, :], ALU.mult).then_inc(r_ps, 1)
            dve.wait_ge(r_ps, 2)
            softmax(3, 5, 3, 2, EXP)
            link(dve.max(r[:, 6, :], r[:, 5, :]))
            dve.max_index(idx[:], r[:, 6, :], r[:, 5, :]).then_inc(idx_ready, 1)
            softmax(6, 1, 5, 3, TOPK)
            dve.wait_ge(r_ps, 3)
            link(dve.tensor_copy(wb[:], psRt[:, 8:8 + TOPK]))

            def normalize(b, par):
                if due(b - 1):
                    dve.wait_ge(xt5_ps, b - 1)
                    dve.wait_ge(u5_ready, b - 1)
                for t in range(2):
                    n = 2 * b + t
                    last = dve.tensor_scalar(xn5[:, par, t, :], x[:, bass.ds(n, 1), :].rearrange("p o d -> p (o d)"),
                                             mv[:, bass.ds(n, 1), 0:1].rearrange("p o d -> p (o d)"),
                                             rstd[:, bass.ds(n, 1), :].rearrange("p o d -> p (o d)"),
                                             ALU.subtract, ALU.mult)
                last.then_inc(xn5_ready, 1)

            def lower_x(b, par):
                dve.wait_ge(xh5_ready, b + 1)
                dve.tensor_tensor(xs[1][:, par], psT, xs[0][:, par].bitcast(F32), ALU.subtract).then_inc(xl5_ready, 1)

            def step(k, kp):
                if live(k - 2):
                    dve.wait_ge(e_ps, k - 1)
                    dve.wait_ge(u5_ready, k - 1)
                    if due(k - 3):
                        dve.wait_ge(zn_ready, k - 3)
                    dve.tensor_tensor(z5[:, kp], psE, u5[:, kp], ALU.add).then_inc(z5_ready, 1)
                    dve.wait_ge(z5_ready, k - 1)
                    if due(k - 2):
                        dve.wait_ge(mv5_ready, k - 2)
                    for t in range(2):
                        last = dve.bn_stats(bn5[:, t, :], z5[:, kp, t, :])
                    last.then_inc(bn5_ready, 1)
                    dve.wait_ge(bn5_ready, k - 1)
                if live(k + 1):
                    normalize(k + 1, 1 - kp)
                if live(k - 2):
                    if not live(k + 1):
                        dve.wait_ge(bn5_ready, k - 1)
                    for t in range(2):
                        last = dve.bn_aggr(mvs[:, kp, t, :], bn5[:, t, :])
                    last.then_inc(mv5_ready, 1)
                    dve.wait_ge(mv5_ready, k - 1)
                    seed_root(dve, mvs[:, kp, :, 1:2], root_of(kp), ROOTS3 + k - 2)
                for j in range(4):
                    if live(k):
                        lower_part(k, kp, j)
                    if j == 2 and live(k + 1):
                        lower_x(k + 1, 1 - kp)
                    if j == 2 and live(k - 2):
                        last_norm(k - 2, kp)
                    if j == 3 and live(k - 3):
                        last_sum(k - 3, 1 - kp)

            def lower_part(k, par, j):
                dve.wait_ge(gh_done, 4 * k + j + 1)
                dve.tensor_tensor(gs[1][:, par, 2 * j:2 * j + 2, :], g[:, j], gs[0][:, par, 2 * j:2 * j + 2, :].bitcast(F32),
                                  ALU.subtract).then_inc(gl_done, 1)

            def last_norm(b, par):
                dve.wait_ge(root_step, ROOT_OPS * (ROOTS3 + b + 1))
                if due(b):
                    dve.wait_ge(zg_ready, b)
                for t in range(2):
                    last = dve.tensor_scalar(zn[:, t, :], z5[:, par, t, :], mvs[:, par, t, 0:1], ny[:, par, t, :],
                                             ALU.subtract, ALU.mult)
                last.then_inc(zn_ready, 1)

            def last_sum(b, par):
                dve.wait_ge(zg_ready, b + 1)
                dve.wait_ge(x1b_ready, b + 1)
                if due(b - 1):
                    dve.wait_ge(out_done[par], 8 * (b - par))
                dve.tensor_tensor(o5[:, par], zg[:], rows2(x, b), ALU.add).then_inc(o5_ready, 1)
            step(-1, 1)
            for i in range(TOPK):
                dve.wait_ge(e1_h, i + 1)
                dve.tensor_tensor(e1[1][:, i], raw1[:, i], e1[0][:, i].bitcast(F32), ALU.subtract).then_inc(e1_l, 1)
            dve.wait_ge(e2_in, 16 * TOPK)
            for i in range(TOPK):
                last = dve.tensor_scalar(ws2[:, i], raw2[:, i], wb[:, i:i + 1], None, ALU.mult)
            last.then_inc(e2_w, 1)
            dve.wait_ge(eb_in, 16 * TOPK)
            dve.tensor_scalar(b2w[:], eb2[:, 0], wb[0:TOK, 0:1], None, ALU.mult).then_inc(b2_ready, 1)
            dve.wait_ge(b2_ready, 1)
            dve.scalar_tensor_tensor(b2w[:], eb2[:, 1], wb[0:TOK, 1:2], b2w[:], ALU.mult, ALU.add).then_inc(b2_ready, 1)
            step(0, 0)
            dve.wait_ge(e2_h, 1)
            dve.tensor_tensor(e2[1][:], ws2[:], e2[0][:].bitcast(F32), ALU.subtract).then_inc(e2_l, 1)
            run_steps(dve, step, 1, 5, 9, 28)

        @block.tensor
        def _(pe):
            pe.wait_ge(chain, 4 + 3 * ROOT_STEPS)
            for t in range(NT):
                q = t % 4
                last = pe.matmul(psX[32 * q:32 * q + 32, :], rstd[:, t, :].to_broadcast([TOK, 32]), x[:, t, :],
                                 start=(t < 4), stop=(t >= NT - 4), skip_group_check=True)
            last.then_inc(xr_ps, 1)
            pe.wait_ge(xr_ready, 1)
            pe.wait_ge(rm_ready, 1)
            for c in range(KC):
                pe.matmul(psMean[:, c:c + 1], xr[:, 128 * c:128 * c + 128], ones[:, 0:1], start=(c == 0), stop=False,
                          skip_group_check=True)
                last = pe.matmul(psMean[:, c:c + 1], ones[0:TOK, :], rm_sum[:, 1:2], start=False, stop=(c == KC - 1),
                                 skip_group_check=True)
            last.then_inc(mean_ps, 1)
            pe.wait_ge(r_in, 64)
            pe.wait_ge(mean_out, 1)
            for c in range(KC):
                last = pe.matmul(psRt[0:1, 0:EXP], mean_t[:, c:c + 1], wr[:, c, :], start=(c == 0), stop=(c == KC - 1))
            last.then_inc(r_ps, 1)
            pe.wait_ge(r_dve, 20)
            pe.matmul(psRt[:, 8:8 + TOPK], ones[0:1, :], r[0:1, 1, 0:TOPK], start=True, stop=True).then_inc(r_ps, 1)

            def transposes(b, par):
                pe.wait_ge(xn5_ready, b + 1)
                if due(b):
                    pe.wait_ge(xl5_ready, b)
                for t in range(2):
                    for c in range(KC):
                        last = pe.transpose(psT[:, c, TOK * t:TOK * t + TOK], xn5[:, par, t, 128 * c:128 * c + 128],
                                            ident[0:TOK, 0:TOK])
                last.then_inc(xt5_ps, 1)

            def step(k, kp):
                if live(k):
                    pe.wait_ge(xl5_ready, k + 1)
                    for j in range(4):
                        if isinstance(k, int) and k == 0 and j % 2 == 0:
                            pe.wait_ge(e1_l, j // 2 + 1)
                        if due(k):
                            pe.wait_ge(g_act, 4 * (k - 1) + j + 1)
                        for i in range(2):
                            c = 2 * j + i
                            e, f = c // FC, c % FC
                            for kc in range(KC):
                                last = three_products(pe, psF[j][:, i, :], [w[:, e, kc, 128 * f:128 * f + 128] for w in e1],
                                                      [w[:, kp, kc, :] for w in xs], kc == 0, kc == KC - 1)
                        last.then_inc(f_ps, 1)
                        if j == 2 and live(k + 1):
                            transposes(k + 1, 1 - kp)
                elif k == -1:
                    transposes(0, 0)
                if isinstance(k, int) and k == 1:
                    pe.wait_ge(e2_l, 1)
                if live(k - 1):
                    pe.wait_ge(gl_done, 4 * k)
                    if due(k - 1):
                        pe.wait_ge(z5_ready, k - 1)
                    for t in range(2):
                        for c in range(8):
                            last = three_products(pe, psE[:, t, :],
                                                  [w[:, 1 - kp, c, TOK * t:TOK * t + TOK] for w in gs],
                                                  [w[:, c // FC, c % FC, :] for w in e2], c == 0, c == 7)
                    last.then_inc(e_ps, 1)
            run_steps(pe, step, -1, 2, 11, 26)


_NAMES = {
    "edge": "edge_attr_256", "x": "x", "wk": "L0_mix_wk", "wv": "L0_mix_wv", "wq": "L0_mix_wq", "wo": "L0_mix_wo",
    "bk": "L0_mix_bk", "bv": "L0_mix_bv", "bo": "L0_mix_bo", "gnn_b2": "L0_gnn_b2", "wr": "L0_ffn_Wr",
    "gamma": "L0_ffn_gamma", "beta": "L0_ffn_beta", "w1": "L0_ffn_W1", "w2": "L0_ffn_W2", "b2": "L0_ffn_b2",
}


def kernel(**inputs):
    import concourse.bacc as bacc
    from concourse.bass_utils import run_bass_kernel_spmd

    host = {k: np.ascontiguousarray(inputs[v]) for k, v in _NAMES.items()}
    host["bq"] = np.ascontiguousarray(np.asarray(inputs["L0_mix_bq"]).reshape(KC, 128).T)
    host["gnn_b1"] = np.ascontiguousarray(np.asarray(inputs["L0_gnn_b1"]).reshape(KC, 128).T)
    host["gnn_w1t"] = np.ascontiguousarray(np.asarray(inputs["L0_gnn_W1"]).T)
    host["gnn_w2t"] = np.ascontiguousarray(np.asarray(inputs["L0_gnn_W2"]).T)
    host["b1"] = np.ascontiguousarray(np.asarray(inputs["L0_ffn_b1"]).reshape(EXP, FC, 128).transpose(0, 2, 1))
    host["br"] = np.asarray(inputs["L0_ffn_br"]).reshape(1, EXP)
    dst = np.asarray(inputs["dst"])
    sups = np.concatenate([dst[:(NSUP - 1) * SUP], dst[LAST:]]).reshape(NSUP, NG, 128, 2)
    host["dst_t"] = np.ascontiguousarray(sups.transpose(2, 0, 1, 3)).reshape(128, NSUP, NG * 2)
    host["dst_base"] = np.ascontiguousarray(sups[:, :, 0, 0]).reshape(-1)
    host["dst_row"] = np.ascontiguousarray(sups[:, :, 0, 0].T)

    nc = bacc.Bacc("TRN2", target_bir_lowering=False, num_devices=1)
    args = {k: nc.dram_tensor(f"in_{k}", list(v.shape), mybir.dt.from_np(v.dtype), kind="ExternalInput").ap()
            for k, v in host.items()}
    out = nc.dram_tensor("out_x", [N, D], F32, kind="ExternalOutput").ap()
    build(nc, args, out)
    result = run_bass_kernel_spmd(nc, [{f"in_{k}": v for k, v in host.items()}], core_ids=[0])
    return result.results[0]["out_x"]
```

```python
import numpy as np
import concourse.bass as bass
from concourse import mybir
from contextlib import ExitStack

F32 = mybir.dt.float32
F32R = mybir.dt.float32r
I32 = mybir.dt.int32
U32 = mybir.dt.uint32
ALU = mybir.AluOpType
ACT = mybir.ActivationFunctionType
AX = mybir.AxisListType

N = 6250
D = 256
KC = D // 128
NE = 106250
TOK = 125
NT = N // TOK
BLK = 2 * TOK
NB = N // BLK
HD = 32
EXP, FF, TOPK = 8, 512, 2
FC = FF // 128
CAP = float(-(-N * 5 // (4 * EXP)))
EPS = 1e-5
SLOPE = 0.015

GRP, NG = 256, 4
SUP = GRP * NG
NSUP = -(-NE // SUP)
NPAIR = NSUP // 2
LAST = NE - SUP
OVER = (NSUP - 1) * SUP - LAST
GWIN = 32
SHIFT = 60
WIN = 160
PAD = 38
AGW = SHIFT * (NSUP - 1) + WIN
PW = SHIFT + WIN
assert NSUP % 2 == 0 and AGW >= PAD + N and N % BLK == 0

MAGIC = 1597463007.0
ROOT_STEPS = 3
ROOT_OPS = 4 * ROOT_STEPS
SOON = 36


def due(n):
    return not isinstance(n, int) or n > 0


def live(b, n=NB):
    return not isinstance(b, int) or 0 <= b < n


def run_steps(eng, step, first, low, doubles, end):
    for k in range(first, low):
        step(k, k % 2)
    with eng.Fori(0, doubles) as i:
        for p in range(2):
            step(2 * i + (low + p), (low + p) % 2)
    for k in range(low + 2 * doubles, end):
        step(k, k % 2)


def three_products(pe, out, a, b, first, last):
    (ah, al), (bh, bl) = a, b
    pe.matmul(out, ah, bh, start=first, stop=False)
    pe.matmul(out, ah, bl, start=False, stop=False)
    return pe.matmul(out, al, bh, start=False, stop=last)


def build(nc, a, out):
    with ExitStack() as ctx:
        _build(nc, a, out, ctx)


def _build(nc, a, out, ctx):
    def sb(name, shape, dt=F32, stack=None):
        return (stack or ctx).enter_context(nc.sbuf_tensor(name, shape, dt))

    def sem(name, stack=None):
        return ctx.enter_context(nc.semaphore(name))

    ps = ctx.enter_context(nc.psum_tensor("ps", [128, 8, 512], F32))

    def bank(i, n=1):
        return ps[:, i:i + n, :].rearrange("p b n -> p (b n)")

    x = sb("x", [TOK, NT, D])
    mv = sb("mv", [TOK, NT, 2])
    rstd = sb("rstd", [TOK, NT, 1])
    half3 = sb("half3", [TOK, 1])
    nv, nh, ny, nw = (sb(n, [TOK, 2, 2, 1]) for n in ("nv", "nh", "ny", "nw"))
    ni = sb("ni", [TOK, 2, 2, 1], I32)
    mvs = sb("mvs", [TOK, 2, 2, 2])
    ident = sb("ident", [128, 128])
    ones = sb("ones", [128, 128])
    flag = sb("flag", [1, 1], I32)
    mean_t = sb("mean_t", [128, KC])

    agg_stack = ctx.enter_context(ExitStack())
    aggT = sb("aggT", [128, KC, AGW], F32, agg_stack)
    dstf = sb("dstf", [128, NSUP, 8], F32, agg_stack)
    edge_stack = ExitStack()
    ring = sb("ring", [128, 4, NG, 2 * D], F32, edge_stack)
    rel = sb("rel", [128, NSUP, 8], F32, edge_stack)
    rowrel = sb("rowrel", [128, NSUP], F32, edge_stack)
    iota = sb("iota", [128, WIN], F32, edge_stack)
    oh1 = sb("oh1", [128, 2, 16, GWIN], F32, edge_stack)
    oh2 = sb("oh2", [128, 2, 2, WIN], F32, edge_stack)
    rows = sb("rows", [128, 2, 2, D], F32, edge_stack)

    first_x = [sem(f"first_x{c}") for c in range(4)]
    x_in = [sem(f"x_in{c}") for c in range(2)]
    edges_in = [sem(f"edges_in{c}") for c in range(4)]
    edges_used = sem("edges_used")
    oh1_ready, oh2_ready = sem("oh1_ready"), sem("oh2_ready")
    rows_ps, rows_ready = sem("rows_ps"), sem("rows_ready")
    win_ps, agg_added = sem("win_ps"), sem("agg_added")
    consts = sem("consts")
    zeroed = sem("zeroed")
    EARLY = 5
    dst_in = sem("dst_in")
    dst_ready = sem("dst_ready")

    psR = bank(0).rearrange("p (h n) -> p h n", h=2)
    psW = bank(1).rearrange("p (h n) -> p h n", h=2)
    e_sup = a["edge"][0:(NSUP - 1) * SUP, :].rearrange("(s g p j) d -> s p g (j d)", g=NG, p=128, j=2)
    e_last = a["edge"][LAST:NE, :].rearrange("(g p j) d -> p g (j d)", g=NG, p=128, j=2)

    def load_pair(sp, u, par):
        for h in range(2):
            if due(2 * u + h - 3):
                sp.wait_ge(edges_used, 2 * u + h - 3)
            dst = ring[:, 2 * par + h]
            if isinstance(u, int) and 2 * u + h == NSUP - 1:
                src = e_last
            elif isinstance(u, int):
                src = e_sup[2 * u + h]
            else:
                src = e_sup[bass.ds(2 * u + h, 1)].rearrange("o p g n -> (o p) g n")
            sp.dma_start(dst, src).then_inc(edges_in[2 * par + h], 16)

    def onehot1(dve, u, par):
        if due(2 * u - 2):
            dve.wait_ge(edges_used, 2 * u - 2)
        dve.tensor_tensor(
            oh1[:, par],
            rel[:, bass.ds(2 * u, 2), :].rearrange("p s c -> p (s c)").unsqueeze(2).to_broadcast([128, 16, GWIN]),
            iota[:, 0:GWIN].unsqueeze(1).to_broadcast([128, 16, GWIN]), ALU.is_equal).then_inc(oh1_ready, 1)

    def onehot2(dve, u, par):
        if due(u - 1):
            dve.wait_ge(win_ps, u - 1)
        dve.tensor_tensor(
            oh2[:, par],
            rowrel[:, bass.ds(2 * u, 2)].unsqueeze(2).to_broadcast([128, 2, WIN]),
            iota[:, 0:WIN].unsqueeze(1).to_broadcast([128, 2, WIN]), ALU.is_equal).then_inc(oh2_ready, 1)

    def sum_groups(pe, u, par, h):
        if h == 0:
            pe.wait_ge(oh1_ready, u + 1)
            if due(u):
                pe.wait_ge(rows_ready, u)
        pe.wait_ge(edges_in[2 * par + h], 8 * u + (16 - 8 * par))
        for j in range(2):
            for g in range(NG):
                last = pe.matmul(psR[32 * g:32 * g + 32, h, :], oh1[:, par, 8 * h + 2 * g + j, :],
                                 ring[:, 2 * par + h, g, j * D:(j + 1) * D],
                                 start=(j == 0), stop=(j == 1), skip_group_check=True)
        last.then_inc(edges_used, 1)

    def rows_out(act, u, par):
        act.wait_ge(edges_used, 2 * u + 2)
        if due(u - 1):
            act.wait_ge(win_ps, u - 1)
        act.activation(rows[:, par], psR[:, :, :], ACT.Copy).then_inc(rows_ready, 1)

    def sum_windows(pe, u, par, follows):
        if not follows:
            pe.wait_ge(rows_ready, u + 1)
        pe.wait_ge(oh2_ready, u + 1)
        if due(u):
            pe.wait_ge(agg_added, u)
        for h in range(2):
            for f in range(KC):
                last = pe.matmul(psW[:, f, SHIFT * h:SHIFT * h + WIN], rows[:, par, h, 128 * f:128 * f + 128],
                                 oh2[:, par, h, :], start=(h == 0 and f == 0), stop=(h == 1 and f == 1),
                                 skip_group_check=True)
        last.then_inc(win_ps, 1)

    def add_window(dve, u, par):
        dve.wait_ge(win_ps, u + 1)
        if due(u):
            dve.wait_ge(agg_added, u)
        if isinstance(u, int) and u in (0, EARLY):
            dve.wait_ge(zeroed, 1 if u == 0 else 2)
        w = aggT[:, :, bass.ds(2 * SHIFT * u, PW)]
        dve.tensor_tensor(w, w, psW[:, :, 0:PW], ALU.add).then_inc(agg_added, 1)

    root_seed, root_step = sem("root_seed"), sem("root_step")

    def root_of(par):
        return nv[:, par], nh[:, par], ni[:, par], ny[:, par], nw[:, par]

    def seed_root(dve, var, tiles_of, done):
        v, h, i, y, _ = tiles_of
        dve.tensor_scalar(v, var, EPS, None, ALU.add).then_inc(root_seed, 1)
        dve.tensor_scalar(h, var, EPS, -0.5, ALU.add, ALU.mult).then_inc(root_seed, 1)
        dve.wait_ge(root_seed, 4 * done + 1)
        dve.tensor_scalar(i, v.bitcast(I32), 1, None, ALU.logical_shift_right).then_inc(root_seed, 1)
        dve.wait_ge(root_seed, 4 * done + 3)
        dve.tensor_scalar(y.bitcast(I32), i, -1.0, MAGIC, ALU.mult, ALU.add).then_inc(root_seed, 1)

    def newton_root(pool, tiles_of, done):
        _, h, _, y, w = tiles_of
        pool.wait_ge(root_seed, 4 * done + 4)
        c = ROOT_OPS * done
        for it in range(ROOT_STEPS):
            if it:
                pool.wait_ge(root_step, c)
            pool.tensor_tensor(w, y, y, ALU.mult).then_inc(root_step, 1)
            pool.wait_ge(root_step, c + 1)
            pool.tensor_tensor(w, w, h, ALU.mult).then_inc(root_step, 1)
            pool.wait_ge(root_step, c + 2)
            pool.tensor_tensor(w, w, half3[:].unsqueeze(1).to_broadcast(w.shape), ALU.add).then_inc(root_step, 1)
            pool.wait_ge(root_step, c + 3)
            pool.tensor_tensor(y, y, w, ALU.mult).then_inc(root_step, 1)
            c = c + 4

    def bcast(row, n=TOK):
        return row.partition_broadcast(n)

    attn_stack = ExitStack()
    wq = [sb(f"wq{i}", [128, KC, D], F32R, attn_stack) for i in range(2)]
    wo = [sb(f"wo{i}", [128, KC, D], F32R, attn_stack) for i in range(2)]
    kvm = [sb(f"kvm{i}", [128, KC, 132], F32R, attn_stack) for i in range(2)]
    xn = sb("xn", [TOK, 2, 2, D], F32, attn_stack)
    xt = [sb(f"xt{i}", [128, 2, KC, BLK], F32R, attn_stack) for i in range(2)]
    bq = sb("bq", [128, KC], F32, attn_stack)

    s1 = ExitStack()
    wkv = [sb(f"wkv{i}", [128, KC, 2 * D], F32R, s1) for i in range(2)]
    wraw = sb("wraw", [128, KC, 2, D], F32, s1)
    bkv = sb("bkv", [TOK, 4, 128], F32, s1)
    bn1 = sb("bn1", [TOK, 2, 6], F32, s1)
    kvt = sb("kvt", [TOK, 2, 2, 4, 130], F32, s1)
    kf_ = sb("kf", [128, 2, 2, D], F32, s1)
    ek_ = sb("ek", [128, 2, D], F32, s1)
    rk_ = sb("rk", [128, 2, D], F32, s1)
    kf, ek, rk = kf_[0:TOK], ek_[0:TOK], rk_[0:TOK]
    rowi = sb("rowi", [128, NSUP], I32, s1)

    def scratch(t, dims, shape, dt):
        flat = t[:].rearrange(dims).bitcast(dt)[:, 0:NSUP * shape]
        return flat.rearrange("p (s g) -> p s g", g=shape)

    dsti = scratch(kf_, "p a b n -> p (a b n)", 8, I32)
    basei = scratch(ek_, "p a n -> p (a n)", NG, I32)
    basef = scratch(rk_, "p a n -> p (a n)", NG, F32)
    wrel = scratch(kf_, "p a b n -> p (a b n)", 8, F32)
    woff = sb("woff", [128, NSUP], F32, s1)
    rowoff = sb("rowoff", [128, NSUP], F32, s1)
    mm4 = sb("mm4", [128, 4], F32, s1)
    bad = sb("bad", [128, 4], F32, s1)
    badsum = sb("badsum", [128, 1], F32, s1)
    mask = rk_[:, 0, 0:128]
    kvf = kf_[:].rearrange("p a b n -> p (a b n)")[:, 0:KC * 132].rearrange("p (c n) -> p c n", c=KC)

    w_in = [sem("w_in_kv"), sem("w_in_qo"), sem("b_in")]
    w_split, w_rest = sem("w_split"), sem("w_rest")
    stats, dchk = sem("stats"), sem("dchk")
    mask_ready = sem("mask_ready")
    bn1_ready, mv1_ready = sem("bn1_ready"), sem("mv1_ready")
    flag_ps, flag_set = sem("flag_ps"), sem("flag_set")
    xn_ready, xt_ps, xh_ready, xl_ready = sem("xn_ready"), sem("xt_ps"), sem("xh_ready"), sem("xl_ready")
    kv_ps, kvt_ready, ek_ready, kf_ready = (sem(n) for n in ("kv_ps", "kvt_ready", "ek_ready", "kf_ready"))
    kv_summed, kvm_f, kvm_h, kvm_l = sem("kv_summed"), sem("kvm_f"), sem("kvm_h"), sem("kvm_l")

    psT = bank(2)[:, 0:2 * BLK].rearrange("p (c n) -> p c n", c=KC)
    psKV = [bank(3), bank(4)]
    psA = bank(5)[:, 0:2 * 130].rearrange("p (c n) -> p c n", c=KC)
    xv = a["x"].rearrange("(t p) d -> p t d", p=TOK)
    FIRST_PAIRS = 28

    with nc.Block() as block:
        @block.sync
        def _(sp):
            def load_x(b, par):
                if due(b - 5):
                    sp.wait_ge(bn1_ready, b - 1)
                sp.dma_start(x[:, bass.ds(2 * b, 2), :], xv[:, bass.ds(2 * b, 2), :]).then_inc(
                    first_x[b] if isinstance(b, int) and b < 4 else x_in[par], 16)

            load_x(0, 0)
            sp.dma_start(dsti[:], a["dst_t"]).then_inc(dst_in, 16)
            sp.dma_start(basei[:].rearrange("p s g -> p (s g)"), bcast(a["dst_base"], 128)).then_inc(dst_in, 16)
            for g in range(NG):
                sp.dma_start(rowi[32 * g:32 * g + 32, :], bcast(a["dst_row"][g], 32)).then_inc(dst_in, 16)
            load_x(1, 1)
            load_pair(sp, 0, 0)
            load_x(2, 0)
            load_x(3, 1)
            load_pair(sp, 1, 1)

            def step(k, kp):
                load_pair(sp, k + 4, kp)
                if live(k + 6):
                    load_x(k + 6, kp)
            run_steps(sp, step, -2, 1, 9, 26)

        @block.scalar
        def _(act):
            act.dma_start(wraw[:, :, 0, :], a["wk"].rearrange("(c p) n -> p c n", p=128)).then_inc(w_in[0], 16)
            act.dma_start(wraw[:, :, 1, :], a["wv"].rearrange("(c p) n -> p c n", p=128)).then_inc(w_in[0], 16)
            act.dma_start(bkv[:, 0:2, :].rearrange("p a n -> p (a n)"), bcast(a["bk"])).then_inc(w_in[2], 16)
            act.dma_start(bkv[:, 2:4, :].rearrange("p a n -> p (a n)"), bcast(a["bv"])).then_inc(w_in[2], 16)
            act.dma_start(bq[:], a["bq"]).then_inc(w_in[2], 16)
            act.wait_ge(w_in[0], 32)
            act.activation(wkv[0][:], wraw[:].rearrange("p c a n -> p c (a n)"), ACT.Copy).then_inc(w_split, 1)

            def step(k, kp):
                if live(k + 1):
                    act.wait_ge(xt_ps, k + 2)
                    if due(2 * k - 2 + 2):
                        act.wait_ge(kv_ps, 2 * k)
                    act.activation(xt[0][:, 1 - kp], psT[:, :, :], ACT.Copy).then_inc(xh_ready, 1)
                if live(k):
                    for t in range(2):
                        act.wait_ge(kvt_ready, 2 * k + t + 1)
                        if due(2 * k + t - 1):
                            act.wait_ge(kf_ready, 2 * k + t - 1)
                        act.activation(ek[:, t, :].rearrange("p (a n) -> p a n", a=2),
                                       kvt[:, kp, t, 0:2, 0:128], ACT.Exp)
                        act.activation(rk[:, t, :].rearrange("p (a n) -> p a n", a=2),
                                       kvt[:, kp, t, 0:2, 0:128], ACT.Relu).then_inc(ek_ready, 1)
                if isinstance(k, int) and k == 0:
                    act.wait_ge(w_rest, 1)
                    act.dma_start(wraw[:, :, 0, :], a["wq"].rearrange("(c p) n -> p c n", p=128)).then_inc(w_in[1], 16)
                    act.dma_start(wraw[:, :, 1, :], a["wo"].rearrange("(c p) n -> p c n", p=128)).then_inc(w_in[1], 16)
                if isinstance(k, int) and k == 23:
                    act.wait_ge(w_in[1], 32)
                    act.activation(wq[0][:], wraw[:, :, 0, :], ACT.Copy).then_inc(w_split, 1)
                    act.activation(wo[0][:], wraw[:, :, 1, :], ACT.Copy).then_inc(w_split, 1)
                if live(k + 2, FIRST_PAIRS):
                    rows_out(act, k + 2, kp)
            run_steps(act, step, -4, 3, 9, 26)
            act.wait_ge(kvm_f, 2)
            act.activation(kvm[0][:], kvf, ACT.Copy).then_inc(kvm_h, 1)

        @block.gpsimd
        def _(pool):
            pool.memset(ones[:], 1.0).then_inc(consts, 1)
            pool.memset(ident[:], 0.0).then_inc(consts, 1)
            pool.iota(iota[:], pattern=[[1, WIN]], base=0, channel_multiplier=0,
                      allow_small_or_imprecise_dtypes=True).then_inc(consts, 1)
            pool.wait_ge(consts, 3)
            pool.affine_select(out=ident[:], in_=ident[:], compare_op=ALU.not_equal, fill=1.0, base=0,
                               pattern=[[-1, 128]], channel_multiplier=1).then_inc(consts, 1)
            pool.iota(woff[:], pattern=[[-SHIFT, NSUP]], base=PAD, channel_multiplier=0,
                      allow_small_or_imprecise_dtypes=True).then_inc(dst_ready, 1)
            for g in range(NG):
                pool.wait_ge(dst_ready, g + 1)
                pool.iota(rowoff[32 * g:32 * g + 32, :], pattern=[[-SHIFT, NSUP]], base=PAD, channel_multiplier=1,
                          allow_small_or_imprecise_dtypes=True).then_inc(dst_ready, 1)
            pool.wait_ge(dst_ready, 5)
            early = 2 * SHIFT * (EARLY - 1) + PW
            pool.memset(aggT[:, :, 0:early], 0.0).then_inc(zeroed, 1)
            pool.memset(kvt[:, :, :, :, 128:130], 1.0).then_inc(consts, 1)
            pool.memset(half3[:], 1.5).then_inc(consts, 1)
            pool.wait_ge(consts, 6)

            def step(k, kp):
                newton_root(pool, root_of(kp), k + 4)
                if isinstance(k, int) and k == -3:
                    pool.memset(aggT[:, :, early:], 0.0).then_inc(zeroed, 1)
                if isinstance(k, int) and k == -2:
                    pool.wait_ge(dchk, 7)
                    pool.affine_select(out=dstf[:, NSUP - 1, 0:2], in_=dstf[:, NSUP - 1, 0:2], compare_op=ALU.is_ge,
                                       fill=-1.0, base=-OVER, pattern=[[1, 2]], channel_multiplier=2).then_inc(dst_ready, 1)
                    pool.affine_select(out=rel[:, NSUP - 1, 0:2], in_=rel[:, NSUP - 1, 0:2], compare_op=ALU.is_ge,
                                       fill=-1.0, base=-OVER, pattern=[[1, 2]], channel_multiplier=2).then_inc(dst_ready, 1)
            run_steps(pool, step, -4, -1, 11, 21)
            pool.wait_ge(kf_ready, NT)
            pool.memset(mask, 0.0).then_inc(mask_ready, 1)
            for h in range(4):
                pool.wait_ge(mask_ready, h + 1)
                pool.memset(mask[32 * h:32 * h + 32, 32 * h:32 * h + 32], 1.0).then_inc(mask_ready, 1)

        @block.vector
        def _(dve):
            def normalize(b, par):
                dve.wait_ge(root_step, ROOT_OPS * (b + 1))
                dve.tensor_scalar(rstd[:, bass.ds(2 * b, 2), :], ny[:, par], 1.0, None, ALU.mult)
                dve.tensor_scalar(mv[:, bass.ds(2 * b, 2), 0:1], mvs[:, par, :, 0:1], 1.0, None, ALU.mult)
                if due(b - 1):
                    dve.wait_ge(xt_ps, b - 1)
                for t in range(2):
                    last = dve.tensor_scalar(xn[:, par, t, :], x[:, bass.ds(2 * b + t, 1), :].rearrange("p o d -> p (o d)"),
                                             mvs[:, par, t, 0:1], ny[:, par, t, :], ALU.subtract, ALU.mult)
                last.then_inc(xn_ready, 1)

            def step(k, kp):
                if live(k + 4):
                    if isinstance(k, int) and k < 0:
                        dve.wait_ge(first_x[k + 4], 16)
                    else:
                        dve.wait_ge(x_in[kp], 8 * k + (16 - 8 * kp))
                if live(k + 2, FIRST_PAIRS):
                    onehot2(dve, k + 2, kp)
                if live(k + 4):
                    for t in range(2):
                        last = dve.bn_stats(bn1[:, t, :], x[:, bass.ds(2 * (k + 4) + t, 1), :].rearrange("p o d -> p (o d)"))
                    last.then_inc(bn1_ready, 1)
                if live(k + 2):
                    normalize(k + 2, kp)
                    if live(k + 4):
                        dve.wait_ge(xn_ready, k + 3)
                if live(k + 4):
                    dve.wait_ge(bn1_ready, k + 5)
                if live(k + 1):
                    dve.wait_ge(xh_ready, k + 2)
                    dve.tensor_tensor(xt[1][:, 1 - kp], psT[:, :, :], xt[0][:, 1 - kp].bitcast(F32),
                                      ALU.subtract).then_inc(xl_ready, 1)
                if live(k + 4):
                    for t in range(2):
                        last = dve.bn_aggr(mvs[:, kp, t, :], bn1[:, t, :])
                    last.then_inc(mv1_ready, 1)
                    dve.wait_ge(mv1_ready, k + 5)
                    seed_root(dve, mvs[:, kp, :, 1:2], root_of(kp), k + 4)
                if isinstance(k, int) and k == -2:
                    dve.wait_ge(w_split, 1)
                    dve.tensor_tensor(wkv[1][:], wraw[:].rearrange("p c a n -> p c (a n)"), wkv[0][:].bitcast(F32),
                                      ALU.subtract).then_inc(w_rest, 1)
                    dve.wait_ge(w_in[2], 48)
                    dve.wait_ge(consts, 5)
                if live(k - 1):
                    for t in range(2):
                        n = 2 * (k - 1) + t + 1
                        dve.wait_ge(ek_ready, n)
                        if due(k - 2):
                            dve.wait_ge(kv_summed, k - 2)
                        dve.scalar_tensor_tensor(kf[:, 1 - kp, t, :], ek[:, t, :], 1.0, rk[:, t, :],
                                                 ALU.min, ALU.add).then_inc(kf_ready, 1)
                if live(k):
                    for t in range(2):
                        dve.wait_ge(kv_ps, 2 * k + t + 1)
                        if due(k - 1):
                            dve.wait_ge(kv_summed, k - 1)
                        dve.tensor_tensor(kvt[:, kp, t, :, 0:128], psKV[t][0:TOK, :].rearrange("p (a n) -> p a n", a=4),
                                          bkv[:], ALU.add).then_inc(kvt_ready, 1)
                if isinstance(k, int) and k == 1:
                    dve.wait_ge(flag_ps, 1)
                    dve.tensor_copy(flag[:], bank(7)[0:1, 0:1]).then_inc(flag_set, 1)
                    dve.wait_ge(dst_ready, 7)
                if isinstance(k, int) and k == 24:
                    dve.wait_ge(w_split, 3)
                    dve.tensor_tensor(wq[1][:], wraw[:, :, 0, :], wq[0][:].bitcast(F32), ALU.subtract).then_inc(w_rest, 1)
                    dve.tensor_tensor(wo[1][:], wraw[:, :, 1, :], wo[0][:].bitcast(F32), ALU.subtract).then_inc(w_rest, 1)
                if live(k + 3, FIRST_PAIRS + 1):
                    onehot1(dve, k + 3, 1 - kp)
                if live(k + 1, FIRST_PAIRS - 1):
                    add_window(dve, k + 1, 1 - kp)
            step(-4, 0)
            dve.wait_ge(dst_in, 96)
            dve.tensor_copy(dstf[:], dsti[:]).then_inc(dchk, 1)
            dve.tensor_copy(basef[:], basei[:]).then_inc(dchk, 1)
            dve.tensor_copy(rowrel[:], rowi[:]).then_inc(dchk, 1)
            dve.wait_ge(dchk, 3)
            dve.wait_ge(dst_ready, 5)
            d4 = dstf[:].rearrange("p s (g j) -> p (s g) j", j=2)
            dve.tensor_tensor(rel[:].rearrange("p s (g j) -> p (s g) j", j=2), d4,
                              basef[:].rearrange("p s g -> p (s g)").unsqueeze(2).to_broadcast([128, NSUP * NG, 2]),
                              ALU.subtract).then_inc(dchk, 1)
            dve.tensor_tensor(rowrel[:], rowrel[:], rowoff[:], ALU.add).then_inc(dchk, 1)
            dve.tensor_tensor(wrel[:], dstf[:], woff[:].unsqueeze(2).to_broadcast([128, NSUP, 8]), ALU.add)\
               .then_inc(dchk, 1)
            dve.wait_ge(dchk, 5)
            step(-3, 1)
            dve.wait_ge(dchk, 6)
            dve.tensor_reduce(mm4[:, 0:1], rel[:].rearrange("p s c -> p (s c)"), AX.X, ALU.min)
            dve.tensor_reduce(mm4[:, 1:2], rel[:].rearrange("p s c -> p (s c)"), AX.X, ALU.max)
            dve.tensor_reduce(mm4[:, 2:3], wrel[:].rearrange("p s c -> p (s c)"), AX.X, ALU.min)
            dve.tensor_reduce(mm4[:, 3:4], wrel[:].rearrange("p s c -> p (s c)"), AX.X, ALU.max).then_inc(dchk, 1)
            dve.wait_ge(dchk, 7)
            for c in range(4):
                limit, op = ((0.0, ALU.is_lt), (GWIN - 1.0, ALU.is_gt), (0.0, ALU.is_lt), (WIN - 1.0, ALU.is_gt))[c]
                last = dve.tensor_scalar(bad[:, c:c + 1], mm4[:, c:c + 1], limit, None, op)
            last.then_inc(dchk, 1)
            dve.wait_ge(dchk, 8)
            dve.tensor_reduce(badsum[:], bad[:], AX.X, ALU.add).then_inc(dchk, 1)
            run_steps(dve, step, -2, 3, 9, 26)
            dve.wait_ge(kv_summed, NB)
            dve.wait_ge(mask_ready, 5)
            dve.tensor_tensor(kvf[:, :, 0:128], psA[:, :, 0:128], mask.unsqueeze(1).to_broadcast([128, KC, 128]),
                              ALU.mult)
            for c in range(KC):
                heads = mask.rearrange("p (h n) -> p h n", n=HD)[:, :, 0]
                last = dve.tensor_scalar(kvf[:, c, 128:132], heads, psA[:, c, 128:129], None, ALU.mult)
            last.then_inc(kvm_f, 2)
            dve.wait_ge(kvm_h, 1)
            dve.tensor_tensor(kvm[1][:], kvf, kvm[0][:].bitcast(F32), ALU.subtract).then_inc(kvm_l, 1)

        @block.tensor
        def _(pe):
            pe.wait_ge(consts, 4)

            def step(k, kp):
                if live(k + 1):
                    pe.wait_ge(xn_ready, k + 2)
                    if due(k + 1):
                        pe.wait_ge(xl_ready, k + 1)
                    for t in range(2):
                        for c in range(KC):
                            last = pe.transpose(psT[:, c, TOK * t:TOK * t + TOK], xn[:, 1 - kp, t, 128 * c:128 * c + 128],
                                                ident[0:TOK, 0:TOK])
                    last.then_inc(xt_ps, 1)
                if isinstance(k, int) and k == 0:
                    pe.wait_ge(dchk, 9)
                    pe.matmul(bank(7)[0:1, 0:1], badsum[:], ones[:, 0:1], start=True, stop=True).then_inc(flag_ps, 1)
                if live(k + 2, FIRST_PAIRS):
                    sum_groups(pe, k + 2, kp, 0)
                    if not live(k):
                        sum_groups(pe, k + 2, kp, 1)
                if live(k):
                    if not live(k + 1):
                        pe.wait_ge(xl_ready, k + 1)
                    if isinstance(k, int) and k == 0:
                        pe.wait_ge(w_rest, 1)
                    for t in range(2):
                        if t == 1:
                            sum_groups(pe, k + 2, kp, 1)
                        if due(2 * k + t - 1):
                            pe.wait_ge(kvt_ready, 2 * k + t - 1)
                        for c in range(KC):
                            last = three_products(pe, psKV[t][0:TOK, :],
                                                  [w[:, kp, c, TOK * t:TOK * t + TOK] for w in xt],
                                                  [w[:, c, :] for w in wkv], c == 0, c == KC - 1)
                        last.then_inc(kv_ps, 1)
                if live(k + 1, FIRST_PAIRS - 1):
                    sum_windows(pe, k + 1, 1 - kp, live(k + 2, FIRST_PAIRS))
                if live(k - 1):
                    pe.wait_ge(kf_ready, 2 * k)
                    for t in range(2):
                        for c in range(KC):
                            first = isinstance(k, int) and k == 1 and t == 0 and c == 0
                            end = isinstance(k, int) and k == NB and t == 1
                            last = pe.matmul(psA[:, c, :], kf[:, 1 - kp, t, 128 * c:128 * c + 128],
                                             kvt[:, 1 - kp, t, 2 + c, :], start=first, stop=end, skip_group_check=True)
                    last.then_inc(kv_summed, 1)
            run_steps(pe, step, -4, 3, 9, 26)


    s1.close()
    s2 = ExitStack()
    eq = sb("eq", [128, KC, BLK], F32, s2)
    rq = sb("rq", [128, KC, BLK], F32, s2)
    qf = sb("qf", [128, KC, BLK], F32, s2)
    qs = [sb(f"qs{i}", [128, 2, KC, BLK], F32R, s2) for i in range(2)]
    den = sb("den", [TOK, 2, KC, 4], F32, s2)
    rden = sb("rden", [TOK, 2, KC, 4], F32, s2)
    at = sb("at", [TOK, 2, 2, D], F32, s2)
    ats = [sb(f"ats{i}", [128, 2, KC, BLK], F32R, s2) for i in range(2)]
    b_out = sb("b_out", [TOK, D], F32, s2)
    b_out2 = sb("b_out2", [TOK, D], F32, s2)
    xnb = sb("xnb", [TOK, 2, D], F32, s2)

    b2_in, b2_sum = sem("b2_in"), sem("b2_sum")
    xn2_ready, xt2_ps, xh2_ready, xl2_ready = (sem(n) for n in ("xn2_ready", "xt2_ps", "xh2_ready", "xl2_ready"))
    q_ps, eq_ready, rq_ready, q_ready, qh_ready, ql_ready = (
        sem(n) for n in ("q_ps", "eq_ready", "rq_ready", "q_ready", "qh_ready", "ql_ready"))
    att_ps, den_ready, rden_ready, at_ready, at_t, ah_ready, al_ready = (
        sem(n) for n in ("att_ps", "den_ready", "rden_ready", "at_ready", "at_t", "ah_ready", "al_ready"))
    mix_ps, xnb_ready, x_xn, x_mixed = sem("mix_ps"), sem("xnb_ready"), sem("x_xn"), sem("x_mixed")

    def halves(i):
        return bank(i)[:, 0:KC * BLK].rearrange("p (c n) -> p c n", c=KC)

    def tiles(i):
        return bank(i)[0:TOK, :].rearrange("p (t n) -> p t n", t=2)

    psT, psQ, psO, psM = halves(2), halves(3), halves(6), tiles(7)
    psN = ps[0:TOK, 4:6, 0:KC * 132].rearrange("p t (c n) -> p t c n", c=KC)
    U0 = FIRST_PAIRS
    flat = ring[:].rearrange("p s g n -> p s (g n)")
    raw3 = flat[:, 0, 0:2 * KC * D].rearrange("p (w c n) -> p w c n", w=2, c=KC)
    w1 = wq
    w2 = [t[:].rearrange("p b c n -> p (b c n)")[:, 0:KC * D].rearrange("p (c n) -> p c n", c=KC) for t in xt]
    w3_in, w3_h, w3_l = sem("w3_in"), sem("w3_h"), sem("w3_l")
    g_edges = ring[:, 1]
    g_oh = flat[:, 2, 0:8 * BLK].rearrange("p (c n) -> p c n", c=8)
    g_node = flat[:, 3, 0:BLK]
    g_in, g_ready, g_ps, g_added, g_nodes, g_zero, agg_final = (
        sem(n) for n in ("g_in", "g_ready", "g_ps", "g_added", "g_nodes", "g_zero", "agg_final"))
    psG = halves(0)
    b1 = sb("b1", [128, KC], F32, s2)
    bn3 = sb("bn3", [TOK, 2, 6], F32, s2)
    ag, z, hf, hs = qs, [eq, rq], [qf[:], flat[:, 2, 0:KC * BLK].rearrange("p (c n) -> p c n", c=KC)], ats
    b1_in = sem("b1_in")
    gh_ready, gl_ready, h_ps, z_ready, hf_ready, hh_ready, hl_ready, y_ps = (
        sem(n) for n in ("gh_ready", "gl_ready", "h_ps", "z_ready", "hf_ready", "hh_ready", "hl_ready", "y_ps"))
    x1_ready, bn3_ready, mv3_ready, kept3 = (sem(n) for n in ("x1_ready", "bn3_ready", "mv3_ready", "kept3"))
    psH, psY = [halves(0), halves(1)], [tiles(2), tiles(3)]
    sv, sh, sw = (sb(n, [TOK, SOON, 1], F32, s2) for n in ("sv", "sh", "sw"))
    si = sb("si", [TOK, SOON, 1], I32, s2)
    soon = (sv[:], sh[:], si[:], rstd[:, 0:SOON, :], sw[:])
    gdone = sb("gdone", [1, 1], F32, s2)
    psX = bank(6)[:, 0:D]
    SAME = 32

    def sum_tokens(pe, first, end):
        for t in range(first, end):
            q = t % 4
            last = pe.matmul(psX[SAME * q:SAME * q + SAME, :], rstd[:, t, :].to_broadcast([TOK, SAME]), x[:, t, :],
                             start=(t < 4), stop=(t >= NT - 4), skip_group_check=True)
        last.then_inc(xr_ps, 1)

    xr_ps = sem("xr_ps")
    END2 = 23

    with nc.Block() as block:
        @block.sync
        def _(sp):
            def step(k, kp):
                load_pair(sp, k + (2 + U0), kp)
            run_steps(sp, step, 0, 2, 9, 22)
            sp.dma_start(b1[:], a["gnn_b1"]).then_inc(b1_in, 16)
            def load(n, src):
                sp.wait_ge(g_added, n + 1)
                sp.dma_start(g_edges, src).then_inc(g_in, 16)

            general = sp.value_load(flag[0:1, 0:1], min_val=0, max_val=512)
            with sp.If(general != 0):
                with sp.Fori(0, NB) as nb:
                    with sp.Fori(0, NSUP - 1) as s:
                        load(nb * NSUP + s, e_sup[bass.ds(s, 1)].rearrange("o p g n -> (o p) g n"))
                    load(nb * NSUP + (NSUP - 1), e_last)
            sp.end_ifs()

        @block.scalar
        def _(act):
            act.dma_start(b_out[:], bcast(a["bo"])).then_inc(b2_in, 16)
            act.dma_start(b_out2[:], bcast(a["gnn_b2"])).then_inc(b2_in, 16)

            def step(k, kp):
                if live(k + 1):
                    act.wait_ge(xt2_ps, k + 2)
                    if due(k):
                        act.wait_ge(q_ps, k)
                    act.activation(xt[0][:, 1 - kp], psT, ACT.Copy).then_inc(xh2_ready, 1)
                if live(k):
                    act.wait_ge(q_ps, k + 1)
                    if due(k):
                        act.wait_ge(q_ready, k)
                    for c in range(KC):
                        act.activation(eq[:, c, :], psQ[:, c, :], ACT.Exp, bias=bq[:, c:c + 1])
                        last = act.activation(rq[:, c, :], psQ[:, c, :], ACT.Relu, bias=bq[:, c:c + 1])
                    last.then_inc(eq_ready, 1)
                if live(k - 2):
                    act.wait_ge(at_t, k - 1)
                    if due(k - 3):
                        act.wait_ge(mix_ps, k - 3)
                    act.activation(ats[0][:, kp], psO, ACT.Copy).then_inc(ah_ready, 1)
                if live(k):
                    act.wait_ge(q_ready, k + 1)
                    if due(k - 1):
                        act.wait_ge(att_ps, k - 1)
                    act.activation(qs[0][:, kp], qf[:], ACT.Copy).then_inc(qh_ready, 1)
                if live(k + 2, NPAIR - U0):
                    rows_out(act, k + (2 + U0), kp)
                if isinstance(k, int) and k == 22:
                    act.wait_ge(edges_used, 2 * NPAIR - 2)
                    act.dma_start(raw3[:, 0], a["gnn_w1t"].rearrange("(c p) n -> p c n", p=128)).then_inc(w3_in, 16)
                    act.dma_start(raw3[:, 1], a["gnn_w2t"].rearrange("(c p) n -> p c n", p=128)).then_inc(w3_in, 16)
                if isinstance(k, int) and k == 24:
                    act.wait_ge(w3_in, 32)
                    act.wait_ge(q_ps, NB)
                    act.activation(w1[0][:], raw3[:, 0], ACT.Copy).then_inc(w3_h, 1)
                    act.activation(w2[0], raw3[:, 1], ACT.Copy).then_inc(w3_h, 1)
            def step3(k, kp):
                if live(k + 1):
                    if due(k):
                        act.wait_ge(h_ps, k)
                    if isinstance(k, int) and k < 1:
                        act.wait_ge(att_ps, NB + k)
                    act.activation(ag[0][:, kp], aggT[:, :, bass.ds(BLK * (k + 1) + PAD, BLK)], ACT.Copy)\
                       .then_inc(gh_ready, 1)
                if live(k - 1):
                    act.wait_ge(hf_ready, k)
                    if due(k - 2):
                        act.wait_ge(y_ps, k - 2)
                    if isinstance(k, int) and k < 3:
                        act.wait_ge(mix_ps, NB + k - 2)
                    act.activation(hs[0][:, kp], hf[1 - kp], ACT.Copy).then_inc(hh_ready, 1)
                if live(k):
                    act.wait_ge(h_ps, k + 1)
                    if due(k - 1):
                        act.wait_ge(hf_ready, k - 1)
                    for c in range(KC):
                        last = act.activation(z[kp][:, c, :], psH[kp][:, c, :], ACT.Identity, bias=b1[:, c:c + 1])
                    last.then_inc(z_ready, 1)

            run_steps(act, step, -2, 4, 7, 26)
            act.wait_ge(b1_in, 16)
            act.wait_ge(agg_final, 1)
            step3(-1, 1)
            step(26, 0)
            run_steps(act, step3, 0, 3, 10, 26)

        @block.gpsimd
        def _(pool):
            pool.wait_ge(b2_in, 32)
            pool.tensor_tensor(b_out[:], b_out[:], b_out2[:], ALU.add).then_inc(b2_sum, 1)
            pool.wait_ge(b2_sum, 1)

            def step(k, kp):
                if live(k):
                    pool.wait_ge(xn2_ready, k + 1)
                    if due(k):
                        pool.wait_ge(x_xn, k)
                    pool.tensor_tensor(xnb[:], xn[:, kp], b_out[:].unsqueeze(1).to_broadcast([TOK, 2, D]), ALU.add)\
                        .then_inc(xnb_ready, 1)
                    pool.wait_ge(xnb_ready, k + 1)
                    xb = x[:, bass.ds(2 * k, 2), :]
                    pool.tensor_tensor(xb, xb, xnb[:], ALU.add).then_inc(x_xn, 1)
                    pool.wait_ge(qh_ready, k + 1)
                    pool.tensor_tensor(qs[1][:, kp], qf[:], qs[0][:, kp].bitcast(F32), ALU.subtract)\
                        .then_inc(ql_ready, 1)
            def step3(k, kp):
                if live(k + 1):
                    pool.wait_ge(gh_ready, k + 2)
                    pool.tensor_tensor(ag[1][:, kp], aggT[:, :, bass.ds(BLK * (k + 1) + PAD, BLK)],
                                       ag[0][:, kp].bitcast(F32), ALU.subtract).then_inc(gl_ready, 1)
                if live(k - 1):
                    pool.wait_ge(hh_ready, k)
                    pool.tensor_tensor(hs[1][:, kp], hf[1 - kp], hs[0][:, kp].bitcast(F32),
                                       ALU.subtract).then_inc(hl_ready, 1)

            run_steps(pool, step, -2, 4, 7, 22)
            pool.wait_ge(edges_used, 2 * NPAIR)
            pool.iota(g_node, pattern=[[1, BLK]], base=-BLK, channel_multiplier=0,
                      allow_small_or_imprecise_dtypes=True).then_inc(g_zero, 1)
            for k in range(22, NB):
                step(k, k % 2)
            run_steps(pool, step3, -1, 1, 11, 24)
            newton_root(pool, soon, NB)

        @block.vector
        def _(dve):
            def normalize(b, par):
                if due(b - 1):
                    dve.wait_ge(xt2_ps, b - 1)
                    dve.wait_ge(x_xn, b - 1)
                for t in range(2):
                    last = dve.tensor_scalar(xn[:, par, t, :], x[:, bass.ds(2 * b + t, 1), :].rearrange("p o d -> p (o d)"),
                                             mv[:, bass.ds(2 * b + t, 1), 0:1].rearrange("p o d -> p (o d)"),
                                             rstd[:, bass.ds(2 * b + t, 1), :].rearrange("p o d -> p (o d)"),
                                             ALU.subtract, ALU.mult)
                last.then_inc(xn2_ready, 1)

            def step(k, kp):
                if live(k + 2, NPAIR - U0):
                    onehot2(dve, k + (2 + U0), kp)
                if live(k - 2):
                    dve.wait_ge(att_ps, k - 1)
                    dve.tensor_scalar(den[:], psN[:, :, :, 128:132], 1e-6, None, ALU.add).then_inc(den_ready, 1)
                    dve.wait_ge(den_ready, k - 1)
                    dve.reciprocal(rden[:], den[:]).then_inc(rden_ready, 1)
                    dve.wait_ge(rden_ready, k - 1)
                    if due(k - 3):
                        dve.wait_ge(at_t, k - 3)
                    for t in range(2):
                        last = dve.tensor_tensor(
                            at[:, kp, t, :].rearrange("p (c h n) -> p c h n", c=KC, h=4),
                            psN[:, t, :, 0:128].rearrange("p c (h n) -> p c h n", h=4),
                            rden[:, t].unsqueeze(3).to_broadcast([TOK, KC, 4, HD]), ALU.mult)
                    last.then_inc(at_ready, 1)
                if live(k + 2):
                    normalize(k + 2, kp)
                if live(k + 1):
                    dve.wait_ge(xh2_ready, k + 2)
                    dve.tensor_tensor(xt[1][:, 1 - kp], psT, xt[0][:, 1 - kp].bitcast(F32),
                                      ALU.subtract).then_inc(xl2_ready, 1)
                if live(k):
                    dve.wait_ge(eq_ready, k + 1)
                    if due(k):
                        dve.wait_ge(ql_ready, k)
                    dve.scalar_tensor_tensor(qf[:], eq[:], 1.0, rq[:], ALU.min, ALU.add).then_inc(q_ready, 1)
                if live(k - 2):
                    dve.wait_ge(ah_ready, k - 1)
                    dve.tensor_tensor(ats[1][:, kp], psO, ats[0][:, kp].bitcast(F32), ALU.subtract).then_inc(al_ready, 1)
                if live(k + 3, NPAIR - U0):
                    onehot1(dve, k + (3 + U0), 1 - kp)
                if live(k + 2, NPAIR - U0 + 1):
                    add_window(dve, k + (1 + U0), 1 - kp)
                if live(k - 3):
                    dve.wait_ge(mix_ps, k - 2)
                    dve.wait_ge(x_xn, k - 2)
                    xb = x[:, bass.ds(2 * (k - 3), 2), :]
                    dve.tensor_tensor(xb, xb, psM, ALU.add).then_inc(x_mixed, 1)
                if isinstance(k, int) and k == 25:
                    for i, w in enumerate((w1, w2)):
                        dve.wait_ge(w3_h, i + 1)
                        dve.tensor_tensor(w[1][:], raw3[:, i], w[0][:].bitcast(F32), ALU.subtract).then_inc(w3_l, 1)
            def step3(k, kp):
                if live(k - 1):
                    if due(k - 4):
                        dve.wait_ge(mv3_ready, k - 4)
                    dve.wait_ge(z_ready, k)
                    if due(k - 2):
                        dve.wait_ge(hl_ready, k - 2)
                    zb = z[1 - kp][:]
                    dve.scalar_tensor_tensor(hf[1 - kp], zb, SLOPE, zb, ALU.mult, ALU.max).then_inc(hf_ready, 1)
                if live(k - 4):
                    if not live(k - 1) or isinstance(k, int) and k == 4:
                        dve.wait_ge(x1_ready, k - 3)
                    if not live(k - 1):
                        dve.wait_ge(mv3_ready, k - 4)
                    for t in range(2):
                        last = dve.bn_stats(bn3[:, t, :], x[:, bass.ds(2 * (k - 4) + t, 1), :].rearrange("p o d -> p (o d)"))
                    last.then_inc(bn3_ready, 1)
                    dve.wait_ge(bn3_ready, k - 3)
                if live(k - 3):
                    dve.wait_ge(y_ps, k - 2)
                    xb = x[:, bass.ds(2 * (k - 3), 2), :]
                    dve.tensor_tensor(xb, xb, psY[1 - kp], ALU.add).then_inc(x1_ready, 1)
                if live(k - 5):
                    if not live(k - 4):
                        dve.wait_ge(mv3_ready, k - 4)
                    dve.tensor_scalar(mv[:, bass.ds(2 * (k - 5), 2), :], mvs[:, 1 - kp], 1.0, None, ALU.mult)\
                       .then_inc(kept3, 1)
                if live(k - 4):
                    for t in range(2):
                        last = dve.bn_aggr(mvs[:, kp, t, :], bn3[:, t, :])
                    last.then_inc(mv3_ready, 1)
                if isinstance(k, int) and k - 1 in (NB - 2, NB - 1):
                    dve.wait_ge(hh_ready, k)
                    dve.wait_ge(hl_ready, k - 1)
                    dve.tensor_tensor(hs[1][:, kp], hf[1 - kp], hs[0][:, kp].bitcast(F32),
                                      ALU.subtract).then_inc(hl_ready, 1)
                if isinstance(k, int) and k == SOON // 2 + 4:
                    dve.wait_ge(kept3, SOON // 2)
                    dve.tensor_scalar(sv[:], mv[:, 0:SOON, 1:2], EPS, None, ALU.add).then_inc(root_seed, 1)
                    dve.tensor_scalar(sh[:], mv[:, 0:SOON, 1:2], EPS, -0.5, ALU.add, ALU.mult).then_inc(root_seed, 1)
                if isinstance(k, int) and k == SOON // 2 + 5:
                    dve.wait_ge(root_seed, 4 * NB + 1)
                    dve.tensor_scalar(si[:], sv[:].bitcast(I32), 1, None, ALU.logical_shift_right).then_inc(root_seed, 1)
                    dve.wait_ge(root_seed, 4 * NB + 3)
                    dve.tensor_scalar(rstd[:, 0:SOON, :].bitcast(I32), si[:], -1.0, MAGIC, ALU.mult, ALU.add)\
                       .then_inc(root_seed, 1)

            run_steps(dve, step, -2, 4, 7, END2)
            def take(n, s, nb):
                dve.wait_ge(g_nodes, nb + 1)
                dve.tensor_tensor(g_oh, dstf[:, bass.ds(s, 1), :].rearrange("p s c -> p (s c)").unsqueeze(2).to_broadcast([128, 8, BLK]),
                                  g_node.unsqueeze(1).to_broadcast([128, 8, BLK]), ALU.is_equal).then_inc(g_ready, 1)
                dve.wait_ge(g_ps, n + 1)
                w = aggT[:, :, bass.ds(BLK * nb + PAD, BLK)]
                dve.tensor_tensor(w, w, psG, ALU.add).then_inc(g_added, 1)
                dve.wait_ge(g_added, n + 2)

            dve.wait_ge(g_zero, 1)
            dve.wait_ge(agg_added, NPAIR)
            general = dve.value_load(flag[0:1, 0:1], min_val=0, max_val=512)
            with dve.If(general != 0):
                dve.memset(aggT[:], 0.0).then_inc(g_added, 1)
                dve.wait_ge(g_added, 1)
                with dve.Fori(0, NB) as nb:
                    dve.tensor_scalar(g_node, g_node, float(BLK), None, ALU.add).then_inc(g_nodes, 1)
                    with dve.Fori(0, NSUP - 1) as s:
                        take(nb * NSUP + s, s, nb)
                    take(nb * NSUP + (NSUP - 1), NSUP - 1, nb)
            dve.end_ifs()
            dve.memset(gdone[:], 0.0).then_inc(agg_final, 1)
            for k in range(END2, 27):
                step(k, k % 2)
            step3(1, 1)
            step(27, 1)
            run_steps(dve, step3, 2, 6, 8, 30)

        @block.tensor
        def _(pe):
            def step(k, kp):
                if live(k + 1):
                    pe.wait_ge(xn2_ready, k + 2)
                    if due(k + 1):
                        pe.wait_ge(xl2_ready, k + 1)
                    for t in range(2):
                        for c in range(KC):
                            last = pe.transpose(psT[:, c, TOK * t:TOK * t + TOK], xn[:, 1 - kp, t, 128 * c:128 * c + 128],
                                                ident[0:TOK, 0:TOK])
                    last.then_inc(xt2_ps, 1)
                if live(k):
                    if not live(k + 1):
                        pe.wait_ge(xl2_ready, k + 1)
                    if due(k):
                        pe.wait_ge(eq_ready, k)
                    for o in range(KC):
                        for c in range(KC):
                            last = three_products(pe, psQ[:, o, :], [w[:, c, 128 * o:128 * o + 128] for w in wq],
                                                  [w[:, kp, c, :] for w in xt], c == 0, c == KC - 1)
                    last.then_inc(q_ps, 1)
                if live(k + 2, NPAIR - U0):
                    sum_groups(pe, k + (2 + U0), kp, 0)
                if live(k + 2, NPAIR - U0 + 1):
                    sum_windows(pe, k + (1 + U0), 1 - kp, live(k + 2, NPAIR - U0))
                if live(k - 2):
                    pe.wait_ge(at_ready, k - 1)
                    if due(k - 2):
                        pe.wait_ge(al_ready, k - 2)
                    for t in range(2):
                        for c in range(KC):
                            last = pe.transpose(psO[:, c, TOK * t:TOK * t + TOK], at[:, kp, t, 128 * c:128 * c + 128],
                                                ident[0:TOK, 0:TOK])
                    last.then_inc(at_t, 1)
                if live(k + 2, NPAIR - U0):
                    sum_groups(pe, k + (2 + U0), kp, 1)
                if live(k - 3):
                    if not live(k - 2):
                        pe.wait_ge(al_ready, k - 2)
                    if due(k - 3):
                        pe.wait_ge(x_mixed, k - 3)
                    for t in range(2):
                        for c in range(KC):
                            last = three_products(pe, psM[:, t, :], [w[:, 1 - kp, c, TOK * t:TOK * t + TOK] for w in ats],
                                                  [w[:, c, :] for w in wo], c == 0, c == KC - 1)
                    last.then_inc(mix_ps, 1)
                if live(k - 1):
                    pe.wait_ge(ql_ready, k)
                    if isinstance(k, int) and k == 1:
                        pe.wait_ge(kvm_l, 1)
                    for t in range(2):
                        for c in range(KC):
                            last = three_products(pe, psN[:, t, c, :],
                                                  [w[:, 1 - kp, c, TOK * t:TOK * t + TOK] for w in qs],
                                                  [w[:, c, :] for w in kvm], True, True)
                    last.then_inc(att_ps, 1)
            def step3(k, kp):
                if live(k):
                    pe.wait_ge(gl_ready, k + 1)
                    if due(k - 1):
                        pe.wait_ge(z_ready, k - 1)
                    for o in range(KC):
                        for c in range(KC):
                            last = three_products(pe, psH[kp][:, o, :], [w[:, c, 128 * o:128 * o + 128] for w in w1],
                                                  [w[:, 1 - kp, c, :] for w in ag], c == 0, c == KC - 1)
                    last.then_inc(h_ps, 1)
                if live(k - 2):
                    pe.wait_ge(hl_ready, k - 1)
                    if due(k - 3):
                        pe.wait_ge(x1_ready, k - 3)
                    for t in range(2):
                        for c in range(KC):
                            last = three_products(pe, psY[kp][:, t, :], [w[:, 1 - kp, c, TOK * t:TOK * t + TOK] for w in hs],
                                                  [w[:, c, :] for w in w2], c == 0, c == KC - 1)
                    last.then_inc(y_ps, 1)

            run_steps(pe, step, -2, 4, 7, END2)
            def sums(n):
                pe.wait_ge(g_in, 16 * n + 16)
                pe.wait_ge(g_ready, n + 1)
                for f in range(KC):
                    for c in range(8):
                        o = (c % 2) * D + 128 * f
                        last = pe.matmul(psG[:, f, :], g_edges[:, c // 2, o:o + 128], g_oh[:, c, :],
                                         start=(c == 0), stop=(c == 7))
                last.then_inc(g_ps, 1)

            general = pe.value_load(flag[0:1, 0:1], min_val=0, max_val=512)
            with pe.If(general != 0):
                with pe.Fori(0, NB * NSUP) as n:
                    sums(n)
            pe.end_ifs()
            for k in range(END2, 28):
                step(k, k % 2)
                if k == 25:
                    pe.wait_ge(w3_l, 2)
                if k in (25, 26):
                    step3(k - 25, (k - 25) % 2)
            run_steps(pe, step3, 2, 5, 10, 26)
            pe.wait_ge(root_step, ROOT_OPS * (NB + 1))
            sum_tokens(pe, 0, 10)
            step3(26, 0)
            sum_tokens(pe, 10, SOON)

    s2.close()
    attn_stack.close()
    edge_stack.close()
    agg_stack.close()

    vroot, hroot, wroot = (sb(n, [TOK, NT - SOON, 1]) for n in ("vroot", "hroot", "wroot"))
    iroot = sb("iroot", [TOK, NT - SOON, 1], I32)
    rm = sb("rm", [TOK, NT, 1])
    rm_sum = sb("rm_sum", [TOK, 2])
    xr = sb("xr", [128, D])
    gelu_one = sb("gelu_one", [1, 2])
    raw1 = sb("raw1", [128, TOPK, KC, FF])
    raw2 = sb("raw2", [128, TOPK, FC, D])
    ws2 = sb("ws2", [128, TOPK, FC, D])
    e1 = [sb(f"e1{i}", [128, TOPK, KC, FF], F32R) for i in range(2)]
    e2 = [sb(f"e2{i}", [128, TOPK, FC, D], F32R) for i in range(2)]
    eb1 = sb("eb1", [128, TOPK, FC])
    eb2 = sb("eb2", [TOK, TOPK, D])
    b2w = sb("b2w", [TOK, D])
    gamma, beta = sb("gamma", [TOK, D]), sb("beta", [TOK, D])
    wr = sb("wr", [128, KC, EXP])
    br = sb("br", [1, EXP])
    r = sb("r", [1, 12, EXP])
    idx = sb("idx", [1, EXP], U32)
    wb = sb("wb", [128, TOPK])
    r_in, r_dve, r_act, r_ps = sem("r_in"), sem("r_dve"), sem("r_act"), sem("r_ps")
    idx_ready = sem("idx_ready")
    e1_in = [sem(f"e1_in{i}") for i in range(TOPK)]
    e2_in, eb_in = sem("e2_in"), sem("eb_in")
    e1_h, e1_l, e2_w, e2_h, e2_l, b2_ready = (sem(n) for n in ("e1_h", "e1_l", "e2_w", "e2_h", "e2_l", "b2_ready"))
    chain, xr_ready, rm_ready, mean_ps, mean_out = (
        sem(n) for n in ("chain", "xr_ready", "rm_ready", "mean_ps", "mean_out"))

    xn5 = sb("xn5", [TOK, 2, 2, D])
    u5 = sb("u5", [TOK, 2, 2, D])
    xs = [sb(f"xs{i}", [128, 2, KC, BLK], F32R) for i in range(2)]
    g = sb("g", [128, 4, 2, BLK])
    gs = [sb(f"gs{i}", [128, 2, 8, BLK], F32R) for i in range(2)]
    z5 = sb("z5", [TOK, 2, 2, D])
    bn5 = sb("bn5", [TOK, 2, 6])
    zn = sb("zn", [TOK, 2, D])
    zg = sb("zg", [TOK, 2, D])
    o5 = sb("o5", [TOK, 2, 2, D])
    names = ("xn5_ready", "u5_ready", "xt5_ps", "xh5_ready", "xl5_ready", "f_ps", "g_act", "gh_done", "gl_done",
             "e_ps", "z5_ready", "bn5_ready", "mv5_ready", "zn_ready", "zg_ready", "x1b_ready", "o5_ready")
    (xn5_ready, u5_ready, xt5_ps, xh5_ready, xl5_ready, f_ps, g_act, gh_done, gl_done,
     e_ps, z5_ready, bn5_ready, mv5_ready, zn_ready, zg_ready, x1b_ready, o5_ready) = (sem(n) for n in names)
    out_done = [sem(f"out_done{i}") for i in range(2)]
    psF = [halves(j) for j in range(4)]
    psT, psE = halves(4), tiles(5)
    psMean, psRt = bank(7)[:, 0:KC], bank(7)[:, KC:KC + 16]
    halves_of_f = [slice(0, FF // 2), slice(FF // 2, FF)]
    ROOTS3 = NB + 1
    ov = out.rearrange("(t p) d -> p t d", p=TOK)

    def rows2(t, b, n=2):
        return t[:, bass.ds(2 * b, n), :]

    with nc.Block() as block:
        @block.sync
        def _(sp):
            sp.dma_start(wr[:], a["wr"].rearrange("(c p) n -> p c n", p=128)).then_inc(r_in, 16)
            sp.dma_start(br[:], a["br"]).then_inc(r_in, 16)
            sp.dma_start(gamma[:], bcast(a["gamma"])).then_inc(r_in, 16)
            sp.dma_start(beta[:], bcast(a["beta"])).then_inc(r_in, 16)
            sp.wait_ge(idx_ready, 1)
            es = [sp.value_load(idx[0:1, i:i + 1], min_val=0, max_val=EXP - 1) for i in range(TOPK)]
            for i, e in enumerate(es):
                sp.dma_start(raw1[:, i], a["w1"].rearrange("e (c p) n -> e p c n", p=128)[bass.ds(e, 1)]
                             .rearrange("o p c n -> (o p) c n")).then_inc(e1_in[i], 16)
                sp.dma_start(eb1[:, i], a["b1"][bass.ds(e, 1)].rearrange("o p c -> (o p) c")).then_inc(e1_in[i], 16)
            for i, e in enumerate(es):
                sp.dma_start(raw2[:, i], a["w2"].rearrange("e (c p) n -> e p c n", p=128)[bass.ds(e, 1)]
                             .rearrange("o p c n -> (o p) c n")).then_inc(e2_in, 16)
                sp.dma_start(eb2[:, i], bcast(a["b2"][bass.ds(e, 1)].rearrange("o n -> (o n)"))).then_inc(eb_in, 16)

            def step(k, kp):
                sp.wait_ge(o5_ready, k + 1)
                sp.dma_start(ov[:, bass.ds(2 * k, 2), :], o5[:, kp]).then_inc(out_done[kp], 16)
            run_steps(sp, step, 0, 1, 12, 25)
            sp.wait_ge(out_done[0], 16 * 13)
            sp.wait_ge(out_done[1], 16 * 12)

        @block.scalar
        def _(act):
            act.wait_ge(xr_ps, 3)
            act.activation(xr[:], psX, ACT.Copy).then_inc(xr_ready, 1)
            act.wait_ge(r_dve, 3)
            act.activation(r[:, 1, :], r[:, 0, :], ACT.Exp, bias=r[:, 8, 0:1]).then_inc(r_act, 1)
            act.wait_ge(r_dve, 11)
            act.activation(r[:, 4, :], r[:, 3, :], ACT.Exp, bias=r[:, 8, 3:4]).then_inc(r_act, 1)
            act.wait_ge(r_dve, 17)
            act.activation(r[:, 7, 0:TOPK], r[:, 6, 0:TOPK], ACT.Exp, bias=r[:, 8, 6:7]).then_inc(r_act, 1)
            act.activation(gelu_one[:, 0:1], half3[0:1, :], ACT.Gelu)

            def step(k, kp):
                if live(k):
                    for j in range(4):
                        act.wait_ge(f_ps, 4 * k + j + 1)
                        if due(4 * k + j - 3):
                            act.wait_ge(gl_done, 4 * k + j - 3)
                        for i in range(2):
                            c = 2 * j + i
                            last = act.activation(g[:, j, i, :], psF[j][:, i, :], ACT.Gelu,
                                                  bias=eb1[:, c // FC, c % FC:c % FC + 1])
                        last.then_inc(g_act, 1)
                        act.wait_ge(g_act, 4 * k + j + 1)
                        if j == 0 and due(k - 1):
                            act.wait_ge(e_ps, k - 1)
                        act.activation(gs[0][:, kp, 2 * j:2 * j + 2, :], g[:, j], ACT.Copy).then_inc(gh_done, 1)
                        if j == 2 and live(k + 1):
                            act.wait_ge(xt5_ps, k + 2)
                            act.activation(xs[0][:, 1 - kp], psT, ACT.Copy).then_inc(xh5_ready, 1)
                elif k == -1:
                    act.wait_ge(xt5_ps, 1)
                    act.activation(xs[0][:, 0], psT, ACT.Copy).then_inc(xh5_ready, 1)
            step(-1, 1)
            for i in range(TOPK):
                act.wait_ge(e1_in[i], 32)
                for part in halves_of_f:
                    act.activation(e1[0][:, i, :, part], raw1[:, i, :, part], ACT.Copy).then_inc(e1_h, 1)
            step(0, 0)
            act.wait_ge(e2_w, 1)
            act.activation(e2[0][:], ws2[:], ACT.Copy).then_inc(e2_h, 1)
            run_steps(act, step, 1, 2, 11, 25)

        @block.gpsimd
        def _(pool):
            gb = gamma[:].unsqueeze(1).to_broadcast([TOK, 2, D])
            bb = beta[:].unsqueeze(1).to_broadcast([TOK, 2, D])
            b2 = b2w[:].unsqueeze(1).to_broadcast([TOK, 2, D])
            pool.wait_ge(b2_ready, 2)

            def step(k, kp):
                if live(k - 3):
                    pool.wait_ge(zn_ready, k - 2)
                    if due(k - 3):
                        pool.wait_ge(o5_ready, k - 3)
                    pool.tensor_tensor(zg[:], zn[:], gb, ALU.mult).then_inc(zg_ready, 1)
                if live(k - 2):
                    newton_root(pool, root_of(kp), ROOTS3 + k - 2)
                    xb = rows2(x, k - 2)
                    pool.tensor_tensor(xb, xb, bb, ALU.add).then_inc(x1b_ready, 1)
                if live(k):
                    pool.wait_ge(xn5_ready, k + 1)
                    if due(k - 1):
                        pool.wait_ge(z5_ready, k - 1)
                    pool.tensor_tensor(u5[:, kp], xn5[:, kp], b2, ALU.add).then_inc(u5_ready, 1)
            run_steps(pool, step, 0, 5, 9, 28)

        @block.vector
        def _(dve):
            c = [0]

            def chained(ins):
                c[0] += 1
                ins.then_inc(chain, 1)
                dve.wait_ge(chain, c[0])

            late = rstd[:, SOON:NT, :]
            chained(dve.tensor_scalar(vroot[:], mv[:, SOON:NT, 1:2], EPS, None, ALU.add))
            chained(dve.tensor_scalar(iroot[:], vroot[:].bitcast(I32), 1, None, ALU.logical_shift_right))
            chained(dve.tensor_scalar(late.bitcast(I32), iroot[:], -1.0, MAGIC, ALU.mult, ALU.add))
            chained(dve.tensor_scalar(hroot[:], vroot[:], -0.5, None, ALU.mult))
            for _ in range(ROOT_STEPS):
                chained(dve.tensor_tensor(wroot[:], late, late, ALU.mult))
                chained(dve.tensor_tensor(wroot[:], wroot[:], hroot[:], ALU.mult))
                chained(dve.scalar_tensor_tensor(late, wroot[:], 1.5, late, ALU.add, ALU.mult))
            chained(dve.tensor_tensor(rm[:], rstd[:], mv[:, :, 0:1], ALU.mult))
            chained(dve.tensor_reduce(rm_sum[:, 0:1], rm[:].rearrange("p t o -> p (t o)"), AX.X, ALU.add))
            dve.tensor_scalar(rm_sum[:, 1:2], rm_sum[:, 0:1], -float(SAME), None, ALU.mult).then_inc(rm_ready, 1)
            dve.wait_ge(mean_ps, 1)
            dve.tensor_scalar(mean_t[:], psMean, 1.0 / (SAME * N), None, ALU.mult).then_inc(mean_out, 1)

            n = [0]

            def link(ins):
                n[0] += 1
                ins.then_inc(r_dve, 1)
                dve.wait_ge(r_dve, n[0])

            def softmax(src, dst, col, act_done, width):
                link(dve.tensor_reduce(r[:, 8, col + 1:col + 2], r[:, src, 0:width], AX.X, ALU.max))
                link(dve.tensor_scalar(r[:, 8, col:col + 1], r[:, 8, col + 1:col + 2], -1.0, None, ALU.mult))
                dve.wait_ge(r_act, act_done)
                link(dve.tensor_reduce(r[:, 8, col + 2:col + 3], r[:, src + 1, 0:width], AX.X, ALU.add))
                link(dve.reciprocal(r[:, 9, col:col + 1], r[:, 8, col + 2:col + 3]))
                link(dve.tensor_scalar(r[:, dst, 0:width], r[:, src + 1, 0:width], r[:, 9, col:col + 1], None, ALU.mult))

            dve.wait_ge(r_in, 64)
            dve.wait_ge(r_ps, 1)
            link(dve.tensor_tensor(r[:, 0, :], psRt[0:1, 0:EXP], br[:], ALU.add))
            softmax(0, 2, 0, 1, EXP)
            link(dve.tensor_scalar(r[:, 10, :], r[:, 2, :], float(N), None, ALU.mult))
            link(dve.reciprocal(r[:, 11, :], r[:, 10, :]))
            link(dve.tensor_scalar(r[:, 10, :], r[:, 11, :], CAP, 1.0, ALU.mult, ALU.min))
            dve.tensor_tensor(r[:, 3, :], r[:, 2, :], r[:, 10, :], ALU.mult).then_inc(r_ps, 1)
            dve.wait_ge(r_ps, 2)
            softmax(3, 5, 3, 2, EXP)
            link(dve.max(r[:, 6, :], r[:, 5, :]))
            dve.max_index(idx[:], r[:, 6, :], r[:, 5, :]).then_inc(idx_ready, 1)
            softmax(6, 1, 5, 3, TOPK)
            dve.wait_ge(r_ps, 3)
            link(dve.tensor_copy(wb[:], psRt[:, 8:8 + TOPK]))

            def normalize(b, par):
                if due(b - 1):
                    dve.wait_ge(xt5_ps, b - 1)
                    dve.wait_ge(u5_ready, b - 1)
                for t in range(2):
                    n = 2 * b + t
                    last = dve.tensor_scalar(xn5[:, par, t, :], x[:, bass.ds(n, 1), :].rearrange("p o d -> p (o d)"),
                                             mv[:, bass.ds(n, 1), 0:1].rearrange("p o d -> p (o d)"),
                                             rstd[:, bass.ds(n, 1), :].rearrange("p o d -> p (o d)"),
                                             ALU.subtract, ALU.mult)
                last.then_inc(xn5_ready, 1)

            def lower_x(b, par):
                dve.wait_ge(xh5_ready, b + 1)
                dve.tensor_tensor(xs[1][:, par], psT, xs[0][:, par].bitcast(F32), ALU.subtract).then_inc(xl5_ready, 1)

            def step(k, kp):
                if live(k - 2):
                    dve.wait_ge(e_ps, k - 1)
                    dve.wait_ge(u5_ready, k - 1)
                    if due(k - 3):
                        dve.wait_ge(zn_ready, k - 3)
                    dve.tensor_tensor(z5[:, kp], psE, u5[:, kp], ALU.add).then_inc(z5_ready, 1)
                    dve.wait_ge(z5_ready, k - 1)
                    if due(k - 2):
                        dve.wait_ge(mv5_ready, k - 2)
                    for t in range(2):
                        last = dve.bn_stats(bn5[:, t, :], z5[:, kp, t, :])
                    last.then_inc(bn5_ready, 1)
                    dve.wait_ge(bn5_ready, k - 1)
                if live(k + 1):
                    normalize(k + 1, 1 - kp)
                if live(k - 2):
                    if not live(k + 1):
                        dve.wait_ge(bn5_ready, k - 1)
                    for t in range(2):
                        last = dve.bn_aggr(mvs[:, kp, t, :], bn5[:, t, :])
                    last.then_inc(mv5_ready, 1)
                    dve.wait_ge(mv5_ready, k - 1)
                    seed_root(dve, mvs[:, kp, :, 1:2], root_of(kp), ROOTS3 + k - 2)
                for j in range(4):
                    if live(k):
                        lower_part(k, kp, j)
                    if j == 2 and live(k + 1):
                        lower_x(k + 1, 1 - kp)
                    if j == 2 and live(k - 2):
                        last_norm(k - 2, kp)
                    if j == 3 and live(k - 3):
                        last_sum(k - 3, 1 - kp)

            def lower_part(k, par, j):
                dve.wait_ge(gh_done, 4 * k + j + 1)
                dve.tensor_tensor(gs[1][:, par, 2 * j:2 * j + 2, :], g[:, j], gs[0][:, par, 2 * j:2 * j + 2, :].bitcast(F32),
                                  ALU.subtract).then_inc(gl_done, 1)

            def last_norm(b, par):
                dve.wait_ge(root_step, ROOT_OPS * (ROOTS3 + b + 1))
                if due(b):
                    dve.wait_ge(zg_ready, b)
                for t in range(2):
                    last = dve.tensor_scalar(zn[:, t, :], z5[:, par, t, :], mvs[:, par, t, 0:1], ny[:, par, t, :],
                                             ALU.subtract, ALU.mult)
                last.then_inc(zn_ready, 1)

            def last_sum(b, par):
                dve.wait_ge(zg_ready, b + 1)
                dve.wait_ge(x1b_ready, b + 1)
                if due(b - 1):
                    dve.wait_ge(out_done[par], 8 * (b - par))
                dve.tensor_tensor(o5[:, par], zg[:], rows2(x, b), ALU.add).then_inc(o5_ready, 1)
            step(-1, 1)
            for i in range(TOPK):
                for h, part in enumerate(halves_of_f):
                    dve.wait_ge(e1_h, 2 * i + h + 1)
                    dve.tensor_tensor(e1[1][:, i, :, part], raw1[:, i, :, part], e1[0][:, i, :, part].bitcast(F32),
                                      ALU.subtract).then_inc(e1_l, 1)
            dve.wait_ge(e2_in, 16 * TOPK)
            for i in range(TOPK):
                last = dve.tensor_scalar(ws2[:, i], raw2[:, i], wb[:, i:i + 1], None, ALU.mult)
            last.then_inc(e2_w, 1)
            dve.wait_ge(eb_in, 16 * TOPK)
            dve.tensor_scalar(b2w[:], eb2[:, 0], wb[0:TOK, 0:1], None, ALU.mult).then_inc(b2_ready, 1)
            dve.wait_ge(b2_ready, 1)
            dve.scalar_tensor_tensor(b2w[:], eb2[:, 1], wb[0:TOK, 1:2], b2w[:], ALU.mult, ALU.add).then_inc(b2_ready, 1)
            step(0, 0)
            dve.wait_ge(e2_h, 1)
            dve.tensor_tensor(e2[1][:], ws2[:], e2[0][:].bitcast(F32), ALU.subtract).then_inc(e2_l, 1)
            run_steps(dve, step, 1, 5, 9, 28)

        @block.tensor
        def _(pe):
            pe.wait_ge(chain, 4 + 3 * ROOT_STEPS)
            sum_tokens(pe, SOON, NT)
            pe.wait_ge(xr_ready, 1)
            pe.wait_ge(rm_ready, 1)
            for c in range(KC):
                pe.matmul(psMean[:, c:c + 1], xr[:, 128 * c:128 * c + 128], ones[:, 0:1], start=(c == 0), stop=False,
                          skip_group_check=True)
                last = pe.matmul(psMean[:, c:c + 1], ones[0:TOK, :], rm_sum[:, 1:2], start=False, stop=(c == KC - 1),
                                 skip_group_check=True)
            last.then_inc(mean_ps, 1)
            pe.wait_ge(r_in, 64)
            pe.wait_ge(mean_out, 1)
            for c in range(KC):
                last = pe.matmul(psRt[0:1, 0:EXP], mean_t[:, c:c + 1], wr[:, c, :], start=(c == 0), stop=(c == KC - 1))
            last.then_inc(r_ps, 1)
            pe.wait_ge(r_dve, 20)
            pe.matmul(psRt[:, 8:8 + TOPK], ones[0:1, :], r[0:1, 1, 0:TOPK], start=True, stop=True).then_inc(r_ps, 1)

            def transposes(b, par):
                pe.wait_ge(xn5_ready, b + 1)
                if due(b):
                    pe.wait_ge(xl5_ready, b)
                for t in range(2):
                    for c in range(KC):
                        last = pe.transpose(psT[:, c, TOK * t:TOK * t + TOK], xn5[:, par, t, 128 * c:128 * c + 128],
                                            ident[0:TOK, 0:TOK])
                last.then_inc(xt5_ps, 1)

            def step(k, kp):
                if live(k):
                    pe.wait_ge(xl5_ready, k + 1)
                    for j in range(4):
                        if isinstance(k, int) and k == 0:
                            pe.wait_ge(e1_l, j + 1)
                        if due(k):
                            pe.wait_ge(g_act, 4 * (k - 1) + j + 1)
                        for i in range(2):
                            c = 2 * j + i
                            e, f = c // FC, c % FC
                            for kc in range(KC):
                                last = three_products(pe, psF[j][:, i, :], [w[:, e, kc, 128 * f:128 * f + 128] for w in e1],
                                                      [w[:, kp, kc, :] for w in xs], kc == 0, kc == KC - 1)
                        last.then_inc(f_ps, 1)
                        if j == 2 and live(k + 1):
                            transposes(k + 1, 1 - kp)
                elif k == -1:
                    transposes(0, 0)
                if isinstance(k, int) and k == 1:
                    pe.wait_ge(e2_l, 1)
                if live(k - 1):
                    pe.wait_ge(gl_done, 4 * k)
                    if due(k - 1):
                        pe.wait_ge(z5_ready, k - 1)
                    for t in range(2):
                        for c in range(8):
                            last = three_products(pe, psE[:, t, :],
                                                  [w[:, 1 - kp, c, TOK * t:TOK * t + TOK] for w in gs],
                                                  [w[:, c // FC, c % FC, :] for w in e2], c == 0, c == 7)
                    last.then_inc(e_ps, 1)
            run_steps(pe, step, -1, 2, 11, 26)


_NAMES = {
    "edge": "edge_attr_256", "x": "x", "wk": "L0_mix_wk", "wv": "L0_mix_wv", "wq": "L0_mix_wq", "wo": "L0_mix_wo",
    "bk": "L0_mix_bk", "bv": "L0_mix_bv", "bo": "L0_mix_bo", "gnn_b2": "L0_gnn_b2", "wr": "L0_ffn_Wr",
    "gamma": "L0_ffn_gamma", "beta": "L0_ffn_beta", "w1": "L0_ffn_W1", "w2": "L0_ffn_W2", "b2": "L0_ffn_b2",
}


def kernel(**inputs):
    import concourse.bacc as bacc
    from concourse.bass_utils import run_bass_kernel_spmd

    host = {k: np.ascontiguousarray(inputs[v]) for k, v in _NAMES.items()}
    host["bq"] = np.ascontiguousarray(np.asarray(inputs["L0_mix_bq"]).reshape(KC, 128).T)
    host["gnn_b1"] = np.ascontiguousarray(np.asarray(inputs["L0_gnn_b1"]).reshape(KC, 128).T)
    host["gnn_w1t"] = np.ascontiguousarray(np.asarray(inputs["L0_gnn_W1"]).T)
    host["gnn_w2t"] = np.ascontiguousarray(np.asarray(inputs["L0_gnn_W2"]).T)
    host["b1"] = np.ascontiguousarray(np.asarray(inputs["L0_ffn_b1"]).reshape(EXP, FC, 128).transpose(0, 2, 1))
    host["br"] = np.asarray(inputs["L0_ffn_br"]).reshape(1, EXP)
    dst = np.asarray(inputs["dst"])
    sups = np.concatenate([dst[:(NSUP - 1) * SUP], dst[LAST:]]).reshape(NSUP, NG, 128, 2)
    host["dst_t"] = np.ascontiguousarray(sups.transpose(2, 0, 1, 3)).reshape(128, NSUP, NG * 2)
    host["dst_base"] = np.ascontiguousarray(sups[:, :, 0, 0]).reshape(-1)
    host["dst_row"] = np.ascontiguousarray(sups[:, :, 0, 0].T)

    nc = bacc.Bacc("TRN2", target_bir_lowering=False, num_devices=1)
    args = {k: nc.dram_tensor(f"in_{k}", list(v.shape), mybir.dt.from_np(v.dtype), kind="ExternalInput").ap()
            for k, v in host.items()}
    out = nc.dram_tensor("out_x", [N, D], F32, kind="ExternalOutput").ap()
    build(nc, args, out)
    result = run_bass_kernel_spmd(nc, [{f"in_{k}": v for k, v in host.items()}], core_ids=[0])
    return result.results[0]["out_x"]
```
